# Optimizing a Trainium2 kernel written in Bass

```python
import numpy as np
import jax
import jax.numpy as jnp

def _softmax(x, axis=-1):
    return jax.nn.softmax(x, axis=axis)

def _gelu(x):
    return jax.nn.gelu(x, approximate=True)

def _silu(x):
    return jax.nn.silu(x)

def _sigmoid(x):
    return jax.nn.sigmoid(x)

def _layernorm(x, axis=-1, eps=1e-05):
    m = jnp.mean(x, axis=axis, keepdims=True)
    v = jnp.var(x, axis=axis, keepdims=True)
    return (x - m) / jnp.sqrt(v + eps)

def _scatter_add(tgt, idx, src, axis=0):
    return tgt.at[idx].add(src)

def _segment_sum(src, seg, n):
    return jax.ops.segment_sum(src, seg, n)
kernel_name = 'mk_metaformer_d2_conv_nchw384_r4_8709e0'

def setup_inputs(seed: int=0):
    np.random.seed(seed)
    _w = jnp.asarray

    def _rec_inputs():
        import jax
        import jax.numpy as jnp
        _gk = jax.random.key(seed)
        x = -9.309e-05 + 1 * jax.random.normal(jax.random.fold_in(_gk, 1), (4, 96, 56, 56), jnp.float32)
        return x
    x = _rec_inputs()

    def _L0_conv_setup():
        import jax, jax.numpy as jnp
        import numpy as np
        from jax import lax
        B, C, H, W = (4, 96, 56, 56)
        NH, HC, STRIDE = (12, 32, 2)
        SCALE = HC ** (-0.5)

        def _dwconv(x, w, b, stride):
            y = lax.conv_general_dilated(x, w, (stride, stride), [(1, 1), (1, 1)], dimension_numbers=('NCHW', 'OIHW', 'NCHW'), feature_group_count=x.shape[1])
            return y + b[None, :, None, None]

        def _grid_sample_bilinear(value, grid):
            Hh, Ww = (value.shape[2], value.shape[3])
            ix = (grid[..., 0] + 1.0) * 0.5 * (Ww - 1)
            iy = (grid[..., 1] + 1.0) * 0.5 * (Hh - 1)
            x0 = jnp.floor(ix)
            y0 = jnp.floor(iy)
            wx = ix - x0
            wy = iy - y0
            x0i = jnp.clip(x0, 0, Ww - 1).astype(jnp.int32)
            x1i = jnp.clip(x0 + 1, 0, Ww - 1).astype(jnp.int32)
            y0i = jnp.clip(y0, 0, Hh - 1).astype(jnp.int32)
            y1i = jnp.clip(y0 + 1, 0, Hh - 1).astype(jnp.int32)

            def per_b(img, y0i, y1i, x0i, x1i, wx, wy):
                v00 = img[:, y0i, x0i]
                v01 = img[:, y0i, x1i]
                v10 = img[:, y1i, x0i]
                v11 = img[:, y1i, x1i]
                return v00 * (1 - wx) * (1 - wy) + v01 * wx * (1 - wy) + v10 * (1 - wx) * wy + v11 * wx * wy
            return jax.vmap(per_b)(value, y0i, y1i, x0i, x1i, wx, wy)

        def _ref_points(Hk, Wk):
            ref_y = jnp.linspace(0.5, Hk - 0.5, Hk)
            ref_x = jnp.linspace(0.5, Wk - 0.5, Wk)
            ry, rx = jnp.meshgrid(ref_y, ref_x, indexing='ij')
            return jnp.stack([ry / Hk * 2 - 1, rx / Wk * 2 - 1], axis=-1)
        key = jax.random.key(seed)
        ks = jax.random.split(key, 10)
        s = 0.05
        return {'x': jax.random.normal(ks[0], (B, C, H, W), jnp.float32), 'w_v': jax.random.normal(ks[1], (C, 1, 3, 3), jnp.float32) * s, 'b_v': jnp.zeros((C,), jnp.float32), 'w_q': jax.random.normal(ks[2], (C, 1, 3, 3), jnp.float32) * s, 'b_q': jnp.zeros((C,), jnp.float32), 'w_k': jax.random.normal(ks[3], (C, 1, 3, 3), jnp.float32) * s, 'b_k': jnp.zeros((C,), jnp.float32), 'w_off1': jax.random.normal(ks[4], (C, 1, 3, 3), jnp.float32) * s, 'b_off1': jnp.zeros((C,), jnp.float32), 'ln_g': jnp.ones((C,), jnp.float32), 'ln_b': jnp.zeros((C,), jnp.float32), 'w_off2': jax.random.normal(ks[5], (2, C), jnp.float32) * s, 'w_out': jax.random.normal(ks[6], (C, C), jnp.float32) * s}
    _L0_conv_all = _L0_conv_setup()
    _L0_conv_in = {k: v for k, v in _L0_conv_all.items() if k in ('w_v', 'b_v', 'w_q', 'b_q', 'w_k', 'b_k', 'w_off1', 'b_off1', 'ln_g', 'ln_b', 'w_off2', 'w_out')}
    del _L0_conv_all

    def _L0_ffn_setup():
        import jax, jax.numpy as jnp
        import numpy as np
        NUM_EXPERTS = 4
        TOP_K = 2
        DIM = 96
        HID = 4 * DIM
        key = jax.random.key(seed)
        ks = jax.random.split(key, 5)
        B, S = (16, 512)
        scale_in = 1.0 / np.sqrt(DIM)
        scale_hid = 1.0 / np.sqrt(HID)
        return {'x': jax.random.normal(ks[0], (B, S, DIM), dtype=jnp.float32), 'gate_w': jax.random.normal(ks[1], (DIM, NUM_EXPERTS), dtype=jnp.float32) * scale_in, 'gate_b': jnp.zeros((NUM_EXPERTS,), dtype=jnp.float32), 'w1': jax.random.normal(ks[2], (NUM_EXPERTS, DIM, HID), dtype=jnp.float32) * scale_in, 'b1': jnp.zeros((NUM_EXPERTS, HID), dtype=jnp.float32), 'w2': jax.random.normal(ks[3], (NUM_EXPERTS, HID, DIM), dtype=jnp.float32) * scale_hid, 'b2': jnp.zeros((NUM_EXPERTS, DIM), dtype=jnp.float32)}
    _L0_ffn_all = _L0_ffn_setup()
    _L0_ffn_in = {k: v for k, v in _L0_ffn_all.items() if k in ('gate_w', 'gate_b', 'w1', 'b1', 'w2', 'b2')}
    del _L0_ffn_all

    def _L1_conv_setup():
        import jax, jax.numpy as jnp
        import numpy as np
        C = 96

        def dwconv(x, w, pad_h, pad_w, stride=(1, 1)):
            return jax.lax.conv_general_dilated(x, w, window_strides=stride, padding=((pad_h, pad_h), (pad_w, pad_w)), dimension_numbers=('NCHW', 'OIHW', 'NCHW'), feature_group_count=C)
        key = jax.random.key(seed)
        ks = jax.random.split(key, 12)
        f = lambda k, shape: jax.random.normal(k, shape, dtype=jnp.float32) * 0.05
        return {'x': jax.random.normal(ks[0], (32, C, 56, 56), dtype=jnp.float32), 'w77': f(ks[1], (C, 1, 7, 7)), 'b77': f(ks[2], (C,)), 'w53': f(ks[3], (C, 1, 5, 3)), 'b53': f(ks[4], (C,)), 'w35': f(ks[5], (C, 1, 3, 5)), 'b35': f(ks[6], (C,)), 'w7w': f(ks[7], (C, 1, 1, 7)), 'w7h': f(ks[8], (C, 1, 7, 1)), 'w5w': f(ks[9], (C, 1, 1, 5)), 'w5h': f(ks[10], (C, 1, 5, 1))}
    _L1_conv_all = _L1_conv_setup()
    _L1_conv_in = {k: v for k, v in _L1_conv_all.items() if k in ('w77', 'b77', 'w53', 'b53', 'w35', 'b35', 'w7w', 'w7h', 'w5w', 'w5h')}
    del _L1_conv_all

    def _L1_ffn_setup():
        import jax, jax.numpy as jnp
        import numpy as np
        NUM_EXPERTS = 4
        TOP_K = 2
        DIM = 96
        HID = 4 * DIM
        key = jax.random.key(seed)
        ks = jax.random.split(key, 5)
        B, S = (16, 512)
        scale_in = 1.0 / np.sqrt(DIM)
        scale_hid = 1.0 / np.sqrt(HID)
        return {'x': jax.random.normal(ks[0], (B, S, DIM), dtype=jnp.float32), 'gate_w': jax.random.normal(ks[1], (DIM, NUM_EXPERTS), dtype=jnp.float32) * scale_in, 'gate_b': jnp.zeros((NUM_EXPERTS,), dtype=jnp.float32), 'w1': jax.random.normal(ks[2], (NUM_EXPERTS, DIM, HID), dtype=jnp.float32) * scale_in, 'b1': jnp.zeros((NUM_EXPERTS, HID), dtype=jnp.float32), 'w2': jax.random.normal(ks[3], (NUM_EXPERTS, HID, DIM), dtype=jnp.float32) * scale_hid, 'b2': jnp.zeros((NUM_EXPERTS, DIM), dtype=jnp.float32)}
    _L1_ffn_all = _L1_ffn_setup()
    _L1_ffn_in = {k: v for k, v in _L1_ffn_all.items() if k in ('gate_w', 'gate_b', 'w1', 'b1', 'w2', 'b2')}
    del _L1_ffn_all
    return {'x': x, 'L0_conv_w_v': _L0_conv_in['w_v'], 'L0_conv_b_v': _L0_conv_in['b_v'], 'L0_conv_w_q': _L0_conv_in['w_q'], 'L0_conv_b_q': _L0_conv_in['b_q'], 'L0_conv_w_k': _L0_conv_in['w_k'], 'L0_conv_b_k': _L0_conv_in['b_k'], 'L0_conv_w_off1': _L0_conv_in['w_off1'], 'L0_conv_b_off1': _L0_conv_in['b_off1'], 'L0_conv_ln_g': _L0_conv_in['ln_g'], 'L0_conv_ln_b': _L0_conv_in['ln_b'], 'L0_conv_w_off2': _L0_conv_in['w_off2'], 'L0_conv_w_out': _L0_conv_in['w_out'], 'L0_ffn_gate_w': _L0_ffn_in['gate_w'], 'L0_ffn_gate_b': _L0_ffn_in['gate_b'], 'L0_ffn_w1': _L0_ffn_in['w1'], 'L0_ffn_b1': _L0_ffn_in['b1'], 'L0_ffn_w2': _L0_ffn_in['w2'], 'L0_ffn_b2': _L0_ffn_in['b2'], 'L1_conv_w77': _L1_conv_in['w77'], 'L1_conv_b77': _L1_conv_in['b77'], 'L1_conv_w53': _L1_conv_in['w53'], 'L1_conv_b53': _L1_conv_in['b53'], 'L1_conv_w35': _L1_conv_in['w35'], 'L1_conv_b35': _L1_conv_in['b35'], 'L1_conv_w7w': _L1_conv_in['w7w'], 'L1_conv_w7h': _L1_conv_in['w7h'], 'L1_conv_w5w': _L1_conv_in['w5w'], 'L1_conv_w5h': _L1_conv_in['w5h'], 'L1_ffn_gate_w': _L1_ffn_in['gate_w'], 'L1_ffn_gate_b': _L1_ffn_in['gate_b'], 'L1_ffn_w1': _L1_ffn_in['w1'], 'L1_ffn_b1': _L1_ffn_in['b1'], 'L1_ffn_w2': _L1_ffn_in['w2'], 'L1_ffn_b2': _L1_ffn_in['b2']}

def reference(x, L0_conv_w_v, L0_conv_b_v, L0_conv_w_q, L0_conv_b_q, L0_conv_w_k, L0_conv_b_k, L0_conv_w_off1, L0_conv_b_off1, L0_conv_ln_g, L0_conv_ln_b, L0_conv_w_off2, L0_conv_w_out, L0_ffn_gate_w, L0_ffn_gate_b, L0_ffn_w1, L0_ffn_b1, L0_ffn_w2, L0_ffn_b2, L1_conv_w77, L1_conv_b77, L1_conv_w53, L1_conv_b53, L1_conv_w35, L1_conv_b35, L1_conv_w7w, L1_conv_w7h, L1_conv_w5w, L1_conv_w5h, L1_ffn_gate_w, L1_ffn_gate_b, L1_ffn_w1, L1_ffn_b1, L1_ffn_w2, L1_ffn_b2):
    import jax
    import jax.numpy as jnp

    def _L0_conv_ref(x, w_v, b_v, w_q, b_q, w_k, b_k, w_off1, b_off1, ln_g, ln_b, w_off2, w_out):
        import jax, jax.numpy as jnp
        import numpy as np
        from jax import lax
        B, C, H, W = (4, 96, 56, 56)
        NH, HC, STRIDE = (12, 32, 2)
        SCALE = HC ** (-0.5)

        def _dwconv(x, w, b, stride):
            y = lax.conv_general_dilated(x, w, (stride, stride), [(1, 1), (1, 1)], dimension_numbers=('NCHW', 'OIHW', 'NCHW'), feature_group_count=x.shape[1])
            return y + b[None, :, None, None]

        def _grid_sample_bilinear(value, grid):
            Hh, Ww = (value.shape[2], value.shape[3])
            ix = (grid[..., 0] + 1.0) * 0.5 * (Ww - 1)
            iy = (grid[..., 1] + 1.0) * 0.5 * (Hh - 1)
            x0 = jnp.floor(ix)
            y0 = jnp.floor(iy)
            wx = ix - x0
            wy = iy - y0
            x0i = jnp.clip(x0, 0, Ww - 1).astype(jnp.int32)
            x1i = jnp.clip(x0 + 1, 0, Ww - 1).astype(jnp.int32)
            y0i = jnp.clip(y0, 0, Hh - 1).astype(jnp.int32)
            y1i = jnp.clip(y0 + 1, 0, Hh - 1).astype(jnp.int32)

            def per_b(img, y0i, y1i, x0i, x1i, wx, wy):
                v00 = img[:, y0i, x0i]
                v01 = img[:, y0i, x1i]
                v10 = img[:, y1i, x0i]
                v11 = img[:, y1i, x1i]
                return v00 * (1 - wx) * (1 - wy) + v01 * wx * (1 - wy) + v10 * (1 - wx) * wy + v11 * wx * wy
            return jax.vmap(per_b)(value, y0i, y1i, x0i, x1i, wx, wy)

        def _ref_points(Hk, Wk):
            ref_y = jnp.linspace(0.5, Hk - 0.5, Hk)
            ref_x = jnp.linspace(0.5, Wk - 0.5, Wk)
            ry, rx = jnp.meshgrid(ref_y, ref_x, indexing='ij')
            return jnp.stack([ry / Hk * 2 - 1, rx / Wk * 2 - 1], axis=-1)
        Bx, Cx, Hx, Wx = x.shape
        value = _dwconv(x, w_v, b_v, 1)
        query = _dwconv(x, w_q, b_q, 1).reshape(Bx * NH, HC, -1)
        key = _dwconv(x, w_k, b_k, STRIDE).reshape(Bx * NH, HC, -1)
        off = _dwconv(x, w_off1, b_off1, STRIDE)
        o = jnp.transpose(off, (0, 2, 3, 1))
        mu = o.mean(-1, keepdims=True)
        var = o.var(-1, keepdims=True)
        o = (o - mu) / jnp.sqrt(var + 1e-05) * ln_g + ln_b
        o = jax.nn.gelu(o, approximate=False)
        offset = jnp.einsum('bhwc,pc->bhwp', o, w_off2)
        Hk, Wk = (offset.shape[1], offset.shape[2])
        ref = _ref_points(Hk, Wk)[None]
        pos = jnp.tanh(offset + ref)
        grid = pos[..., ::-1]
        v_sampled = _grid_sample_bilinear(value, grid)
        v_sampled = v_sampled.reshape(Bx * NH, HC, -1)
        attn = jnp.einsum('bcm,bcn->bmn', query, key) * SCALE
        out = jnp.einsum('bmn,bcn->bcm', attn, v_sampled)
        out = out.reshape(Bx, Cx, Hx, Wx)
        y = jnp.einsum('bchw,oc->bohw', out, w_out)
        return y

    def _L0_ffn_ref(x, gate_w, gate_b, w1, b1, w2, b2):
        import jax, jax.numpy as jnp
        import numpy as np
        NUM_EXPERTS = 4
        TOP_K = 2
        DIM = 96
        HID = 4 * DIM
        scores = jnp.einsum('bsd,de->bse', x, gate_w) + gate_b
        probs = jax.nn.softmax(scores, axis=-1)
        topk_vals, topk_idx = jax.lax.top_k(probs, TOP_K)
        mask = jnp.sum(jax.nn.one_hot(topk_idx, NUM_EXPERTS, dtype=probs.dtype), axis=-2)
        masked = probs * mask
        masked = masked / (jnp.sum(masked, axis=-1, keepdims=True) + 1e-09)
        h = jax.nn.gelu(jnp.einsum('bsd,edh->ebsh', x, w1) + b1[:, None, None, :], approximate=False)
        y = jnp.einsum('ebsh,ehd->ebsd', h, w2) + b2[:, None, None, :]
        out = jnp.einsum('bse,ebsd->bsd', masked, y)
        return out

    def _L1_conv_ref(x, w77, b77, w53, b53, w35, b35, w7w, w7h, w5w, w5h):
        import jax, jax.numpy as jnp
        import numpy as np
        C = 96

        def dwconv(x, w, pad_h, pad_w, stride=(1, 1)):
            return jax.lax.conv_general_dilated(x, w, window_strides=stride, padding=((pad_h, pad_h), (pad_w, pad_w)), dimension_numbers=('NCHW', 'OIHW', 'NCHW'), feature_group_count=C)
        bias = (b77 + b53 + b35)[None, :, None, None]
        out = dwconv(x, w77, 3, 3) + dwconv(x, w53, 2, 1) + dwconv(x, w35, 1, 2) + dwconv(dwconv(x, w7w, 0, 3), w7h, 3, 0) + dwconv(dwconv(x, w5w, 0, 2), w5h, 2, 0) + bias
        return out

    def _L1_ffn_ref(x, gate_w, gate_b, w1, b1, w2, b2):
        import jax, jax.numpy as jnp
        import numpy as np
        NUM_EXPERTS = 4
        TOP_K = 2
        DIM = 96
        HID = 4 * DIM
        scores = jnp.einsum('bsd,de->bse', x, gate_w) + gate_b
        probs = jax.nn.softmax(scores, axis=-1)
        topk_vals, topk_idx = jax.lax.top_k(probs, TOP_K)
        mask = jnp.sum(jax.nn.one_hot(topk_idx, NUM_EXPERTS, dtype=probs.dtype), axis=-2)
        masked = probs * mask
        masked = masked / (jnp.sum(masked, axis=-1, keepdims=True) + 1e-09)
        h = jax.nn.gelu(jnp.einsum('bsd,edh->ebsh', x, w1) + b1[:, None, None, :], approximate=False)
        y = jnp.einsum('ebsh,ehd->ebsd', h, w2) + b2[:, None, None, :]
        out = jnp.einsum('bse,ebsd->bsd', masked, y)
        return out

    def _gn(v, G=32, eps=1e-05):
        B_, C_, H_, W_ = v.shape
        g = v.reshape(B_, G, C_ // G, H_, W_)
        m = jnp.mean(g, axis=(2, 3, 4), keepdims=True)
        s = jnp.var(g, axis=(2, 3, 4), keepdims=True)
        return ((g - m) / jnp.sqrt(s + eps)).reshape(v.shape)

    def _ln_c(v, eps=1e-06):
        m = jnp.mean(v, axis=1, keepdims=True)
        s = jnp.var(v, axis=1, keepdims=True)
        return (v - m) / jnp.sqrt(s + eps)

    def _ln_t(v, eps=1e-05):
        m = jnp.mean(v, axis=-1, keepdims=True)
        s = jnp.var(v, axis=-1, keepdims=True)
        return (v - m) / jnp.sqrt(s + eps)

    def _to_tokens(v):
        B_, C_, H_, W_ = v.shape
        return v.reshape(B_, C_, H_ * W_).transpose(0, 2, 1)

    def _from_tokens(t, like):
        B_, C_, H_, W_ = like.shape
        return t.transpose(0, 2, 1).reshape(B_, C_, H_, W_)
    x = x + _L0_conv_ref(_ln_c(x), L0_conv_w_v, L0_conv_b_v, L0_conv_w_q, L0_conv_b_q, L0_conv_w_k, L0_conv_b_k, L0_conv_w_off1, L0_conv_b_off1, L0_conv_ln_g, L0_conv_ln_b, L0_conv_w_off2, L0_conv_w_out)
    t = _to_tokens(x)
    t = t + _L0_ffn_ref(_ln_t(t), L0_ffn_gate_w, L0_ffn_gate_b, L0_ffn_w1, L0_ffn_b1, L0_ffn_w2, L0_ffn_b2)
    x = _from_tokens(t, x)
    x = x + _L1_conv_ref(_ln_c(x), L1_conv_w77, L1_conv_b77, L1_conv_w53, L1_conv_b53, L1_conv_w35, L1_conv_b35, L1_conv_w7w, L1_conv_w7h, L1_conv_w5w, L1_conv_w5h)
    t = _to_tokens(x)
    t = t + _L1_ffn_ref(_ln_t(t), L1_ffn_gate_w, L1_ffn_gate_b, L1_ffn_w1, L1_ffn_b1, L1_ffn_w2, L1_ffn_b2)
    x = _from_tokens(t, x)
    return x

_drawn_inputs = setup_inputs


def setup_inputs(seed=0):
    import zlib

    import numpy as np

    out = dict(_drawn_inputs(seed))
    spreads = {'L0_conv_b_v': (0.0, 0.1),
     'L0_conv_b_q': (0.0, 0.1),
     'L0_conv_b_k': (0.0, 0.1),
     'L0_conv_b_off1': (0.0, 0.1),
     'L0_conv_ln_g': (1.0, 0.2),
     'L0_conv_ln_b': (0.0, 0.1),
     'L0_ffn_gate_b': (0.0, 0.1),
     'L0_ffn_b1': (0.0, 0.1),
     'L0_ffn_b2': (0.0, 0.1),
     'L1_ffn_gate_b': (0.0, 0.1),
     'L1_ffn_b1': (0.0, 0.1),
     'L1_ffn_b2': (0.0, 0.1)}
    factors = {'L1_conv_w5w': 2.966, 'L1_conv_w5h': 2.857}
    for name, (base, spread) in spreads.items():
        noise = np.random.default_rng([zlib.crc32(name.encode()), seed]).standard_normal(out[name].shape)
        drawn = base * np.exp(spread * noise) if base else spread * noise
        out[name] = jnp.asarray(drawn.astype(out[name].dtype))
    for name, factor in factors.items():
        out[name] = (out[name] * factor).astype(out[name].dtype)
    return out
```

```python
from contextlib import ExitStack

import concourse.bass as bass
from concourse import mybir

F32 = mybir.dt.float32
F32R = mybir.dt.float32r
I32 = mybir.dt.int32
U32 = mybir.dt.uint32
ALU = mybir.AluOpType
ACT = mybir.ActivationFunctionType
AX_X = mybir.AxisListType.X

NB, C, SIDE = 4, 96, 56
PIX = SIDE * SIDE
KSIDE = SIDE // 2
POINTS = KSIDE * KSIDE
E, HID = 4, 384
SCALE = 32 ** -0.5

SUB = 2 * SIDE
NSUB = 4
TILE = NSUB * SUB
TILES = PIX // TILE
SUBS = TILES * NSUB
CHUNKS = E * HID // 128
CPE = HID // 128
G = 3
Q = 4
QPIX = PIX // Q
QROWS = SIDE // Q
QPTS = POINTS // Q
HPTS = QPTS // 2
GQ = 2 * Q
VBLK = QPIX // SUB
YCOL = QPIX // 2
PAD_A, PAD_C = 1, 3
ROWS_A, ROWS_C = QROWS + 2 * PAD_A, QROWS + 2 * PAD_C
LN_C_EPS, LN_T_EPS, TOPK_EPS = 1e-6, 1e-5, 1e-9

HID_RING, H_BANKS, Y_BANKS = 4, 2, 2

SLOTS = [
    dict(lnc=("a", 0)),
    dict(lnc=("a", 1), attn=0),
    dict(lnf=0, lnc=("a", 2), attn=1),
    dict(ffn=0, lnf=1, lnc=("a", 3), attn=2),
    dict(ffn=1, lnf=2, lnc=("c", 0), attn=3),
    dict(ffn=2, lnf=3, lnc=("c", 1), conv=0),
    dict(ffn=3, lnf=4, lnc=("c", 2), conv=1),
    dict(ffn=4, lnf=5, lnc=("c", 3), conv=2),
    dict(ffn=5, lnf=6, conv=3),
    dict(ffn=6, lnf=7),
    dict(ffn=7),
]
_ln_jobs, _lnc_jobs, _last = 0, 0, None
for _s in SLOTS:
    for _k in ("ffn", "lnf", "lnc", "attn", "conv"):
        _s.setdefault(_k, None)
    _s["ln_base"] = _ln_jobs
    _s["lnc_base"] = _lnc_jobs
    _lnc_jobs += TILES * (_s["lnc"] is not None)
    _s["ln_step"] = (_s["lnc"] is not None) + (_s["lnf"] is not None)
    _ln_jobs += TILES * _s["ln_step"]
    _s["before"] = _last
    _last = _s


def metaformer_kernel(nc, a, out):
    with ExitStack() as ctx:
        def sb(name, shape, dt=F32):
            return ctx.enter_context(nc.sbuf_tensor(name, shape, dt))

        def bank(name):
            return ctx.enter_context(nc.psum_tensor(name, [128, 512], F32))

        def sem(name):
            return ctx.enter_context(nc.semaphore(name))

        def scratch(name, shape):
            return nc.dram_tensor(name, shape, F32, kind="Internal").ap()

        norm = {"a": scratch("norm_a", (NB, C, (SIDE + 2 * PAD_A) * SIDE)),
                "c": scratch("norm_c", (NB, C, (SIDE + 2 * PAD_C) * SIDE))}
        pad = {"a": PAD_A, "c": PAD_C}
        x_in = a["x"].rearrange("b c h w -> b c (h w)")
        x_attn = scratch("x_attn", (NB + 1, C, PIX))[1:NB + 1]
        x_ffn0 = scratch("x_ffn0", (NB + 1, C, PIX))[1:NB + 1]
        x_conv = scratch("x_conv", (NB + 1, C, PIX))[1:NB + 1]
        x_out = out.rearrange("b c h w -> b c (h w)")
        value_rows = [scratch(f"value_rows{b}", (PIX, C)) for b in range(NB)]
        gates_dram = scratch("gates_dram", (2 * NB + 1, E * PIX))[1:2 * NB + 1]
        ln_src = {"a": x_in, "c": x_ffn0}
        ffn_src = [x_attn] * NB + [x_conv] * NB
        ffn_dst = [x_ffn0] * NB + [x_out] * NB

        ident = sb("ident", [128, 128])
        before = sb("before", [SUB, E * E])
        q_mask = sb("q_mask", [128, Q])
        ref_pos = sb("ref_pos", [HPTS, 2 * GQ])
        zeros = sb("zeros", [128, PAD_C * SIDE])
        minus_half = sb("minus_half", [128, GQ])
        eps = {"c": sb("eps_c", [128, GQ]), "f": sb("eps_f", [128, GQ])}
        w1h = [sb(f"w1h{l}", [C, E * HID], F32R) for l in range(2)]
        w1l = [sb(f"w1l{l}", [C, E * HID], F32R) for l in range(2)]
        w2 = [sb(f"w2_{l}", [128, CHUNKS, C]) for l in range(2)]
        b1 = [sb(f"b1_{l}", [128, CHUNKS]) for l in range(2)]
        b2 = [sb(f"b2_{l}", [C, E]) for l in range(2)]
        gate_w = [sb(f"gate_w{l}", [C, E]) for l in range(2)]
        gate_b = [sb(f"gate_b{l}", [SUB, E]) for l in range(2)]
        w_a = sb("w_a", [128, 4, G, 9])
        b_a = sb("b_a", [128, 4, G])
        ln_gb = sb("ln_gb", [HPTS, 2, C])
        w_off2 = sb("w_off2", [HPTS, 2, C])
        w_out = sb("w_out", [C, C])
        w_out_q = sb("w_out_q", [C, C * Q])
        w_exp = sb("w_exp", [128, G, Q * C])
        w_c = sb("w_c", [128, G, 49])
        w53 = sb("w53", [128, G, 15])
        w35 = sb("w35", [128, G, 15])
        w7 = sb("w7", [128, 2, G, 7])
        w5 = sb("w5", [128, 2, G, 5])
        b_c = sb("b_c", [128, 3, G])

        ln_x = {"f": sb("ln_x_f", [C, TILE]), "c": sb("ln_x_c", [C, TILE])}
        ln_stats = sb("ln_stats", [SUB, NSUB, 6])
        ln_mv = sb("ln_mv", [SUB, NSUB, 2])
        ln_ve = sb("ln_ve", [SUB, NSUB])
        ln_rstd = sb("ln_rstd", [SUB, NSUB])
        ln_tok = sb("ln_tok", [SUB, NSUB, C])
        ln_cm = {"f": sb("ln_cm_f", [C, TILE]), "c": sb("ln_cm_c", [C, TILE])}

        xh = sb("xh", [C, PIX], F32R)
        xl = sb("xl", [C, PIX], F32R)
        hidden = [sb(f"hidden{i}", [128, TILE]) for i in range(HID_RING)]
        gate_t = [sb(f"gate_t{i}", [C, 2, TILE]) for i in range(2)]
        part = sb("part", [C, E, TILE])
        pair = sb("pair", [C, 2, TILE])
        res = sb("res", [C, TILE])
        ffn_out = sb("ffn_out", [C, TILE])

        SE = E * SUBS
        g_s = sb("g_s", [SUB, E, SUBS])
        g_p = sb("g_p", [SUB, E, SUBS])
        g_m = sb("g_m", [SUB, SUBS])
        g_r = sb("g_r", [SUB, SUBS])
        g_gt = sb("g_gt", [SUB, E, E, SUBS])
        g_eq = sb("g_eq", [SUB, E, E, SUBS])
        g_rank = sb("g_rank", [SUB, E, SUBS])
        g_tr = sb("g_tr", [SE, SUB])

        xq = sb("xq", [128, G, ROWS_C * SIDE])
        acc = [sb(f"acc{i}", [128, G, QPIX]) for i in range(2)]
        value, query = acc
        key = sb("key", [128, G, QPTS])
        off = sb("off", [128, G, QPTS])
        pixels = sb("pixels", [SUB, 4 * GQ * C])
        v_tok = pixels[:, 0:VBLK * Q * C].rearrange("p (q j c) -> p q j c", j=VBLK, q=Q)
        corners = pixels[0:HPTS, :].rearrange("p (k g c) -> p k g c", k=4, g=GQ)
        off_t = sb("off_t", [HPTS, 2, G * 128])
        key_t = sb("key_t", [HPTS, 2, G * 128])
        val_t = sb("val_t", [HPTS, 2, G * 128])
        o_stats = sb("o_stats", [HPTS, GQ, 6])
        o_mv = sb("o_mv", [HPTS, GQ, 2])
        o_ve = sb("o_ve", [HPTS, GQ])
        o_rstd = sb("o_rstd", [HPTS, GQ])
        o_n = sb("o_n", [HPTS, GQ, C])
        o_pos = sb("o_pos", [HPTS, 2, GQ])
        o_int = sb("o_int", [HPTS, 2, GQ], I32)
        o_fl = sb("o_fl", [HPTS, 2, GQ])
        o_gt = sb("o_gt", [HPTS, 2, GQ])
        o_w = sb("o_w", [HPTS, 2, GQ])
        o_u = sb("o_u", [HPTS, 2, GQ])
        o_idf = sb("o_idf", [HPTS, GQ])
        o_idx = sb("o_idx", [HPTS, 4, GQ], U32)
        o_cw = sb("o_cw", [HPTS, 4, GQ])
        kv = sb("kv", [128, G, 128])
        m2 = sb("m2", [128, G, Q * C])
        x_res = sb("x_res", [C, PIX])

        h_ps = [bank(f"h_ps{i}") for i in range(H_BANKS)]
        y_ps = [bank(f"y_ps{i}") for i in range(Y_BANKS)]
        lt_ps, lb_ps, lg_ps, at_ps = bank("lt_ps"), bank("lb_ps"), bank("lg_ps"), bank("at_ps")
        score_ps = lg_ps[0:SUB, 0:SE].rearrange("p (e s) -> p e s", e=E)

        ident_ld = sem("ident_ld")
        const_ld = sem("const_ld")
        w1_ld = sem("w1_ld")
        w1_split = sem("w1_split")
        pool_set = sem("pool_set")
        pads_done = sem("pads_done")
        wexp_ps = sem("wexp_ps")
        w_out_spread = sem("w_out_spread")
        wexp_done = sem("wexp_done")
        wc_done = sem("wc_done")
        wc_chain_sem = sem("wc_chain_sem")
        val_step = sem("val_step")
        ln_loaded = {"f": sem("ln_loaded_f"), "c": sem("ln_loaded_c")}
        ln_turned = sem("ln_turned")
        ln_stat = sem("ln_stat")
        ln_var = sem("ln_var")
        ln_eps = sem("ln_eps")
        ln_scale = sem("ln_scale")
        ln_applied = sem("ln_applied")
        ln_back = sem("ln_back")
        ln_moved = sem("ln_moved")
        scored = sem("scored")
        split_hi = sem("split_hi")
        split = sem("split")
        norm_st = {(k, b): sem(f"norm_st_{k}{b}") for k in "ac" for b in range(NB)}
        h_full = sem("h_full")
        gelu_done = sem("gelu_done")
        hid_used = sem("hid_used")
        y_used = sem("y_used")
        gate_ld = [sem(f"gate_ld{i}") for i in range(2)]
        res_ld = sem("res_ld")
        summed = sem("summed")
        ffn_st = [sem(f"ffn_st{u}") for u in range(2 * NB)]
        g_step = sem("g_step")
        g_exp = sem("g_exp")
        g_scores_read = sem("g_scores_read")
        g_turned = sem("g_turned")
        g_moved = sem("g_moved")
        gates_st = [sem(f"gates_st{u}") for u in range(2 * NB)]
        xq_ld = sem("xq_ld")
        a_step = sem("a_step")
        at_full = sem("at_full")
        at_free = sem("at_free")
        o_step = sem("o_step")
        o_var = sem("o_var")
        o_eps = sem("o_eps")
        o_scale = sem("o_scale")
        o_gelu = sem("o_gelu")
        o_tanh = sem("o_tanh")
        o_index = sem("o_index")
        values_st = sem("values_st")
        gathered = sem("gathered")
        val_done = sem("val_done")
        xres_ld = sem("xres_ld")
        y_step = sem("y_step")
        attn_st = [sem(f"attn_st{b}") for b in range(NB)]
        acc_ld = sem("acc_ld")
        c_step = sem("c_step")
        c_bias = sem("c_bias")
        conv_st = [sem(f"conv_st{b}") for b in range(NB)]

        A_TAPS, Q_TAPS = G * 27, G * 9
        A_ALL = A_TAPS + Q_TAPS
        C_ALL = 49 * G
        AT_USES = 2 + VBLK + 2 + 1 + G + 2 * Q
        AT_OFF, AT_VAL, AT_KEY, AT_KV, AT_M2, AT_Y = 0, 2, 2 + VBLK, 4 + VBLK, 5 + VBLK, 5 + VBLK + G
        O_STEPS = 18
        G_STEPS = 14
        const_count = [0]

        def ffn_at(slot, m):
            return slot["ffn"] * TILES + m

        def lnf_at(slot, m):
            return slot["lnf"] * TILES + m

        def stored(u, tiles):
            return (32 if u == NB else 16) * tiles

        def ln_jobs(slot, m):
            jobs = []
            n = slot["ln_base"] + slot["ln_step"] * m
            if slot["lnc"] is not None:
                jobs.append(("c", n))
                n = n + 1
            if slot["lnf"] is not None:
                jobs.append(("f", n))
            return jobs

        def steps(eng, slot, body, pieces):
            if slot["attn"] is None:
                with eng.Fori(0, TILES - 1) as m:
                    body(m)
                body(TILES - 1)
                return
            with eng.Fori(0, 3) as m:
                body(m, "first")
            pieces[0]()
            with eng.Fori(3, 6) as m:
                body(m, "second")
            pieces[1]()
            body(6)
            pieces[2]()

        def norm_before(slot):
            kind, b = slot["lnc"]
            if b > 0:
                return kind, b - 1
            return ("a", NB - 1) if kind == "c" else None

        block = ctx.enter_context(nc.Block())

        @block.sync
        def _(sp):
            sp.dma_start(ident[:, :], a["c_ident"]).then_inc(ident_ld, 16)
            with nc.allow_non_contiguous_dma("small"):
                sp.wait_ge(pool_set, 2)
                for k in "ac":
                    n = pad[k] * SIDE
                    for b in range(NB):
                        for at in (0, n + PIX):
                            sp.dma_start(norm[k][b][:, at:at + n], zeros[0:C, 0:n]).then_inc(pads_done, 16)

            def load_norm(slot, kind, n, at):
                if not (isinstance(n, int) and n == 0):
                    sp.wait_ge(ln_turned, n)
                if kind == "c":
                    k, b = slot["lnc"]
                    src = ln_src[k][b]
                else:
                    u = slot["lnf"]
                    src = ffn_src[u][u % NB]
                sp.dma_start(ln_x[kind][:, :], src[:, at]).then_inc(ln_loaded[kind], 16)

            def load_gates(slot, k, i, at):
                rows = gates_dram[slot["ffn"]].rearrange("(e t) -> e t", e=E)
                sp.wait_ge(y_used, Y_BANKS * i + E * k)
                sp.dma_start(gate_t[i][:, :, :], rows[2 * i:2 * i + 2, at].partition_broadcast(C))\
                    .then_inc(gate_ld[i], 16)

            def load_res(slot, k, at):
                u = slot["ffn"]
                sp.wait_ge(summed, 3 * k)
                sp.dma_start(res[:, :], ffn_src[u][u % NB][:, at]).then_inc(res_ld, 16)

            def body(m, part_of=None):
                slot = body.slot
                more = not (isinstance(m, int) and m == TILES - 1)
                then = bass.ds(m * TILE + TILE, TILE)
                for kind, n in ln_jobs(slot, m):
                    if more:
                        load_norm(slot, kind, n + 1, then)
                    if kind == "c":
                        k, b = slot["lnc"]
                        sp.wait_ge(ln_moved, n + 1)
                        sp.dma_start(norm[k][b][:, bass.ds(m * TILE + pad[k] * SIDE, TILE)], ln_cm["c"][:, :])\
                            .then_inc(norm_st[k, b], 16)
                if slot["ffn"] is not None:
                    u, k = slot["ffn"], ffn_at(slot, m)
                    if more:
                        for i in range(2):
                            load_gates(slot, k + 1, i, then)
                        load_res(slot, k + 1, then)
                    sp.wait_ge(summed, 3 * k + 3)
                    for c0, c1 in ((C // 2, C), (0, C // 2)) if u == NB else ((0, C),):
                        sp.dma_start(ffn_dst[u][u % NB][c0:c1, bass.ds(m * TILE, TILE)], ffn_out[c0:c1, :])\
                            .then_inc(ffn_st[u], 16)

            def load_quarters(k, b, rows):
                src = norm[k][b].rearrange("(g c) n -> c g n", g=G)
                for q in range(Q):
                    sp.dma_start(xq[q::Q, :, 0:rows * SIDE], src[:, :, q * QPIX:q * QPIX + rows * SIDE])\
                        .then_inc(xq_ld, 16)

            def load_acc(b):
                for q in range(Q):
                    sp.dma_start(acc[b % 2][q::Q], x_ffn0[b].rearrange("(g c) (q n) -> q c g n", g=G, q=Q)[q])\
                        .then_inc(acc_ld, 16)

            for slot in SLOTS:
                body.slot = slot
                start = slice(0, TILE)
                if slot["lnc"] is not None:
                    k, b = slot["lnc"]
                    if k == "c":
                        sp.wait_ge(ffn_st[b], stored(b, TILES))
                    load_norm(slot, "c", slot["ln_base"], start)
                if slot["attn"] is not None:
                    b = slot["attn"]
                    if b == 0:
                        sp.wait_ge(pads_done, 16 * 4 * NB)
                    sp.wait_ge(norm_st["a", b], 16 * TILES)
                    sp.wait_ge(a_step, A_ALL * b)
                    load_quarters("a", b, ROWS_A)
                if slot["conv"] is not None:
                    b = slot["conv"]
                    sp.wait_ge(norm_st["c", b], 16 * TILES)
                    sp.wait_ge(a_step, A_ALL * NB)
                    if b > 0:
                        sp.wait_ge(c_step, G + C_ALL * b)
                    load_quarters("c", b, ROWS_C)
                    if b == 0:
                        sp.wait_ge(at_free, AT_USES * NB)
                        load_acc(0)
                before = slot["before"]
                if before is not None:
                    if before["conv"] is not None:
                        b = before["conv"]
                        sp.wait_ge(c_step, G + C_ALL * (b + 1))
                        for q in range(Q):
                            sp.dma_start(x_conv[b].rearrange("(g c) (q n) -> q c g n", g=G, q=Q)[q],
                                         acc[b % 2][q::Q]).then_inc(conv_st[b], 16)
                    if before["lnf"] is not None:
                        u = before["lnf"]
                        sp.wait_ge(g_moved, u + 1)
                        sp.dma_start(gates_dram[u].rearrange("(s t) -> s t", t=SUB), g_tr[:, :])\
                            .then_inc(gates_st[u], 16)
                if slot["lnf"] is not None:
                    u = slot["lnf"]
                    sp.wait_ge(attn_st[u] if u < NB else conv_st[u - NB], 16 if u < NB else 16 * Q)
                    load_norm(slot, "f", slot["ln_base"], start)
                if slot["ffn"] is not None:
                    k = ffn_at(slot, 0)
                    sp.wait_ge(gates_st[slot["ffn"]], 16)
                    for i in range(2):
                        load_gates(slot, k, i, start)
                    load_res(slot, k, start)
                if slot["attn"] is not None:
                    b = slot["attn"]
                    if b > 0:
                        sp.wait_ge(attn_st[b - 1], 16)
                    sp.dma_start(x_res[:, :], x_in[b]).then_inc(xres_ld, 16)
                if slot["conv"] is not None and slot["conv"] + 1 < NB:
                    if slot["conv"] > 0:
                        sp.wait_ge(conv_st[slot["conv"] - 1], 16 * Q)
                    load_acc(slot["conv"] + 1)

                def first():
                    b = slot["attn"]
                    sp.wait_ge(at_free, AT_USES * b + AT_VAL + VBLK)
                    sp.dma_start(value_rows[b].rearrange("(s p) c -> p s c", p=SUB),
                                 pixels[:, 0:Q * VBLK * C].rearrange("p (s c) -> p s c", c=C))\
                        .then_inc(values_st, 16)

                def last():
                    b = slot["attn"]
                    sp.wait_ge(y_step, 2 * Q * (b + 1))
                    sp.dma_start(x_attn[b], x_res[:, :]).then_inc(attn_st[b], 16)

                steps(sp, slot, body, [first, lambda: None, last])
            for u in range(2 * NB):
                sp.wait_ge(ffn_st[u], stored(u, TILES))

        @block.scalar
        def _(act):
            act.sem_inc(gelu_done, H_BANKS)

            def const(dst, src):
                act.dma_start(dst, src).then_inc(const_ld, 16)
                const_count[0] += 1

            def by_quarter(dst, src, **k):
                for q in range(Q):
                    const(dst[q::Q], src)

            with nc.allow_non_contiguous_dma("small"):
                for n, w in enumerate(("w_v", "w_k", "w_off1", "w_q")):
                    src = a[f"L0_conv_{w}"].rearrange("(g c) o h w -> c g (o h w)", g=G)
                    by_quarter(w_a[:, n], src)
                for n, w in enumerate(("b_v", "b_k", "b_off1", "b_q")):
                    by_quarter(b_a[:, n], a[f"L0_conv_{w}"].rearrange("(g c) -> c g", g=G))
                const(w_out[:, :], a["L0_conv_w_out"])
                const(q_mask[:, :], a["c_q_mask"])
                const(before[:, :], a["c_before"].partition_broadcast(SUB))
                const(ref_pos[:, :], a["c_ref_pos"])
                const(ln_gb[:, 0], a["L0_conv_ln_g"].partition_broadcast(HPTS))
                const(ln_gb[:, 1], a["L0_conv_ln_b"].partition_broadcast(HPTS))
                const(w_off2[:, :], a["L0_conv_w_off2"].partition_broadcast(HPTS))
                for l in range(2):
                    f = f"L{l}_ffn_"
                    act.dma_start(acc[l][0:C, :, :].rearrange("p g n -> p (g n)")[:, 0:E * HID]
                                 .rearrange("p (e h) -> p e h", e=E),
                                 a[f + "w1"].rearrange("e d h -> d e h")).then_inc(w1_ld, 16)
                    const(w2[l][:, :, :], a[f + "w2"].rearrange("e (j p) d -> p (e j) d", p=128))
                    const(b1[l][:, :], a[f + "b1"].rearrange("e (j p) -> p (e j)", p=128))
                    const(b2[l][:, :], a[f + "b2"].rearrange("e d -> d e"))
                    const(gate_w[l][:, :], a[f + "gate_w"])
                    const(gate_b[l][:, :], a[f + "gate_b"].partition_broadcast(SUB))
                for dst, w in ((w_c, "w77"), (w53, "w53"), (w35, "w35")):
                    by_quarter(dst, a[f"L1_conv_{w}"].rearrange("(g c) o h w -> c g (o h w)", g=G))
                for dst, w in ((w7[:, 0], "w7h"), (w7[:, 1], "w7w"), (w5[:, 0], "w5h"), (w5[:, 1], "w5w")):
                    by_quarter(dst, a[f"L1_conv_{w}"].rearrange("(g c) o h w -> c g (o h w)", g=G))
                for n, w in enumerate(("b77", "b53", "b35")):
                    by_quarter(b_c[:, n], a[f"L1_conv_{w}"].rearrange("(g c) -> c g", g=G))

            def add_bias(b):
                act.wait_ge(acc_ld, 16 * Q * (b + 1))
                act.wait_ge(wc_done, 1)
                for g in range(G):
                    act.activation(acc[b % 2][:, g, :], acc[b % 2][:, g, :], ACT.Identity, bias=b_c[:, 0, g:g + 1])\
                        .then_inc(c_bias, 1)

            def move(kind, n, slot, m):
                act.wait_ge(ln_back, n + 1)
                if kind == "f":
                    act.wait_ge(scored, lnf_at(slot, m))
                    act.wait_ge(split, lnf_at(slot, m))
                else:
                    act.wait_ge(norm_st[slot["lnc"]], 16 * m)
                act.copy(ln_cm[kind][:, :], lb_ps[0:C, 0:TILE]).then_inc(ln_moved, 1)

            def body(m, part_of=None):
                slot = body.slot
                jobs = ln_jobs(slot, m)
                at = [4, 9] if len(jobs) == 2 else [7]
                hooks = {c: (lambda kind=kind, n=n: move(kind, n, slot, m)) for (kind, n), c in zip(jobs, at)}
                if slot["ffn"] is None:
                    for c in sorted(hooks):
                        hooks[c]()
                    return
                k, l = ffn_at(slot, m), slot["ffn"] // NB
                for c in range(CHUNKS):
                    act.wait_ge(h_full, CHUNKS * k + c + 1)
                    act.wait_ge(hid_used, CHUNKS * k + c + 1)
                    act.activation(hidden[c % HID_RING][:, :], h_ps[c % H_BANKS][:, 0:TILE], ACT.Gelu,
                                   bias=b1[l][:, c:c + 1]).then_inc(gelu_done, 1)
                    if c in hooks:
                        hooks[c]()

            for slot in SLOTS:
                body.slot = slot
                b = slot["attn"]
                base = AT_USES * (b or 0)
                if slot["lnc"] is not None and norm_before(slot) is not None:
                    act.wait_ge(norm_st[norm_before(slot)], 16 * TILES)

                if slot["conv"] == 0:
                    add_bias(0)

                def full(i):
                    act.wait_ge(at_full, base + i + 1)

                def first():
                    for h in range(2):
                        full(AT_OFF + h)
                        act.copy(off_t[:, h, :], at_ps[0:HPTS, 0:G * 128]).then_inc(at_free, 1)
                    for j in range(VBLK):
                        full(AT_VAL + j)
                        act.copy(v_tok[:, :, j, :].rearrange("p q c -> p c q"),
                                 at_ps[0:SUB, 0:G * 128].rearrange("p (c q) -> p c q", q=Q)).then_inc(at_free, 1)
                    for h in range(2):
                        full(AT_KEY + h)
                        act.copy(key_t[:, h, :], at_ps[0:HPTS, 0:G * 128]).then_inc(at_free, 1)
                    act.wait_ge(o_step, O_STEPS * b + 4)
                    act.activation(o_n[:, :, :], o_n[:, :, :], ACT.Gelu).then_inc(o_gelu, 1)
                    act.wait_ge(o_step, O_STEPS * b + 9)
                    act.activation(o_pos[:, :, :], o_pos[:, :, :], ACT.Tanh).then_inc(o_tanh, 1)

                def middle():
                    full(AT_KV)
                    for h in range(4):
                        r = slice(32 * h, 32 * h + 32)
                        ins = act.activation(kv[r, :, r],
                                             at_ps[r, 0:G * 128].rearrange("p (g n) -> p g n", g=G)[:, :, r],
                                             ACT.Copy, scale=SCALE)
                    ins.then_inc(at_free, 1)
                    for g in range(G):
                        full(AT_M2 + g)
                        act.copy(m2[:, g, :], at_ps[:, 0:Q * C]).then_inc(at_free, 1)

                steps(act, slot, body, [first, middle, lambda: None])
                if slot["conv"] is not None and slot["conv"] + 1 < NB:
                    add_bias(slot["conv"] + 1)
                if slot["lnf"] is not None:
                    u = slot["lnf"]
                    act.wait_ge(g_step, G_STEPS * u + 2)
                    act.activation(g_p[:, :, :], g_s[:, :, :], ACT.Exp).then_inc(g_exp, 1)
                    act.wait_ge(g_turned, u + 1)
                    if u > 0:
                        act.wait_ge(gates_st[u - 1], 16)
                    act.copy(g_tr[:, :], lg_ps[0:SE, 128:128 + SUB]).then_inc(g_moved, 1)

        N_CONST = const_count[0]

        @block.gpsimd
        def _(pool):
            pool.memset(zeros[:, :], 0.0).then_inc(pool_set, 1)
            pool.memset(kv[:, :, :], 0.0).then_inc(pool_set, 1)
            pool.memset(minus_half[:, :], -0.5).then_inc(pool_set, 1)
            pool.memset(eps["c"][:, :], LN_C_EPS).then_inc(pool_set, 1)
            pool.memset(eps["f"][:, :], LN_T_EPS).then_inc(pool_set, 1)
            pool.wait_ge(pool_set, 5)

            def body(m, part_of=None):
                slot = body.slot
                for kind, n in ln_jobs(slot, m):
                    pool.wait_ge(ln_var, n + 1)
                    pool.wait_ge(ln_applied, n)
                    pool.tensor_tensor(ln_ve[:, :], ln_mv[:, :, 1], eps[kind][0:SUB, 0:NSUB], ALU.add).then_inc(ln_eps, 1)
                    pool.wait_ge(ln_eps, n + 1)
                    pool.tensor_tensor(ln_rstd[:, :], ln_ve[:, :], minus_half[0:SUB, 0:NSUB], ALU.pow)\
                        .then_inc(ln_scale, 1)

            for slot in SLOTS:
                body.slot = slot

                def first():
                    b = slot["attn"]
                    pool.wait_ge(o_var, b + 1)
                    pool.tensor_scalar(o_ve[:, :], o_mv[:, :, 1], LN_T_EPS, None, ALU.add).then_inc(o_eps, 1)
                    pool.wait_ge(o_eps, b + 1)
                    pool.tensor_tensor(o_rstd[:, :], o_ve[:, :], minus_half[0:HPTS, :], ALU.pow).then_inc(o_scale, 1)
                    pool.wait_ge(o_index, b + 1)
                    pool.wait_ge(values_st, 16 * (b + 1))
                    for k in range(4):
                        for g in range(GQ):
                            pool.indirect_dma_start(
                                corners[:, k, g, :], None, value_rows[b],
                                bass.IndirectOffsetOnAxis(ap=o_idx[:, k, g:g + 1], axis=0)).then_inc(gathered, 16)

                steps(pool, slot, body, [first, lambda: None, lambda: None])

        @block.tensor
        def _(pe):
            pe.sem_inc(hid_used, HID_RING)
            pe.wait_ge(ident_ld, 16)

            def spread_w_out():
              pe.wait_ge(w_out_spread, 1)
              for g in range(G):
                if g > 0:
                    pe.wait_ge(wexp_done, g)
                pe.matmul(at_ps[:, 0:C], w_out_q[:, g * 128:(g + 1) * 128], ident[0:C, 0:C], start=True, stop=True)\
                    .then_inc(wexp_ps, 1)
              pe.wait_ge(wexp_done, G)

            def turn_in(slot, m, kind, n):
                pe.wait_ge(ln_loaded[kind], 16 * ((lnf_at(slot, m) if kind == "f" else slot["lnc_base"] + m) + 1))
                pe.wait_ge(ln_applied, n)
                for s in range(NSUB):
                    last = pe.transpose(lt_ps[0:SUB, s * C:(s + 1) * C], ln_x[kind][:, s * SUB:(s + 1) * SUB],
                                        ident[0:C, 0:C])
                last.then_inc(ln_turned, 1)

            def turn_back(n):
                pe.wait_ge(ln_applied, n + 1)
                pe.wait_ge(ln_moved, n)
                for s in range(NSUB):
                    last = pe.transpose(lb_ps[0:C, s * SUB:(s + 1) * SUB], ln_tok[:, s, :], ident[0:SUB, 0:SUB])
                last.then_inc(ln_back, 1)

            def scores(slot, m, n):
                u = slot["lnf"]
                pe.wait_ge(ln_moved, n + 1)
                for s in range(NSUB):
                    last = pe.matmul(score_ps[:, :, bass.ds(m * NSUB + s, 1)].rearrange("p e s -> p (e s)"),
                                     ln_cm["f"][:, s * SUB:(s + 1) * SUB], gate_w[u // NB][:, :],
                                     start=True, stop=True)
                last.then_inc(scored, 1)

            def second(slot, m, c):
                k, l = ffn_at(slot, m), slot["ffn"] // NB
                e, j = c // CPE, c % CPE
                pe.wait_ge(gelu_done, H_BANKS + CHUNKS * k + c + 1)
                if j == 0:
                    pe.wait_ge(y_used, E * k + e + 1)
                pe.matmul(y_ps[e % Y_BANKS][0:C, 0:TILE], w2[l][:, c, :], hidden[c % HID_RING][:, :],
                          start=(j == 0), stop=(j == CPE - 1)).then_inc(hid_used, 1)

            def body(m, part_of=None):
                slot = body.slot
                jobs = ln_jobs(slot, m)
                hooks = {}
                at = [(1, 3), (6, 8)] if len(jobs) == 2 else [(3, 6)]
                for (kind, n), (c0, c1) in zip(jobs, at):
                    hooks[c0] = lambda kind=kind, n=n: turn_in(slot, m, kind, n)
                    hooks[c1] = lambda n=n: turn_back(n)
                    if kind == "f":
                        hooks[c1 + 2] = lambda n=n: scores(slot, m, n)
                if slot["ffn"] is None:
                    for c in sorted(hooks):
                        hooks[c]()
                    return
                k, l = ffn_at(slot, m), slot["ffn"] // NB
                pe.wait_ge(split, k + 1)
                for c in range(CHUNKS):
                    pe.wait_ge(gelu_done, CHUNKS * k + c + 1)
                    ps = h_ps[c % H_BANKS][:, 0:TILE]
                    cols = bass.ds(m * TILE, TILE)
                    hi, lo = w1h[l][:, c * 128:(c + 1) * 128], w1l[l][:, c * 128:(c + 1) * 128]
                    pe.matmul(ps, hi, xh[:, cols], start=True, stop=False)
                    pe.matmul(ps, hi, xl[:, cols], start=False, stop=False)
                    pe.matmul(ps, lo, xh[:, cols], start=False, stop=True).then_inc(h_full, 1)
                    if c in hooks:
                        hooks[c]()
                    if c > 0:
                        second(slot, m, c - 1)
                second(slot, m, CHUNKS - 1)

            for slot in SLOTS:
                body.slot = slot
                b = slot["attn"]
                base = AT_USES * (b or 0)

                def use(i):
                    if base + i > 0:
                        pe.wait_ge(at_free, base + i)

                def turn(i, src, width):
                    use(i)
                    for g in range(G):
                        last = pe.transpose(at_ps[0:width, g * 128:(g + 1) * 128], src(g), ident[:, :])
                    last.then_inc(at_full, 1)

                def first():
                    pe.wait_ge(a_step, A_ALL * b + A_TAPS)
                    for h in range(2):
                        turn(AT_OFF + h, lambda g: off[:, g, h * HPTS:(h + 1) * HPTS], HPTS)
                    for j in range(VBLK):
                        turn(AT_VAL + j, lambda g: value[:, g, j * SUB:(j + 1) * SUB], SUB)
                    for h in range(2):
                        turn(AT_KEY + h, lambda g: key[:, g, h * HPTS:(h + 1) * HPTS], HPTS)

                def middle():
                    pe.wait_ge(val_done, b + 1)
                    use(AT_KV)
                    for g in range(G):
                        for h in range(2):
                            last = pe.matmul(at_ps[:, g * 128:(g + 1) * 128], val_t[:, h, g * 128:(g + 1) * 128],
                                             key_t[:, h, g * 128:(g + 1) * 128], start=(h == 0), stop=(h == 1))
                    last.then_inc(at_full, 1)
                    for g in range(G):
                        use(AT_M2 + g)
                        pe.matmul(at_ps[:, 0:Q * C], kv[:, g, :], w_exp[:, g, :], start=True, stop=True)\
                            .then_inc(at_full, 1)

                def last_piece():
                    pe.wait_ge(a_step, A_ALL * (b + 1))
                    for i in range(2 * Q):
                        q, h = i // 2, i % 2
                        use(AT_Y + i)
                        for g in range(G):
                            last = pe.matmul(at_ps[0:C, 0:YCOL], m2[:, g, q * C:(q + 1) * C],
                                             query[:, g, h * YCOL:(h + 1) * YCOL], start=(g == 0), stop=(g == G - 1))
                        last.then_inc(at_full, 1)

                if slot["lnf"] is not None and slot["lnf"] > 0:
                    pe.wait_ge(g_scores_read, slot["lnf"])
                    pe.wait_ge(g_moved, slot["lnf"])
                steps(pe, slot, body, [first, middle, last_piece])
                if slot is SLOTS[0]:
                    pe.wait_ge(const_ld, 16 * N_CONST)
                    spread_w_out()
                if slot["lnf"] is not None:
                    u = slot["lnf"]
                    pe.wait_ge(g_step, G_STEPS * (u + 1))
                    pe.transpose(lg_ps[0:SE, 128:128 + SUB], g_s[:, :, :].rearrange("p e s -> p (e s)"),
                                 ident[0:SUB, 0:SUB]).then_inc(g_turned, 1)

        @block.vector
        def _(dve):
            dve.sem_inc(y_used, Y_BANKS)
            def prepare_weights():
                for l in range(2):
                    raw = acc[l][0:C, :, :].rearrange("p g n -> p (g n)")[:, 0:E * HID]
                    dve.wait_ge(w1_ld, 32)
                    dve.tensor_copy(w1h[l][:, :], raw).then_inc(w1_split, 1)
                    dve.wait_ge(w1_split, 2 * l + 1)
                    dve.tensor_tensor(w1l[l][:, :], raw, w1h[l][:, :].bitcast(F32), ALU.subtract).then_inc(w1_split, 1)
                dve.wait_ge(const_ld, 16 * N_CONST)
                dve.tensor_copy(w_out_q[:, :].rearrange("p (c q) -> p c q", q=Q), w_out[:, :].unsqueeze(2).broadcast_to([C, C, Q]))\
                    .then_inc(w_out_spread, 1)
                for g in range(G):
                    dve.wait_ge(wexp_ps, g + 1)
                    for q in range(Q):
                        ins = dve.tensor_scalar(w_exp[:, g, q * C:(q + 1) * C], at_ps[:, 0:C], q_mask[:, q:q + 1], None,
                                                ALU.mult)
                    ins.then_inc(wexp_done, 1)
                n_wc = [0]

                def wc_chain(ins):
                    ins.then_inc(wc_chain_sem, 1)
                    n_wc[0] += 1
                    dve.wait_ge(wc_chain_sem, n_wc[0])

                wcv = w_c[:, :, :].rearrange("p g (h w) -> p g h w", w=7)
                v53 = w53[:, :, :].rearrange("p g (h w) -> p g h w", w=3)
                v35 = w35[:, :, :].rearrange("p g (h w) -> p g h w", w=5)
                wc_chain(dve.tensor_tensor(wcv[:, :, 1:6, 2:5], wcv[:, :, 1:6, 2:5], v53, ALU.add))
                wc_chain(dve.tensor_tensor(wcv[:, :, 2:5, 1:6], wcv[:, :, 2:5, 1:6], v35, ALU.add))
                for w, n in ((w7, 7), (w5, 5)):
                    o = (7 - n) // 2
                    for g in range(G):
                        for i in range(n):
                            row = wcv[:, g, o + i, o:o + n]
                            ins = dve.scalar_tensor_tensor(row, w[:, 1, g, :], w[:, 0, g, i:i + 1], row, ALU.mult, ALU.add)
                    wc_chain(ins)
                wc_chain(dve.tensor_tensor(b_c[:, 0], b_c[:, 0], b_c[:, 1], ALU.add))
                dve.tensor_tensor(b_c[:, 0], b_c[:, 0], b_c[:, 2], ALU.add).then_inc(wc_done, 1)
                dve.wait_ge(wc_done, 1)

            def normalize(n):
                dve.wait_ge(ln_turned, n + 1)
                for s in range(NSUB):
                    ins = dve.bn_stats(ln_stats[:, s, :], lt_ps[0:SUB, s * C:(s + 1) * C])
                ins.then_inc(ln_stat, 1)
                dve.wait_ge(pool_set, 5)
                dve.wait_ge(ln_stat, n + 1)
                for s in range(NSUB):
                    ins = dve.bn_aggr(ln_mv[:, s, :], ln_stats[:, s, :])
                ins.then_inc(ln_var, 1)

            def apply(n):
                dve.wait_ge(ln_scale, n + 1)
                dve.wait_ge(ln_back, n)
                for s in range(NSUB):
                    ins = dve.tensor_scalar(ln_tok[:, s, :], lt_ps[0:SUB, s * C:(s + 1) * C], ln_mv[:, s, 0:1],
                                            ln_rstd[:, s:s + 1], ALU.subtract, ALU.mult)
                ins.then_inc(ln_applied, 1)

            def split_tile(slot, m, n):
                i = lnf_at(slot, m)
                dve.wait_ge(ln_moved, n + 1)
                if slot["ffn"] is not None:
                    dve.wait_ge(h_full, CHUNKS * ffn_at(slot, m) + CHUNKS)
                cols = bass.ds(m * TILE, TILE)
                dve.tensor_copy(xh[:, cols], ln_cm["f"][:, :]).then_inc(split_hi, 1)
                dve.wait_ge(split_hi, i + 1)
                dve.tensor_tensor(xl[:, cols], ln_cm["f"][:, :], xh[:, cols].bitcast(F32), ALU.subtract)\
                    .then_inc(split, 1)

            def combine(slot, m, e):
                k, l = ffn_at(slot, m), slot["ffn"] // NB
                dve.wait_ge(hid_used, HID_RING + CHUNKS * k + CPE * (e + 1))
                dve.wait_ge(gate_ld[e // 2], 16 * (k + 1))
                if e == 0:
                    dve.wait_ge(summed, 3 * k)
                dve.scalar_tensor_tensor(part[:, e, :], y_ps[e % Y_BANKS][0:C, 0:TILE], b2[l][:, e:e + 1],
                                         gate_t[e // 2][:, e % 2, :], ALU.add, ALU.mult).then_inc(y_used, 1)

            def sum_up(slot, m):
                k, u = ffn_at(slot, m), slot["ffn"]
                dve.wait_ge(y_used, Y_BANKS + E * (k + 1))
                dve.tensor_tensor(pair[:, :, :], part[:, 0:2, :], part[:, 2:4, :], ALU.add).then_inc(summed, 1)
                dve.wait_ge(summed, 3 * k + 1)
                dve.tensor_tensor(part[:, 0, :], pair[:, 0, :], pair[:, 1, :], ALU.add).then_inc(summed, 1)
                dve.wait_ge(summed, 3 * k + 2)
                dve.wait_ge(res_ld, 16 * (k + 1))
                dve.wait_ge(ffn_st[u], stored(u, m))
                dve.tensor_tensor(ffn_out[:, :], part[:, 0, :], res[:, :], ALU.add).then_inc(summed, 1)

            def taps3(out_ap, in_ap, n, g, base, at, step, stride):
                side = SIDE // stride
                rows_in = in_ap.rearrange("p (r x) -> p r x", x=SIDE)
                rows_out = out_ap.rearrange("p (r x) -> p r x", x=side)
                order = [(0, 1)] + [(dy, dx) for dy in range(3) for dx in range(3) if (dy, dx) != (0, 1)]
                done = []
                for i, (dy, dx) in enumerate(order):
                    x0 = 1 if dx == 0 else 0
                    x1 = side - 1 if dx == 2 and stride == 1 else side
                    c0 = stride * x0 + dx - 1
                    nr = QROWS // stride
                    src = rows_in[:, dy:dy + stride * (nr - 1) + 1:stride, c0:c0 + stride * (x1 - x0 - 1) + 1:stride]
                    dst = rows_out[:, :, x0:x1]
                    w = w_a[:, n, g, dy * 3 + dx:dy * 3 + dx + 1]

                    def op(i=i, src=src, dst=dst, w=w):
                        if i == 0:
                            ins = dve.tensor_scalar(dst, src, w, b_a[:, n, g], ALU.mult, ALU.add)
                        else:
                            dve.wait_ge(a_step, base + at + step * (i - 1) + 1)
                            ins = dve.scalar_tensor_tensor(dst, src, w, dst, ALU.mult, ALU.add)
                        ins.then_inc(a_step, 1)
                    done.append(op)
                return done

            def attn_taps(slot, m, part_of):
                base = A_ALL * slot["attn"]
                g = bass.ds(m if part_of == "first" else m - 3, 1)
                src = xq[:, g, 0:ROWS_A * SIDE].rearrange("p g n -> p (g n)")

                def one(t):
                    return t[:, g, :].rearrange("p g n -> p (g n)")
                if part_of == "first":
                    base = base + 27 * m
                    lists = [taps3(one(value), src, 0, g, base, 0, 3, 1), taps3(one(key), src, 1, g, base, 1, 3, 2),
                             taps3(one(off), src, 2, g, base, 2, 3, 2)]
                    return [op for three in zip(*lists) for op in three]
                base = base + A_TAPS + 9 * (m - 3)
                return taps3(one(query), src, 3, g, base, 0, 1, 1)

            def conv_taps(slot, m):
                b = slot["conv"]
                ops = []
                for i, dx in enumerate((3, 0, 1, 2, 4, 5, 6)):
                    x0, x1 = max(0, 3 - dx), SIDE - max(0, dx - 3)
                    for g in range(G):
                        src = xq[:, g, bass.ds(m * SIDE, QPIX)].rearrange("p (r x) -> p r x", x=SIDE)[
                            :, :, x0 + dx - 3:x1 + dx - 3]
                        dst = acc[b % 2][:, g, :].rearrange("p (r x) -> p r x", x=SIDE)[:, :, x0:x1]
                        w = w_c[:, g, bass.ds(m * 7 + dx, 1)]

                        def op(n=G * i + g, src=src, dst=dst, w=w):
                            dve.wait_ge(c_step, C_ALL * b + 7 * G * m + n + 1)
                            dve.scalar_tensor_tensor(dst, src, w, dst, ALU.mult, ALU.add).then_inc(c_step, 1)
                        ops.append(op)
                return ops

            def body(m, part_of=None):
                slot = body.slot
                ops = []
                if part_of is not None:
                    ops = attn_taps(slot, m, part_of)
                if slot["conv"] is not None:
                    ops = conv_taps(slot, m)
                jobs = ln_jobs(slot, m)
                work = []
                for kind, n in jobs:
                    work.append(lambda n=n: normalize(n))
                    work.append(lambda n=n: apply(n))
                if slot["ffn"] is not None:
                    c = [lambda e=e: combine(slot, m, e) for e in range(E)]
                    w = work + [lambda: None] * (4 - len(work))
                    work = [w[0], w[1], c[0], w[2], w[3], c[1], c[2]]
                    end = [c[3], lambda: sum_up(slot, m)]
                else:
                    end = []
                if slot["lnf"] is not None:
                    n = jobs[-1][1]
                    end = [lambda: split_tile(slot, m, n)] + end
                work = work + end
                at = 0
                for i, w in enumerate(work):
                    till = len(ops) * (i + 1) // max(1, len(work))
                    for op in ops[at:till]:
                        op()
                    at = till
                    w()

            def chain(b, n0):
                n = [n0]

                def link(ins, wait=True):
                    ins.then_inc(o_step, 1)
                    n[0] += 1
                    if wait:
                        dve.wait_ge(o_step, O_STEPS * b + n[0])
                return link

            for slot in SLOTS:
                body.slot = slot
                b = slot["attn"]

                def first():
                    base = AT_USES * b
                    dve.wait_ge(at_free, base + AT_OFF + 2)
                    link = chain(b, 0)
                    v = off_t[:, :, :].rearrange("p h (c q) -> p h q c", q=Q)
                    for h in range(2):
                        for q in range(Q):
                            ins = dve.bn_stats(o_stats[:, h * Q + q, :], v[:, h, q, :])
                    link(ins)
                    for i in range(GQ):
                        ins = dve.bn_aggr(o_mv[:, i, :], o_stats[:, i, :])
                    ins.then_inc(o_var, 1)
                    dve.wait_ge(o_scale, b + 1)
                    for h in range(2):
                        for q in range(Q):
                            i = h * Q + q
                            ins = dve.tensor_scalar(o_n[:, i, :], v[:, h, q, :], o_mv[:, i, 0:1], o_rstd[:, i:i + 1],
                                                    ALU.subtract, ALU.mult)
                    link(ins)
                    full = [HPTS, GQ, C]
                    link(dve.tensor_tensor(o_n[:, :, :], o_n[:, :, :], ln_gb[:, 0].unsqueeze(1).broadcast_to(full),
                                           ALU.mult))
                    link(dve.tensor_tensor(o_n[:, :, :], o_n[:, :, :], ln_gb[:, 1].unsqueeze(1).broadcast_to(full),
                                           ALU.add))
                    dve.wait_ge(o_gelu, b + 1)
                    tmp = off_t[:, :, :].rearrange("p h n -> p (h n)").rearrange("p (g c) -> p g c", c=C)
                    for i in range(2):
                        link(dve.tensor_tensor(tmp, o_n[:, :, :], w_off2[:, i].unsqueeze(1).broadcast_to(full),
                                               ALU.mult))
                        link(dve.tensor_reduce(o_pos[:, i, :], tmp, AX_X, ALU.add))
                    link(dve.tensor_tensor(o_pos[:, :, :], o_pos[:, :, :],
                                           ref_pos[:, :].rearrange("p (i g) -> p i g", i=2), ALU.add))
                    dve.wait_ge(o_tanh, b + 1)
                    link(dve.tensor_scalar(o_pos[:, :, :], o_pos[:, :, :], 1.0, 0.5 * (SIDE - 1), ALU.add, ALU.mult))
                    link(dve.tensor_copy(o_int[:, :, :], o_pos[:, :, :]))
                    link(dve.tensor_copy(o_fl[:, :, :], o_int[:, :, :]))
                    link(dve.tensor_tensor(o_gt[:, :, :], o_fl[:, :, :], o_pos[:, :, :], ALU.is_gt))
                    link(dve.tensor_tensor(o_fl[:, :, :], o_fl[:, :, :], o_gt[:, :, :], ALU.subtract))
                    link(dve.tensor_scalar(o_fl[:, :, :], o_fl[:, :, :], 0.0, float(SIDE - 2), ALU.max, ALU.min))
                    dve.tensor_tensor(o_w[:, :, :], o_pos[:, :, :], o_fl[:, :, :], ALU.subtract)
                    link(dve.scalar_tensor_tensor(o_idf[:, :], o_fl[:, 0, :], float(SIDE), o_fl[:, 1, :],
                                                  ALU.mult, ALU.add))
                    link(dve.tensor_scalar(o_u[:, :, :], o_w[:, :, :], -1.0, 1.0, ALU.mult, ALU.add))
                    for k, d in enumerate((0, 1, SIDE, SIDE + 1)):
                        ins = dve.tensor_scalar(o_idx[:, k, :], o_idf[:, :], float(d), None, ALU.add)
                    ins.then_inc(o_index, 1)
                    for k, (wy, wx) in enumerate(((o_u, o_u), (o_u, o_w), (o_w, o_u), (o_w, o_w))):
                        ins = dve.tensor_tensor(o_cw[:, k, :], wy[:, 0, :], wx[:, 1, :], ALU.mult)
                    link(ins)

                def middle():
                    dve.wait_ge(gathered, 16 * 4 * GQ * (b + 1))
                    vt = val_t[:, :, :].rearrange("p h (c q) -> p h q c", q=Q)
                    for k in range(4):
                        if k > 0:
                            dve.wait_ge(val_step, 4 * b + k)
                        for h in range(2):
                            for q in range(Q):
                                i = h * Q + q
                                if k == 0:
                                    ins = dve.tensor_scalar(vt[:, h, q, :], corners[:, k, i, :], o_cw[:, k, i:i + 1],
                                                            None, ALU.mult)
                                else:
                                    ins = dve.scalar_tensor_tensor(vt[:, h, q, :], corners[:, k, i, :],
                                                                   o_cw[:, k, i:i + 1], vt[:, h, q, :],
                                                                   ALU.mult, ALU.add)
                        ins.then_inc(val_step, 1)
                    dve.wait_ge(val_step, 4 * b + 4)
                    dve.sem_inc(val_done, 1)

                def last_piece():
                    base = AT_USES * b
                    dve.wait_ge(xres_ld, 16 * (b + 1))
                    for i in range(2 * Q):
                        dve.wait_ge(at_full, base + AT_Y + i + 1)
                        cols = slice(i * YCOL, (i + 1) * YCOL)
                        dve.tensor_tensor(x_res[:, cols], at_ps[0:C, 0:YCOL], x_res[:, cols], ALU.add)\
                            .then_inc(at_free, 1)
                    dve.wait_ge(at_free, base + AT_USES)
                    dve.sem_inc(y_step, 2 * Q)

                if b is not None:
                    dve.wait_ge(xq_ld, 16 * Q * (b + 1))
                if slot["conv"] is not None:
                    dve.wait_ge(xq_ld, 16 * Q * (NB + slot["conv"] + 1))
                    dve.wait_ge(c_bias, G * (slot["conv"] + 1))
                if slot["conv"] == 0:
                    dve.sem_inc(c_step, G)
                if slot["ffn"] is not None and slot["ffn"] > 0:
                    dve.wait_ge(ffn_st[slot["ffn"] - 1], stored(slot["ffn"] - 1, TILES))
                steps(dve, slot, body, [first, middle, last_piece])
                if slot is SLOTS[0]:
                    prepare_weights()
                if slot["lnf"] is not None:
                    u = slot["lnf"]
                    n = [G_STEPS * u]

                    def link(ins):
                        ins.then_inc(g_step, 1)
                        n[0] += 1
                        dve.wait_ge(g_step, n[0])

                    by_e = [SUB, E, SUBS]
                    dve.wait_ge(scored, TILES * (u + 1))
                    dve.tensor_tensor(g_s[:, :, :], score_ps, gate_b[u // NB][:, :].unsqueeze(2).broadcast_to(by_e),
                                      ALU.add).then_inc(g_scores_read, 1)
                    dve.wait_ge(g_scores_read, u + 1)
                    link(dve.tensor_reduce(g_m[:, :], g_s[:, :, :].rearrange("p e s -> p s e"), AX_X, ALU.max))
                    link(dve.tensor_tensor(g_s[:, :, :], g_s[:, :, :], g_m[:, :].unsqueeze(1).broadcast_to(by_e),
                                           ALU.subtract))
                    dve.wait_ge(g_exp, u + 1)
                    link(dve.tensor_reduce(g_m[:, :], g_p[:, :, :].rearrange("p e s -> p s e"), AX_X, ALU.add))
                    link(dve.reciprocal(g_r[:, :], g_m[:, :]))
                    link(dve.tensor_tensor(g_p[:, :, :], g_p[:, :, :], g_r[:, :].unsqueeze(1).broadcast_to(by_e),
                                           ALU.mult))
                    for i in range(E):
                        p_i = g_p[:, i, :].unsqueeze(1).broadcast_to(by_e)
                        dve.tensor_tensor(g_gt[:, i], p_i, g_p[:, :, :], ALU.is_gt)
                        ins = dve.tensor_tensor(g_eq[:, i], p_i, g_p[:, :, :], ALU.is_equal)
                    link(ins)
                    for i in range(E):
                        mask = before[:, i * E:(i + 1) * E].unsqueeze(2).broadcast_to(by_e)
                        ins = dve.tensor_tensor(g_eq[:, i], g_eq[:, i], mask, ALU.mult)
                    link(ins)
                    link(dve.tensor_tensor(g_gt[:, :, :, :].rearrange("p i j s -> p (i j s)"),
                                           g_gt[:, :, :, :].rearrange("p i j s -> p (i j s)"),
                                           g_eq[:, :, :, :].rearrange("p i j s -> p (i j s)"), ALU.add))
                    link(dve.tensor_reduce(g_rank[:, :, :].rearrange("p j s -> p (j s)"),
                                           g_gt[:, :, :, :].rearrange("p i j s -> p (j s) i"), AX_X, ALU.add))
                    link(dve.scalar_tensor_tensor(g_p[:, :, :].rearrange("p e s -> p (e s)"),
                                                  g_rank[:, :, :].rearrange("p e s -> p (e s)"), 1.5,
                                                  g_p[:, :, :].rearrange("p e s -> p (e s)"), ALU.is_lt, ALU.mult))
                    link(dve.tensor_reduce(g_m[:, :], g_p[:, :, :].rearrange("p e s -> p s e"), AX_X, ALU.add))
                    link(dve.tensor_scalar(g_m[:, :], g_m[:, :], TOPK_EPS, None, ALU.add))
                    link(dve.reciprocal(g_r[:, :], g_m[:, :]))
                    link(dve.tensor_tensor(g_s[:, :, :], g_p[:, :, :], g_r[:, :].unsqueeze(1).broadcast_to(by_e),
                                           ALU.mult))


def _constants():
    import numpy as np
    i = np.arange(E)
    before = (i[:, None] < i[None, :]).astype(np.float32).reshape(E * E)
    q_mask = (np.arange(128)[:, None] % Q == np.arange(Q)[None, :]).astype(np.float32)
    ref = (np.linspace(0.5, KSIDE - 0.5, KSIDE).astype(np.float32) / np.float32(KSIDE) * 2 - 1).astype(np.float32)
    point = (np.arange(Q)[None, None, :] * QPTS + np.arange(2)[None, :, None] * HPTS
             + np.arange(HPTS)[:, None, None]).reshape(HPTS, GQ)
    ref_pos = np.stack([ref[point // KSIDE], ref[point % KSIDE]], axis=1).reshape(HPTS, 2 * GQ)
    return {"c_ident": np.eye(128, dtype=np.float32), "c_before": before, "c_q_mask": q_mask,
            "c_ref_pos": np.ascontiguousarray(ref_pos)}


def kernel(**inputs):
    import numpy as np
    import concourse.bacc as bacc
    from concourse.bass_utils import run_bass_kernel_spmd

    nc = bacc.Bacc("TRN2", target_bir_lowering=False, num_devices=1)
    arrays, aps = {}, {}
    for name, value in {**inputs, **_constants()}.items():
        v = np.ascontiguousarray(value)
        arrays[f"in_{name}"] = v
        aps[name] = nc.dram_tensor(f"in_{name}", v.shape, mybir.dt.from_np(v.dtype), kind="ExternalInput").ap()
    out = nc.dram_tensor("out_x", (NB, C, SIDE, SIDE), F32, kind="ExternalOutput").ap()
    metaformer_kernel(nc, aps, out)
    r = run_bass_kernel_spmd(nc, [arrays], core_ids=[0])
    return r.results[0]["out_x"]
```

```python
import math
from contextlib import ExitStack

import concourse.bass as bass
from concourse import mybir

F32 = mybir.dt.float32
F32R = mybir.dt.float32r
I32 = mybir.dt.int32
U32 = mybir.dt.uint32
ALU = mybir.AluOpType
ACT = mybir.ActivationFunctionType
AX_X = mybir.AxisListType.X

NB, C, SIDE = 4, 96, 56
PIX = SIDE * SIDE
KSIDE = SIDE // 2
POINTS = KSIDE * KSIDE
E, HID = 4, 384
SCALE = 32 ** -0.5

SUB = 2 * SIDE
NSUB = 4
TILE = NSUB * SUB
TILES = PIX // TILE
SUBS = TILES * NSUB
CHUNKS = E * HID // 128
CPE = HID // 128
G = 3
Q = 4
QPIX = PIX // Q
QROWS = SIDE // Q
QPTS = POINTS // Q
HPTS = QPTS // 2
GQ = 2 * Q
VBLK = QPIX // SUB
YCOL = QPIX // 2
PAD_A, PAD_C = 1, 3
ROWS_A, ROWS_C = QROWS + 2 * PAD_A, QROWS + 2 * PAD_C
LN_C_EPS, LN_T_EPS, TOPK_EPS = 1e-6, 1e-5, 1e-9

HID_RING, H_BANKS, Y_BANKS = 4, 2, 2

SLOTS = [
    dict(lnc=("a", 0)),
    dict(lnc=("a", 1), attn=0),
    dict(lnf=0, lnc=("a", 2), attn=1),
    dict(ffn=0, lnf=1, lnc=("a", 3), attn=2),
    dict(ffn=1, lnf=2, lnc=("c", 0), attn=3),
    dict(ffn=2, lnf=3, lnc=("c", 1), conv=0),
    dict(ffn=3, lnf=4, lnc=("c", 2), conv=1),
    dict(ffn=4, lnf=5, lnc=("c", 3), conv=2),
    dict(ffn=5, lnf=6, conv=3),
    dict(ffn=6, lnf=7),
    dict(ffn=7),
]
_ln_jobs, _lnc_jobs, _last = 0, 0, None
for _s in SLOTS:
    for _k in ("ffn", "lnf", "lnc", "attn", "conv"):
        _s.setdefault(_k, None)
    _s["ln_base"] = _ln_jobs
    _s["lnc_base"] = _lnc_jobs
    _lnc_jobs += TILES * (_s["lnc"] is not None)
    _s["ln_step"] = (_s["lnc"] is not None) + (_s["lnf"] is not None)
    _ln_jobs += TILES * _s["ln_step"]
    _s["before"] = _last
    _last = _s


def metaformer_kernel(nc, a, out):
    with ExitStack() as ctx:
        def sb(name, shape, dt=F32):
            return ctx.enter_context(nc.sbuf_tensor(name, shape, dt))

        def bank(name):
            return ctx.enter_context(nc.psum_tensor(name, [128, 512], F32))

        def sem(name):
            return ctx.enter_context(nc.semaphore(name))

        def scratch(name, shape):
            return nc.dram_tensor(name, shape, F32, kind="Internal").ap()

        norm = {"a": scratch("norm_a", (NB, C, (SIDE + 2 * PAD_A) * SIDE)),
                "c": scratch("norm_c", (NB, C, (SIDE + 2 * PAD_C) * SIDE))}
        pad = {"a": PAD_A, "c": PAD_C}
        x_in = a["x"].rearrange("b c h w -> b c (h w)")
        x_attn = scratch("x_attn", (NB + 1, C, PIX))[1:NB + 1]
        x_ffn0 = scratch("x_ffn0", (NB + 1, C, PIX))[1:NB + 1]
        x_conv = scratch("x_conv", (NB + 1, C, PIX))[1:NB + 1]
        x_out = out.rearrange("b c h w -> b c (h w)")
        value_rows = [scratch(f"value_rows{b}", (PIX, C)) for b in range(NB)]
        gates_dram = scratch("gates_dram", (2 * NB + 1, E * PIX))[1:2 * NB + 1]
        ln_src = {"a": x_in, "c": x_ffn0}
        ffn_src = [x_attn] * NB + [x_conv] * NB
        ffn_dst = [x_ffn0] * NB + [x_out] * NB

        ident = sb("ident", [128, 128])
        before = sb("before", [SUB, E * E])
        q_mask = sb("q_mask", [128, Q])
        ref_pos = sb("ref_pos", [HPTS, 2 * GQ])
        zeros = sb("zeros", [128, PAD_C * SIDE])
        minus_half = sb("minus_half", [128, GQ])
        eps = {"c": sb("eps_c", [128, GQ]), "f": sb("eps_f", [128, GQ])}
        w1h = [sb(f"w1h{l}", [C, E * HID], F32R) for l in range(2)]
        w1l = [sb(f"w1l{l}", [C, E * HID], F32R) for l in range(2)]
        w2 = [sb(f"w2_{l}", [128, CHUNKS, C]) for l in range(2)]
        b1 = [sb(f"b1_{l}", [128, CHUNKS]) for l in range(2)]
        b2 = [sb(f"b2_{l}", [C, E]) for l in range(2)]
        gate_w = [sb(f"gate_w{l}", [C, E]) for l in range(2)]
        gate_b = [sb(f"gate_b{l}", [SUB, E]) for l in range(2)]
        ln_gb = sb("ln_gb", [HPTS, 2, C])
        w_off2 = sb("w_off2", [HPTS, 2, C])
        w_out = sb("w_out", [C, C])
        w_out_q = sb("w_out_q", [C, C * Q])
        w_exp = sb("w_exp", [128, G, Q * C])
        conv_w = {"w_a": (4, G, 9), "b_a": (4, G), "w_c": (G, 49), "w53": (G, 15), "w35": (G, 15),
                  "w7": (2, G, 7), "w5": (2, G, 5), "b_c": (3, G)}
        CONV_W = sum(math.prod(shape) for shape in conv_w.values())
        rows_w = sb("rows_w", [32, CONV_W])
        all_w = sb("all_w", [128, CONV_W])
        to_quarters = sb("to_quarters", [32, 128])

        def views(tile):
            at, parts = 0, []
            for shape in conv_w.values():
                n = math.prod(shape)
                names = "xyz"[:len(shape)]
                parts.append(tile[:, at:at + n].rearrange(
                    f"p ({' '.join(names)}) -> p {' '.join(names)}", **dict(zip(names, shape))))
                at += n
            return parts

        w_a, b_a, w_c, w53, w35, w7, w5, b_c = views(all_w)

        ln_x = {"f": sb("ln_x_f", [C, TILE]), "c": sb("ln_x_c", [C, TILE])}
        ln_stats = sb("ln_stats", [SUB, NSUB, 6])
        ln_mv = sb("ln_mv", [SUB, NSUB, 2])
        ln_ve = sb("ln_ve", [SUB, NSUB])
        ln_neg = sb("ln_neg", [SUB, NSUB])
        ln_bias = sb("ln_bias", [SUB, NSUB])
        minus_one = sb("minus_one", [SUB, NSUB])
        ln_rstd = sb("ln_rstd", [SUB, NSUB])
        ln_tok = sb("ln_tok", [SUB, NSUB, C])
        ln_cm = {"f": sb("ln_cm_f", [C, TILE]), "c": sb("ln_cm_c", [C, TILE])}

        xh = sb("xh", [C, PIX], F32R)
        xl = sb("xl", [C, PIX], F32R)
        hidden = [sb(f"hidden{i}", [128, TILE]) for i in range(HID_RING)]
        gate_t = [sb(f"gate_t{i}", [C, 2, TILE]) for i in range(2)]
        part = sb("part", [C, E, TILE])
        pair = sb("pair", [C, 2, TILE])
        res = sb("res", [C, TILE])
        ffn_out = sb("ffn_out", [C, TILE])

        raw_w1_1 = sb("raw_w1_1", [C, E * HID])
        raw_w1 = [part[:, :, :].rearrange("p e n -> p (e n)")[:, 0:E * HID], raw_w1_1[:, :]]

        SE = E * SUBS
        g_s = sb("g_s", [SUB, E, SUBS])
        g_p = sb("g_p", [SUB, E, SUBS])
        g_m = sb("g_m", [SUB, SUBS])
        g_r = sb("g_r", [SUB, SUBS])
        g_gt = sb("g_gt", [SUB, E, E, SUBS])
        g_eq = sb("g_eq", [SUB, E, E, SUBS])
        g_rank = sb("g_rank", [SUB, E, SUBS])
        g_tr = sb("g_tr", [SE, SUB])

        xq = sb("xq", [128, G, ROWS_C * SIDE])
        acc = [sb(f"acc{i}", [128, G, QPIX]) for i in range(2)]
        value, query = acc
        key = sb("key", [128, G, QPTS])
        off = sb("off", [128, G, QPTS])
        pixels = sb("pixels", [SUB, 4 * GQ * C])
        v_tok = pixels[:, 0:VBLK * Q * C].rearrange("p (q j c) -> p q j c", j=VBLK, q=Q)
        corners = pixels[0:HPTS, :].rearrange("p (k g c) -> p k g c", k=4, g=GQ)
        off_t = sb("off_t", [HPTS, 2, G * 128])
        key_t = sb("key_t", [HPTS, 2, G * 128])
        val_t = sb("val_t", [HPTS, 2, G * 128])
        o_stats = sb("o_stats", [HPTS, GQ, 6])
        o_mv = sb("o_mv", [HPTS, GQ, 2])
        o_ve = sb("o_ve", [HPTS, GQ])
        o_rstd = sb("o_rstd", [HPTS, GQ])
        o_n = sb("o_n", [HPTS, GQ, C])
        o_pos = sb("o_pos", [HPTS, 2, GQ])
        o_int = sb("o_int", [HPTS, 2, GQ], I32)
        o_fl = sb("o_fl", [HPTS, 2, GQ])
        o_gt = sb("o_gt", [HPTS, 2, GQ])
        o_w = sb("o_w", [HPTS, 2, GQ])
        o_u = sb("o_u", [HPTS, 2, GQ])
        o_idf = sb("o_idf", [HPTS, GQ])
        o_idx = sb("o_idx", [HPTS, 4, GQ], U32)
        o_cw = sb("o_cw", [HPTS, 4, GQ])
        kv = sb("kv", [128, G, 128])
        m2 = sb("m2", [128, G, Q * C])
        x_res = sb("x_res", [C, PIX])

        h_ps = [bank(f"h_ps{i}") for i in range(H_BANKS)]
        y_ps = [bank(f"y_ps{i}") for i in range(Y_BANKS)]
        lt_ps, lb_ps, lg_ps, at_ps = bank("lt_ps"), bank("lb_ps"), bank("lg_ps"), bank("at_ps")
        score_ps = lg_ps[0:SUB, 0:SE].rearrange("p (e s) -> p e s", e=E)

        ident_ld = sem("ident_ld")
        taps_ld = sem("taps_ld")
        const_ld = sem("const_ld")
        taps_spread = sem("taps_spread")
        taps_set = sem("taps_set")
        w1_split = sem("w1_split")
        pool_set = sem("pool_set")
        pads_done = sem("pads_done")
        wexp_ps = sem("wexp_ps")
        w_out_spread = sem("w_out_spread")
        wexp_done = sem("wexp_done")
        wc_done = sem("wc_done")
        wc_chain_sem = sem("wc_chain_sem")
        val_step = sem("val_step")
        ln_loaded = {"f": sem("ln_loaded_f"), "c": sem("ln_loaded_c")}
        ln_turned = sem("ln_turned")
        ln_stat = sem("ln_stat")
        ln_var = sem("ln_var")
        ln_eps = sem("ln_eps")
        ln_root = sem("ln_root")
        ln_scale = sem("ln_scale")
        ln_applied = sem("ln_applied")
        ln_back = sem("ln_back")
        ln_moved = sem("ln_moved")
        scored = sem("scored")
        split = sem("split")
        norm_st = {(k, b): sem(f"norm_st_{k}{b}") for k in "ac" for b in range(NB)}
        h_full = sem("h_full")
        gelu_done = sem("gelu_done")
        hid_used = sem("hid_used")
        y_used = sem("y_used")
        gate_ld = [sem(f"gate_ld{i}") for i in range(2)]
        res_ld = sem("res_ld")
        summed = sem("summed")
        ffn_st = [sem(f"ffn_st{u}") for u in range(2 * NB)]
        g_step = sem("g_step")
        g_exp = sem("g_exp")
        g_scores_read = sem("g_scores_read")
        g_turned = sem("g_turned")
        g_moved = sem("g_moved")
        gates_st = [sem(f"gates_st{u}") for u in range(2 * NB)]
        xq_ld = sem("xq_ld")
        a_step = sem("a_step")
        at_full = sem("at_full")
        at_free = sem("at_free")
        o_step = sem("o_step")
        o_var = sem("o_var")
        o_eps = sem("o_eps")
        o_scale = sem("o_scale")
        o_gelu = sem("o_gelu")
        o_tanh = sem("o_tanh")
        o_index = sem("o_index")
        values_st = sem("values_st")
        gathered = [sem(f"gathered{k}") for k in range(4)]
        val_done = sem("val_done")
        xres_ld = sem("xres_ld")
        y_step = sem("y_step")
        attn_st = [sem(f"attn_st{b}") for b in range(NB)]
        acc_ld = [sem(f"acc_ld{b}") for b in range(NB)]
        c_step = sem("c_step")
        c_bias = sem("c_bias")
        conv_st = [sem(f"conv_st{b}") for b in range(NB)]

        A_TAPS, Q_TAPS = G * 27, G * 9
        A_ALL = A_TAPS + Q_TAPS
        C_ALL = 49 * G
        AT_USES = 2 + VBLK + 2 + 1 + G + 2 * Q
        AT_OFF, AT_VAL, AT_KEY, AT_KV, AT_M2, AT_Y = 0, 2, 2 + VBLK, 4 + VBLK, 5 + VBLK, 5 + VBLK + G
        O_STEPS = 18
        G_STEPS = 14
        GATES_TURN = 3
        const_count, taps_count = [0], [0]

        def ffn_at(slot, m):
            return slot["ffn"] * TILES + m

        def lnf_at(slot, m):
            return slot["lnf"] * TILES + m

        def stored(u, tiles):
            return (32 if u == NB else 16) * tiles

        def ln_jobs(slot, m):
            jobs = []
            n = slot["ln_base"] + slot["ln_step"] * m
            if slot["lnc"] is not None:
                jobs.append(("c", n))
                n = n + 1
            if slot["lnf"] is not None:
                jobs.append(("f", n))
            return jobs

        STAGES = {"c": dict(turn_in=3, apply=6, turn_back=7, move=8), "f": dict(turn_in=8, apply=11)}
        STAGES_BEFORE = dict(turn_back=1, move=2, scores=4)
        LAST_STAGES = {"c": dict(turn_in=3, apply=5, turn_back=6, move=7),
                       "f": dict(turn_in=6, apply=9, turn_back=10, move=11, scores=CHUNKS)}

        def is_last(m):
            return isinstance(m, int) and m == TILES - 1

        def norm_hooks(slot, m, stages, beside):
            hooks = {}

            def put(kind, n, tile, table):
                for stage, c in table.items():
                    if stage in stages:
                        hooks.setdefault(c, []).append(
                            lambda stage=stage: stages[stage](slot, tile, kind, n))

            jobs = ln_jobs(slot, m)
            if slot["lnf"] is not None and not (isinstance(m, int) and m == 0):
                put("f", jobs[-1][1] - slot["ln_step"], m - 1, STAGES_BEFORE)
            for kind, n in jobs:
                put(kind, n, m, (LAST_STAGES if is_last(m) else STAGES)[kind])
            for c, more in beside.items():
                hooks[c] = hooks.get(c, []) + more
            return hooks

        def steps(eng, slot, body, beside, behind={}):
            first = None if slot["attn"] is None else "first"
            body(0, first, beside.get(0, {}))
            if slot["attn"] is None:
                with eng.Fori(1, TILES - 1) as m:
                    body(m, None, {})
                body(TILES - 1, None, {})
                return
            with eng.Fori(1, 3) as m:
                body(m, first, {})
            for m in range(3, TILES):
                body(m, "second" if m < 6 else None, beside.get(m, {}))
                if m in behind:
                    behind[m]()

        def norm_before(slot):
            kind, b = slot["lnc"]
            if b > 0:
                return kind, b - 1
            return ("a", NB - 1) if kind == "c" else None

        block = ctx.enter_context(nc.Block())

        @block.sync
        def _(sp):
            sp.dma_start(ident[:, :], a["c_ident"]).then_inc(ident_ld, 16)
            sp.wait_ge(pool_set, 2)
            for k in "ac":
                n = pad[k] * SIDE
                for at in (0, n + PIX):
                    sp.dma_start(norm[k][:, :, at:at + n].rearrange("b c n -> c b n"),
                                 zeros[0:C, 0:n].unsqueeze(1).broadcast_to([C, NB, n])).then_inc(pads_done, 16)

            def const(dst, src):
                sp.dma_start(dst, src).then_inc(const_ld, 16)
                const_count[0] += 1

            def load_constants():
                with nc.allow_non_contiguous_dma("small"):
                    const(w_out[:, :], a["L0_conv_w_out"])
                    const(q_mask[:, :], a["c_q_mask"])
                    const(before[:, :], a["c_before"].partition_broadcast(SUB))
                    for l in range(2):
                        f = f"L{l}_ffn_"
                        const(raw_w1[l].rearrange("p (e h) -> p e h", e=E), a[f + "w1"].rearrange("e d h -> d e h"))
                        const(w2[l][:, :, :], a[f + "w2"].rearrange("e (j p) d -> p (e j) d", p=128))
                        const(b1[l][:, :], a[f + "b1"].rearrange("e (j p) -> p (e j)", p=128))
                        const(b2[l][:, :], a[f + "b2"].rearrange("e d -> d e"))
                        const(gate_w[l][:, :], a[f + "gate_w"])
                        const(gate_b[l][:, :], a[f + "gate_b"].partition_broadcast(SUB))

            def load_norm(slot, kind, n, at):
                if not (isinstance(n, int) and n == 0):
                    sp.wait_ge(ln_turned, n)
                if kind == "c":
                    k, b = slot["lnc"]
                    src = ln_src[k][b]
                else:
                    u = slot["lnf"]
                    src = ffn_src[u][u % NB]
                sp.dma_start(ln_x[kind][:, :], src[:, at]).then_inc(ln_loaded[kind], 16)

            def load_gates(slot, k, i, at):
                rows = gates_dram[slot["ffn"]].rearrange("(e t) -> e t", e=E)
                sp.wait_ge(y_used, Y_BANKS * i + E * k)
                sp.dma_start(gate_t[i][:, :, :], rows[2 * i:2 * i + 2, at].partition_broadcast(C))\
                    .then_inc(gate_ld[i], 16)

            def load_res(slot, k, at):
                u = slot["ffn"]
                sp.wait_ge(summed, 3 * k)
                sp.dma_start(res[:, :], ffn_src[u][u % NB][:, at]).then_inc(res_ld, 16)

            def body(m, part_of, beside):
                slot = body.slot
                more = not (isinstance(m, int) and m == TILES - 1)
                then = bass.ds(m * TILE + TILE, TILE)
                for kind, n in ln_jobs(slot, m):
                    if more:
                        load_norm(slot, kind, n + 1, then)
                    if kind == "c":
                        k, b = slot["lnc"]
                        sp.wait_ge(ln_moved, n + 1)
                        sp.dma_start(norm[k][b][:, bass.ds(m * TILE + pad[k] * SIDE, TILE)], ln_cm["c"][:, :])\
                            .then_inc(norm_st[k, b], 16)
                if slot["ffn"] is not None:
                    u, k = slot["ffn"], ffn_at(slot, m)
                    if more:
                        for i in range(2):
                            load_gates(slot, k + 1, i, then)
                        load_res(slot, k + 1, then)
                    sp.wait_ge(summed, 3 * k + 3)
                    for c0, c1 in ((C // 2, C), (0, C // 2)) if u == NB else ((0, C),):
                        sp.dma_start(ffn_dst[u][u % NB][c0:c1, bass.ds(m * TILE, TILE)], ffn_out[c0:c1, :])\
                            .then_inc(ffn_st[u], 16)

            def load_quarters(k, b, rows):
                src = norm[k][b].rearrange("(g c) n -> c g n", g=G)
                for q in range(Q):
                    sp.dma_start(xq[q::Q, :, 0:rows * SIDE], src[:, :, q * QPIX:q * QPIX + rows * SIDE])\
                        .then_inc(xq_ld, 16)

            def load_acc(b):
                for q in range(Q):
                    sp.dma_start(acc[b % 2][q::Q], x_ffn0[b].rearrange("(g c) (q n) -> q c g n", g=G, q=Q)[q])\
                        .then_inc(acc_ld[b], 16)

            for slot in SLOTS:
                body.slot = slot
                start = slice(0, TILE)
                if slot["lnc"] is not None:
                    k, b = slot["lnc"]
                    if k == "c":
                        sp.wait_ge(ffn_st[b], stored(b, TILES))
                    load_norm(slot, "c", slot["ln_base"], start)
                if slot["attn"] is not None:
                    b = slot["attn"]
                    if b == 0:
                        sp.wait_ge(pads_done, 16 * 4)
                    sp.wait_ge(norm_st["a", b], 16 * TILES)
                    sp.wait_ge(a_step, A_ALL * b)
                    load_quarters("a", b, ROWS_A)
                if slot["conv"] is not None:
                    b = slot["conv"]
                    sp.wait_ge(norm_st["c", b], 16 * TILES)
                    sp.wait_ge(a_step, A_ALL * NB)
                    if b > 0:
                        sp.wait_ge(c_step, G + C_ALL * b)
                    load_quarters("c", b, ROWS_C)
                    if b == 0:
                        sp.wait_ge(at_free, AT_USES * NB)
                        load_acc(0)
                if slot["before"] is not None and slot["before"]["conv"] is not None:
                    b = slot["before"]["conv"]
                    sp.wait_ge(c_step, G + C_ALL * (b + 1))
                    for q in range(Q):
                        sp.dma_start(x_conv[b].rearrange("(g c) (q n) -> q c g n", g=G, q=Q)[q],
                                     acc[b % 2][q::Q]).then_inc(conv_st[b], 16)
                if slot["ffn"] is not None:
                    u, k = slot["ffn"], ffn_at(slot, 0)
                    load_res(slot, k, start)
                    sp.wait_ge(gates_st[u], 16)
                    for i in range(2):
                        load_gates(slot, k, i, start)
                if slot["lnf"] is not None:
                    u = slot["lnf"]
                    sp.wait_ge(attn_st[u] if u < NB else conv_st[u - NB], 16 if u < NB else 16 * Q)
                    load_norm(slot, "f", slot["ln_base"], start)
                if slot["attn"] is not None:
                    b = slot["attn"]
                    if b > 0:
                        sp.wait_ge(attn_st[b - 1], 16)
                    sp.dma_start(x_res[:, :], x_in[b]).then_inc(xres_ld, 16)
                if slot["conv"] is not None and slot["conv"] + 1 < NB:
                    if slot["conv"] > 0:
                        sp.wait_ge(conv_st[slot["conv"] - 1], 16 * Q)
                    load_acc(slot["conv"] + 1)

                def store_values():
                    b = slot["attn"]
                    sp.wait_ge(at_free, AT_USES * b + AT_VAL + VBLK)
                    sp.dma_start(value_rows[b].rearrange("(s p) c -> p s c", p=SUB),
                                 pixels[:, 0:Q * VBLK * C].rearrange("p (s c) -> p s c", c=C))\
                        .then_inc(values_st, 16)

                def store_x():
                    b = slot["attn"]
                    sp.wait_ge(y_step, 2 * Q * (b + 1))
                    sp.dma_start(x_attn[b], x_res[:, :]).then_inc(attn_st[b], 16)

                if slot["attn"] == 0:
                    load_constants()
                steps(sp, slot, body, {}, {3: store_values, 6: store_x})
            for u in range(2 * NB):
                sp.wait_ge(ffn_st[u], stored(u, TILES))

        @block.scalar
        def _(act):
            act.sem_inc(gelu_done, H_BANKS)

            def load(dst, src):
                act.dma_start(dst, src).then_inc(taps_ld, 16)
                taps_count[0] += 1

            with nc.allow_non_contiguous_dma("small"):
                load(to_quarters[:, :], a["c_to_quarters"])
                r_w_a, r_b_a, r_w_c, r_w53, r_w35, r_w7, r_w5, r_b_c = views(rows_w)
                for n, w in enumerate(("v", "k", "off1", "q")):
                    load(r_w_a[:, n], a[f"L0_conv_w_{w}"].rearrange("(g c) o h w -> c g (o h w)", g=G))
                    load(r_b_a[:, n], a[f"L0_conv_b_{w}"].rearrange("(g c) -> c g", g=G))
                for dst, w in ((r_w_c, "w77"), (r_w53, "w53"), (r_w35, "w35"), (r_w7[:, 0], "w7h"),
                               (r_w7[:, 1], "w7w"), (r_w5[:, 0], "w5h"), (r_w5[:, 1], "w5w")):
                    load(dst, a[f"L1_conv_{w}"].rearrange("(g c) o h w -> c g (o h w)", g=G))
                for n, w in enumerate(("b77", "b53", "b35")):
                    load(r_b_c[:, n], a[f"L1_conv_{w}"].rearrange("(g c) -> c g", g=G))
                load(ref_pos[:, :], a["c_ref_pos"])
                load(ln_gb[:, 0], a["L0_conv_ln_g"].partition_broadcast(HPTS))
                load(ln_gb[:, 1], a["L0_conv_ln_b"].partition_broadcast(HPTS))
                load(w_off2[:, :], a["L0_conv_w_off2"].partition_broadcast(HPTS))

            def add_bias(b):
                act.wait_ge(acc_ld[b], 16 * Q)
                act.wait_ge(wc_done, 1)
                for g in range(G):
                    act.activation(acc[b % 2][:, g, :], acc[b % 2][:, g, :], ACT.Identity, bias=b_c[:, 0, g:g + 1])\
                        .then_inc(c_bias, 1)

            def apply(slot, m, kind, n):
                act.wait_ge(ln_scale, n + 1)
                if not (isinstance(n, int) and n == 0):
                    act.wait_ge(ln_back, n)
                for s in range(NSUB):
                    ins = act.activation(ln_tok[:, s, :], lt_ps[0:SUB, s * C:(s + 1) * C], ACT.Identity,
                                         bias=ln_bias[:, s:s + 1], scale=ln_rstd[:, s:s + 1])
                ins.then_inc(ln_applied, 1)

            def move(slot, m, kind, n):
                act.wait_ge(ln_back, n + 1)
                if kind == "f":
                    act.wait_ge(scored, lnf_at(slot, m))
                    act.wait_ge(split, lnf_at(slot, m))
                else:
                    act.wait_ge(norm_st[slot["lnc"]], 16 * m)
                if kind == "f":
                    if slot["ffn"] is not None:
                        act.wait_ge(h_full, CHUNKS * ffn_at(slot, m) + CHUNKS)
                    act.copy(xh[:, bass.ds(m * TILE, TILE)], lb_ps[0:C, 0:TILE])
                act.copy(ln_cm[kind][:, :], lb_ps[0:C, 0:TILE]).then_inc(ln_moved, 1)

            def body(m, part_of, beside):
                slot = body.slot
                hooks = norm_hooks(slot, m, dict(apply=apply, move=move), beside)
                if slot["ffn"] is None:
                    for c in sorted(hooks):
                        for hook in hooks[c]:
                            hook()
                    return
                k, l = ffn_at(slot, m), slot["ffn"] // NB
                for c in range(CHUNKS):
                    act.wait_ge(h_full, CHUNKS * k + c + 1)
                    act.wait_ge(hid_used, CHUNKS * k + c + 1)
                    act.activation(hidden[c % HID_RING][:, :], h_ps[c % H_BANKS][:, 0:TILE], ACT.Gelu,
                                   bias=b1[l][:, c:c + 1]).then_inc(gelu_done, 1)
                    for hook in hooks.get(c, []):
                        hook()

            for slot in SLOTS:
                body.slot = slot
                b = slot["attn"]
                base = AT_USES * (b or 0)
                if slot["lnc"] is not None and norm_before(slot) is not None:
                    act.wait_ge(norm_st[norm_before(slot)], 16 * TILES)

                if slot["conv"] == 0:
                    add_bias(0)

                def full(i):
                    act.wait_ge(at_full, base + i + 1)

                def take_off(h):
                    full(AT_OFF + h)
                    act.copy(off_t[:, h, :], at_ps[0:HPTS, 0:G * 128]).then_inc(at_free, 1)

                def take_value(j):
                    full(AT_VAL + j)
                    act.copy(v_tok[:, :, j, :].rearrange("p q c -> p c q"),
                             at_ps[0:SUB, 0:G * 128].rearrange("p (c q) -> p c q", q=Q)).then_inc(at_free, 1)

                def take_key(h):
                    full(AT_KEY + h)
                    act.copy(key_t[:, h, :], at_ps[0:HPTS, 0:G * 128]).then_inc(at_free, 1)

                def gelu():
                    act.wait_ge(o_step, O_STEPS * b + 4)
                    act.activation(o_n[:, :, :], o_n[:, :, :], ACT.Gelu).then_inc(o_gelu, 1)

                def tanh():
                    act.wait_ge(o_step, O_STEPS * b + 9)
                    act.activation(o_pos[:, :, :], o_pos[:, :, :], ACT.Tanh).then_inc(o_tanh, 1)

                def take_kv():
                    full(AT_KV)
                    for h in range(4):
                        r = slice(32 * h, 32 * h + 32)
                        ins = act.activation(kv[r, :, r],
                                             at_ps[r, 0:G * 128].rearrange("p (g n) -> p g n", g=G)[:, :, r],
                                             ACT.Copy, scale=SCALE)
                    ins.then_inc(at_free, 1)

                def take_m2(g):
                    full(AT_M2 + g)
                    act.copy(m2[:, g, :], at_ps[:, 0:Q * C]).then_inc(at_free, 1)

                takes = [lambda h=h: take_off(h) for h in range(2)]
                takes += [lambda j=j: take_value(j) for j in range(VBLK)]
                takes += [lambda h=h: take_key(h) for h in range(2)]
                def exp_scores():
                    u = slot["ffn"]
                    act.wait_ge(g_step, G_STEPS * u + 2)
                    act.activation(g_p[:, :, :], g_s[:, :, :], ACT.Exp).then_inc(g_exp, 1)

                def take_gates():
                    u = slot["ffn"]
                    act.wait_ge(g_turned, u + 1)
                    if u > 0:
                        act.wait_ge(gates_st[u - 1], 16)
                    act.copy(g_tr[:, :], lg_ps[0:SE, 128:128 + SUB]).then_inc(g_moved, 1)
                    act.wait_ge(g_moved, u + 1)
                    act.dma_start(gates_dram[u].rearrange("(s t) -> s t", t=SUB), g_tr[:, :]).then_inc(gates_st[u], 16)

                steps(act, slot, body, {
                    0: {} if slot["ffn"] is None else {0: [exp_scores], GATES_TURN: [take_gates]},
                    3: {**{i: [take] for i, take in enumerate(takes)}, CHUNKS - 1: [gelu]},
                    4: {3: [tanh]},
                    6: {4: [take_kv], **{5 + g: [lambda g=g: take_m2(g)] for g in range(G)}}})
                if slot is SLOTS[0]:
                    act.wait_ge(taps_spread, 1)
                    act.copy(all_w[:, :], at_ps[:, 0:CONV_W]).then_inc(taps_set, 1)
                if slot["conv"] is not None and slot["conv"] + 1 < NB:
                    add_bias(slot["conv"] + 1)

        N_CONST, N_TAPS = const_count[0], taps_count[0]

        @block.gpsimd
        def _(pool):
            pool.memset(zeros[:, :], 0.0).then_inc(pool_set, 1)
            pool.memset(kv[:, :, :], 0.0).then_inc(pool_set, 1)
            pool.memset(minus_half[:, :], -0.5).then_inc(pool_set, 1)
            pool.memset(eps["c"][:, :], LN_C_EPS).then_inc(pool_set, 1)
            pool.memset(eps["f"][:, :], LN_T_EPS).then_inc(pool_set, 1)
            pool.memset(minus_one[:, :], -1.0).then_inc(pool_set, 1)
            pool.wait_ge(pool_set, 6)

            def body(m, part_of, beside):
                slot = body.slot
                for i, (kind, n) in enumerate(ln_jobs(slot, m)):
                    pool.wait_ge(ln_var, n + 1)
                    pool.wait_ge(ln_applied, n)
                    pool.tensor_tensor(ln_ve[:, :], ln_mv[:, :, 1], eps[kind][0:SUB, 0:NSUB], ALU.add)
                    pool.tensor_tensor(ln_neg[:, :], ln_mv[:, :, 0], minus_one[:, :], ALU.mult).then_inc(ln_eps, 1)
                    pool.wait_ge(ln_eps, n + 1)
                    pool.tensor_tensor(ln_rstd[:, :], ln_ve[:, :], minus_half[0:SUB, 0:NSUB], ALU.pow)\
                        .then_inc(ln_root, 1)
                    pool.wait_ge(ln_root, n + 1)
                    pool.tensor_tensor(ln_bias[:, :], ln_neg[:, :], ln_rstd[:, :], ALU.mult).then_inc(ln_scale, 1)
                    for more in beside.get(i, []):
                        more()
                for more in beside.get("end", []):
                    more()

            for slot in SLOTS:
                body.slot = slot

                def scale_off():
                    b = slot["attn"]
                    pool.wait_ge(o_var, b + 1)
                    pool.tensor_scalar(o_ve[:, :], o_mv[:, :, 1], LN_T_EPS, None, ALU.add).then_inc(o_eps, 1)
                    pool.wait_ge(o_eps, b + 1)
                    pool.tensor_tensor(o_rstd[:, :], o_ve[:, :], minus_half[0:HPTS, :], ALU.pow).then_inc(o_scale, 1)

                def gather(k):
                    b = slot["attn"]
                    pool.wait_ge(o_index, b + 1)
                    pool.wait_ge(values_st, 16 * (b + 1))
                    for g in range(GQ):
                        pool.indirect_dma_start(
                            corners[:, k, g, :], None, value_rows[b],
                            bass.IndirectOffsetOnAxis(ap=o_idx[:, k, g:g + 1], axis=0)).then_inc(gathered[k], 16)

                steps(pool, slot, body, {
                    3: {0: [scale_off]},
                    4: {0: [lambda: gather(0)], "end": [lambda: gather(1)]},
                    5: {0: [lambda: gather(2)], "end": [lambda: gather(3)]}})

        @block.tensor
        def _(pe):
            pe.sem_inc(hid_used, HID_RING)
            pe.wait_ge(ident_ld, 16)

            def spread_w_out():
                pe.wait_ge(w_out_spread, 1)
                pe.wait_ge(at_free, AT_KV)
                for g in range(G):
                    if g > 0:
                        pe.wait_ge(wexp_done, g)
                    pe.matmul(at_ps[:, 0:C], w_out_q[:, g * 128:(g + 1) * 128], ident[0:C, 0:C],
                              start=True, stop=True).then_inc(wexp_ps, 1)
                pe.wait_ge(wexp_done, G)

            def turn_in(slot, m, kind, n):
                pe.wait_ge(ln_loaded[kind], 16 * ((lnf_at(slot, m) if kind == "f" else slot["lnc_base"] + m) + 1))
                pe.wait_ge(ln_applied, n)
                for s in range(NSUB):
                    last = pe.transpose(lt_ps[0:SUB, s * C:(s + 1) * C], ln_x[kind][:, s * SUB:(s + 1) * SUB],
                                        ident[0:C, 0:C])
                last.then_inc(ln_turned, 1)

            def turn_back(slot, m, kind, n):
                pe.wait_ge(ln_applied, n + 1)
                pe.wait_ge(ln_moved, n)
                for s in range(NSUB):
                    last = pe.transpose(lb_ps[0:C, s * SUB:(s + 1) * SUB], ln_tok[:, s, :], ident[0:SUB, 0:SUB])
                last.then_inc(ln_back, 1)

            def scores(slot, m, kind, n):
                u = slot["lnf"]
                if isinstance(m, int) and m == 0 and u > 0:
                    pe.wait_ge(g_scores_read, u)
                pe.wait_ge(ln_moved, n + 1)
                for s in range(NSUB):
                    last = pe.matmul(score_ps[:, :, bass.ds(m * NSUB + s, 1)].rearrange("p e s -> p (e s)"),
                                     ln_cm["f"][:, s * SUB:(s + 1) * SUB], gate_w[u // NB][:, :],
                                     start=True, stop=True)
                last.then_inc(scored, 1)

            def second(slot, m, c):
                k, l = ffn_at(slot, m), slot["ffn"] // NB
                e, j = c // CPE, c % CPE
                pe.wait_ge(gelu_done, H_BANKS + CHUNKS * k + c + 1)
                if j == 0:
                    pe.wait_ge(y_used, E * k + e + 1)
                pe.matmul(y_ps[e % Y_BANKS][0:C, 0:TILE], w2[l][:, c, :], hidden[c % HID_RING][:, :],
                          start=(j == 0), stop=(j == CPE - 1)).then_inc(hid_used, 1)

            def body(m, part_of, beside):
                slot = body.slot
                hooks = norm_hooks(slot, m, dict(turn_in=turn_in, turn_back=turn_back, scores=scores), beside)
                if slot["ffn"] is None:
                    for c in sorted(hooks):
                        for hook in hooks[c]:
                            hook()
                    return
                k, l = ffn_at(slot, m), slot["ffn"] // NB
                pe.wait_ge(split, k + 1)
                for c in range(CHUNKS):
                    pe.wait_ge(gelu_done, CHUNKS * k + c + 1)
                    ps = h_ps[c % H_BANKS][:, 0:TILE]
                    cols = bass.ds(m * TILE, TILE)
                    hi, lo = w1h[l][:, c * 128:(c + 1) * 128], w1l[l][:, c * 128:(c + 1) * 128]
                    pe.matmul(ps, hi, xh[:, cols], start=True, stop=False)
                    pe.matmul(ps, hi, xl[:, cols], start=False, stop=False)
                    pe.matmul(ps, lo, xh[:, cols], start=False, stop=True).then_inc(h_full, 1)
                    for hook in hooks.get(c, []):
                        hook()
                    if c > 0:
                        second(slot, m, c - 1)
                second(slot, m, CHUNKS - 1)
                for hook in hooks.get(CHUNKS, []):
                    hook()

            for slot in SLOTS:
                body.slot = slot
                b = slot["attn"]
                base = AT_USES * (b or 0)

                def use(i):
                    if base + i > 0:
                        pe.wait_ge(at_free, base + i)

                def turn(i, src, width):
                    use(i)
                    for g in range(G):
                        last = pe.transpose(at_ps[0:width, g * 128:(g + 1) * 128], src(g), ident[:, :])
                    last.then_inc(at_full, 1)

                def turn_off(h):
                    if h == 0:
                        pe.wait_ge(a_step, A_ALL * b + A_TAPS)
                    turn(AT_OFF + h, lambda g: off[:, g, h * HPTS:(h + 1) * HPTS], HPTS)

                def turn_value(j):
                    turn(AT_VAL + j, lambda g: value[:, g, j * SUB:(j + 1) * SUB], SUB)

                def turn_key(h):
                    turn(AT_KEY + h, lambda g: key[:, g, h * HPTS:(h + 1) * HPTS], HPTS)

                def keys_values():
                    pe.wait_ge(val_done, b + 1)
                    use(AT_KV)
                    for g in range(G):
                        for h in range(2):
                            last = pe.matmul(at_ps[:, g * 128:(g + 1) * 128], val_t[:, h, g * 128:(g + 1) * 128],
                                             key_t[:, h, g * 128:(g + 1) * 128], start=(h == 0), stop=(h == 1))
                    last.then_inc(at_full, 1)

                def times_w_out(g):
                    use(AT_M2 + g)
                    pe.matmul(at_ps[:, 0:Q * C], kv[:, g, :], w_exp[:, g, :], start=True, stop=True)\
                        .then_inc(at_full, 1)

                def times_query(i):
                    if i == 0:
                        pe.wait_ge(a_step, A_ALL * (b + 1))
                    q, h = i // 2, i % 2
                    use(AT_Y + i)
                    for g in range(G):
                        last = pe.matmul(at_ps[0:C, 0:YCOL], m2[:, g, q * C:(q + 1) * C],
                                         query[:, g, h * YCOL:(h + 1) * YCOL], start=(g == 0), stop=(g == G - 1))
                    last.then_inc(at_full, 1)

                def rest_of_queries():
                    for i in range(4, 2 * Q):
                        times_query(i)

                turns = [lambda h=h: turn_off(h) for h in range(2)]
                turns += [lambda j=j: turn_value(j) for j in range(VBLK)]
                turns += [lambda h=h: turn_key(h) for h in range(2)]
                def turn_gates():
                    u = slot["ffn"]
                    pe.wait_ge(g_step, G_STEPS * (u + 1))
                    pe.transpose(lg_ps[0:SE, 128:128 + SUB], g_s[:, :, :].rearrange("p e s -> p (e s)"),
                                 ident[0:SUB, 0:SUB]).then_inc(g_turned, 1)

                steps(pe, slot, body, {
                    0: {} if slot["ffn"] is None else {GATES_TURN: [turn_gates]},
                    3: {i: [t] for i, t in enumerate(turns)},
                    6: {4: [keys_values], **{5 + g: [lambda g=g: times_w_out(g)] for g in range(G)},
                        **{8 + i: [lambda i=i: times_query(i)] for i in range(4)}}}, {4: spread_w_out, 6: rest_of_queries} if b == 0 else {6: rest_of_queries})
                if slot is SLOTS[0]:
                    pe.wait_ge(taps_ld, 16 * N_TAPS)
                    pe.matmul(at_ps[:, 0:CONV_W], to_quarters[:, :], rows_w[:, :], start=True, stop=True)\
                        .then_inc(taps_spread, 1)

        @block.vector
        def _(dve):
            dve.sem_inc(y_used, Y_BANKS)
            def prepare_weights():
                dve.wait_ge(const_ld, 16 * N_CONST)
                for l in range(2):
                    raw = raw_w1[l]
                    dve.tensor_copy(w1h[l][:, :], raw).then_inc(w1_split, 1)
                    dve.wait_ge(w1_split, 2 * l + 1)
                    dve.tensor_tensor(w1l[l][:, :], raw, w1h[l][:, :].bitcast(F32), ALU.subtract).then_inc(w1_split, 1)
                dve.tensor_copy(w_out_q[:, :].rearrange("p (c q) -> p c q", q=Q), w_out[:, :].unsqueeze(2).broadcast_to([C, C, Q]))\
                    .then_inc(w_out_spread, 1)
                for g in range(G):
                    dve.wait_ge(wexp_ps, g + 1)
                    for q in range(Q):
                        ins = dve.tensor_scalar(w_exp[:, g, q * C:(q + 1) * C], at_ps[:, 0:C], q_mask[:, q:q + 1], None,
                                                ALU.mult)
                    ins.then_inc(wexp_done, 1)
                n_wc = [0]

                def wc_chain(ins):
                    ins.then_inc(wc_chain_sem, 1)
                    n_wc[0] += 1
                    dve.wait_ge(wc_chain_sem, n_wc[0])

                wcv = w_c[:, :, :].rearrange("p g (h w) -> p g h w", w=7)
                v53 = w53[:, :, :].rearrange("p g (h w) -> p g h w", w=3)
                v35 = w35[:, :, :].rearrange("p g (h w) -> p g h w", w=5)
                wc_chain(dve.tensor_tensor(wcv[:, :, 1:6, 2:5], wcv[:, :, 1:6, 2:5], v53, ALU.add))
                wc_chain(dve.tensor_tensor(wcv[:, :, 2:5, 1:6], wcv[:, :, 2:5, 1:6], v35, ALU.add))
                for w, n in ((w7, 7), (w5, 5)):
                    o = (7 - n) // 2
                    for g in range(G):
                        for i in range(n):
                            row = wcv[:, g, o + i, o:o + n]
                            ins = dve.scalar_tensor_tensor(row, w[:, 1, g, :], w[:, 0, g, i:i + 1], row, ALU.mult, ALU.add)
                    wc_chain(ins)
                wc_chain(dve.tensor_tensor(b_c[:, 0], b_c[:, 0], b_c[:, 1], ALU.add))
                dve.tensor_tensor(b_c[:, 0], b_c[:, 0], b_c[:, 2], ALU.add).then_inc(wc_done, 1)
                dve.wait_ge(wc_done, 1)

            def normalize(n):
                dve.wait_ge(ln_turned, n + 1)
                for s in range(NSUB):
                    ins = dve.bn_stats(ln_stats[:, s, :], lt_ps[0:SUB, s * C:(s + 1) * C])
                ins.then_inc(ln_stat, 1)
                dve.wait_ge(pool_set, 6)
                dve.wait_ge(ln_stat, n + 1)
                for s in range(NSUB):
                    ins = dve.bn_aggr(ln_mv[:, s, :], ln_stats[:, s, :])
                ins.then_inc(ln_var, 1)

            def split_tile(slot, m, n):
                dve.wait_ge(ln_moved, n + 1)
                cols = bass.ds(m * TILE, TILE)
                dve.tensor_tensor(xl[:, cols], ln_cm["f"][:, :], xh[:, cols].bitcast(F32), ALU.subtract)\
                    .then_inc(split, 1)

            def combine(slot, m, e):
                k, l = ffn_at(slot, m), slot["ffn"] // NB
                dve.wait_ge(hid_used, HID_RING + CHUNKS * k + CPE * (e + 1))
                dve.wait_ge(gate_ld[e // 2], 16 * (k + 1))
                if e == 0:
                    dve.wait_ge(summed, 3 * k)
                dve.scalar_tensor_tensor(part[:, e, :], y_ps[e % Y_BANKS][0:C, 0:TILE], b2[l][:, e:e + 1],
                                         gate_t[e // 2][:, e % 2, :], ALU.add, ALU.mult).then_inc(y_used, 1)

            def sum_pairs(slot, m):
                k = ffn_at(slot, m)
                dve.wait_ge(y_used, Y_BANKS + E * (k + 1))
                dve.tensor_tensor(pair[:, :, :], part[:, 0:2, :], part[:, 2:4, :], ALU.add).then_inc(summed, 1)

            def sum_experts(slot, m):
                k = ffn_at(slot, m)
                dve.wait_ge(summed, 3 * k + 1)
                dve.tensor_tensor(part[:, 0, :], pair[:, 0, :], pair[:, 1, :], ALU.add).then_inc(summed, 1)

            def sum_residual(slot, m):
                k, u = ffn_at(slot, m), slot["ffn"]
                dve.wait_ge(summed, 3 * k + 2)
                dve.wait_ge(res_ld, 16 * (k + 1))
                if not (isinstance(m, int) and m == 0):
                    dve.wait_ge(ffn_st[u], stored(u, m))
                dve.tensor_tensor(ffn_out[:, :], part[:, 0, :], res[:, :], ALU.add).then_inc(summed, 1)

            def taps3(out_ap, in_ap, n, g, base, at, step, stride):
                side = SIDE // stride
                rows_in = in_ap.rearrange("p (r x) -> p r x", x=SIDE)
                rows_out = out_ap.rearrange("p (r x) -> p r x", x=side)
                order = [(0, 1)] + [(dy, dx) for dy in range(3) for dx in range(3) if (dy, dx) != (0, 1)]
                done = []
                for i, (dy, dx) in enumerate(order):
                    x0 = 1 if dx == 0 else 0
                    x1 = side - 1 if dx == 2 and stride == 1 else side
                    c0 = stride * x0 + dx - 1
                    nr = QROWS // stride
                    src = rows_in[:, dy:dy + stride * (nr - 1) + 1:stride, c0:c0 + stride * (x1 - x0 - 1) + 1:stride]
                    dst = rows_out[:, :, x0:x1]
                    w = w_a[:, n, g, dy * 3 + dx:dy * 3 + dx + 1]

                    def op(i=i, src=src, dst=dst, w=w):
                        if i == 0:
                            ins = dve.tensor_scalar(dst, src, w, b_a[:, n, g], ALU.mult, ALU.add)
                        else:
                            dve.wait_ge(a_step, base + at + step * (i - 1) + 1)
                            ins = dve.scalar_tensor_tensor(dst, src, w, dst, ALU.mult, ALU.add)
                        ins.then_inc(a_step, 1)
                    done.append(op)
                return done

            def attn_taps(slot, m, part_of):
                base = A_ALL * slot["attn"]
                g = bass.ds(m if part_of == "first" else m - 3, 1)
                src = xq[:, g, 0:ROWS_A * SIDE].rearrange("p g n -> p (g n)")

                def one(t):
                    return t[:, g, :].rearrange("p g n -> p (g n)")
                if part_of == "first":
                    base = base + 27 * m
                    lists = [taps3(one(value), src, 0, g, base, 0, 3, 1), taps3(one(key), src, 1, g, base, 1, 3, 2),
                             taps3(one(off), src, 2, g, base, 2, 3, 2)]
                    return [op for three in zip(*lists) for op in three]
                base = base + A_TAPS + 9 * (m - 3)
                return taps3(one(query), src, 3, g, base, 0, 1, 1)

            def conv_taps(slot, m):
                b = slot["conv"]
                ops = []
                for i, dx in enumerate((3, 0, 1, 2, 4, 5, 6)):
                    x0, x1 = max(0, 3 - dx), SIDE - max(0, dx - 3)
                    for g in range(G):
                        src = xq[:, g, bass.ds(m * SIDE, QPIX)].rearrange("p (r x) -> p r x", x=SIDE)[
                            :, :, x0 + dx - 3:x1 + dx - 3]
                        dst = acc[b % 2][:, g, :].rearrange("p (r x) -> p r x", x=SIDE)[:, :, x0:x1]
                        w = w_c[:, g, bass.ds(m * 7 + dx, 1)]

                        def op(n=G * i + g, src=src, dst=dst, w=w):
                            dve.wait_ge(c_step, C_ALL * b + 7 * G * m + n + 1)
                            dve.scalar_tensor_tensor(dst, src, w, dst, ALU.mult, ALU.add).then_inc(c_step, 1)
                        ops.append(op)
                return ops

            ORDER = ("combine0", "split", "normalize0", "combine1", "combine2", "normalize1", "combine3", "sum",
                     "sum_experts", "sum_residual",                     "end")
            LAST_ORDER = ("combine0", "split", "normalize0", "combine1", "normalize1", "combine2", "combine3",
                          "sum", "sum_experts", "sum_residual", "split_last", "end")
            TAPS_BEFORE = dict(combine0=4, split=1, normalize0=1, combine1=20, combine2=28, normalize1=1, combine3=10,
                               sum=10, sum_experts=4, sum_residual=4, split_last=1)

            def body(m, part_of, beside):
                slot = body.slot
                ops = []
                if part_of is not None:
                    ops = attn_taps(slot, m, part_of)
                if slot["conv"] is not None:
                    ops = conv_taps(slot, m)
                jobs = ln_jobs(slot, m)
                work = {}
                for i, (kind, n) in enumerate(jobs):
                    work[f"normalize{i}"] = lambda n=n: normalize(n)
                if slot["ffn"] is not None:
                    for e in range(E):
                        work[f"combine{e}"] = lambda e=e: combine(slot, m, e)
                    work["sum"] = lambda: sum_pairs(slot, m)
                    work["sum_experts"] = lambda: sum_experts(slot, m)
                    work["sum_residual"] = lambda: sum_residual(slot, m)
                if slot["lnf"] is not None:
                    if not (isinstance(m, int) and m == 0):
                        work["split"] = lambda: split_tile(slot, m - 1, jobs[-1][1] - slot["ln_step"])
                    if is_last(m):
                        work["split_last"] = lambda: split_tile(slot, m, jobs[-1][1])
                order = LAST_ORDER if is_last(m) else ORDER
                whole = sum(TAPS_BEFORE[name] for name in order if name in work)
                at = done = 0
                for name in order:
                    if name in work:
                        done += TAPS_BEFORE[name]
                        till = len(ops) * done // whole
                        for op in ops[at:till]:
                            op()
                        at = till
                    for more in beside.get(name, []):
                        more()
                    if name in work:
                        work[name]()

            def chain(b, n0):
                n = [n0]

                def link(ins, wait=True):
                    ins.then_inc(o_step, 1)
                    n[0] += 1
                    if wait:
                        dve.wait_ge(o_step, O_STEPS * b + n[0])
                return link

            for slot in SLOTS:
                body.slot = slot
                b = slot["attn"]

                def norm_off():
                    base = AT_USES * b
                    dve.wait_ge(at_free, base + AT_OFF + 2)
                    link = chain(b, 0)
                    v = off_t[:, :, :].rearrange("p h (c q) -> p h q c", q=Q)
                    for h in range(2):
                        for q in range(Q):
                            ins = dve.bn_stats(o_stats[:, h * Q + q, :], v[:, h, q, :])
                    link(ins)
                    for i in range(GQ):
                        ins = dve.bn_aggr(o_mv[:, i, :], o_stats[:, i, :])
                    ins.then_inc(o_var, 1)

                def apply_off():
                    link = chain(b, 1)
                    v = off_t[:, :, :].rearrange("p h (c q) -> p h q c", q=Q)
                    dve.wait_ge(o_scale, b + 1)
                    for h in range(2):
                        for q in range(Q):
                            i = h * Q + q
                            ins = dve.tensor_scalar(o_n[:, i, :], v[:, h, q, :], o_mv[:, i, 0:1], o_rstd[:, i:i + 1],
                                                    ALU.subtract, ALU.mult)
                    link(ins)
                    full = [HPTS, GQ, C]
                    link(dve.tensor_tensor(o_n[:, :, :], o_n[:, :, :], ln_gb[:, 0].unsqueeze(1).broadcast_to(full),
                                           ALU.mult))
                    link(dve.tensor_tensor(o_n[:, :, :], o_n[:, :, :], ln_gb[:, 1].unsqueeze(1).broadcast_to(full),
                                           ALU.add))

                def offsets():
                    link = chain(b, 4)
                    full = [HPTS, GQ, C]
                    dve.wait_ge(o_gelu, b + 1)
                    tmp = off_t[:, :, :].rearrange("p h n -> p (h n)").rearrange("p (g c) -> p g c", c=C)
                    for i in range(2):
                        link(dve.tensor_tensor(tmp, o_n[:, :, :], w_off2[:, i].unsqueeze(1).broadcast_to(full),
                                               ALU.mult))
                        link(dve.tensor_reduce(o_pos[:, i, :], tmp, AX_X, ALU.add))
                    link(dve.tensor_tensor(o_pos[:, :, :], o_pos[:, :, :],
                                           ref_pos[:, :].rearrange("p (i g) -> p i g", i=2), ALU.add))

                def positions():
                    link = chain(b, 9)
                    dve.wait_ge(o_tanh, b + 1)
                    link(dve.tensor_scalar(o_pos[:, :, :], o_pos[:, :, :], 1.0, 0.5 * (SIDE - 1), ALU.add, ALU.mult))
                    link(dve.tensor_copy(o_int[:, :, :], o_pos[:, :, :]))
                    link(dve.tensor_copy(o_fl[:, :, :], o_int[:, :, :]))
                    link(dve.tensor_tensor(o_gt[:, :, :], o_fl[:, :, :], o_pos[:, :, :], ALU.is_gt))
                    link(dve.tensor_tensor(o_fl[:, :, :], o_fl[:, :, :], o_gt[:, :, :], ALU.subtract))
                    link(dve.tensor_scalar(o_fl[:, :, :], o_fl[:, :, :], 0.0, float(SIDE - 2), ALU.max, ALU.min))
                    dve.tensor_tensor(o_w[:, :, :], o_pos[:, :, :], o_fl[:, :, :], ALU.subtract)
                    link(dve.scalar_tensor_tensor(o_idf[:, :], o_fl[:, 0, :], float(SIDE), o_fl[:, 1, :],
                                                  ALU.mult, ALU.add))
                    link(dve.tensor_scalar(o_u[:, :, :], o_w[:, :, :], -1.0, 1.0, ALU.mult, ALU.add))
                    for k, d in enumerate((0, 1, SIDE, SIDE + 1)):
                        ins = dve.tensor_scalar(o_idx[:, k, :], o_idf[:, :], float(d), None, ALU.add)
                    ins.then_inc(o_index, 1)
                    for k, (wy, wx) in enumerate(((o_u, o_u), (o_u, o_w), (o_w, o_u), (o_w, o_w))):
                        ins = dve.tensor_tensor(o_cw[:, k, :], wy[:, 0, :], wx[:, 1, :], ALU.mult)
                    link(ins)

                def sample(k):
                    dve.wait_ge(gathered[k], 16 * GQ * (b + 1))
                    vt = val_t[:, :, :].rearrange("p h (c q) -> p h q c", q=Q)
                    if k > 0:
                        dve.wait_ge(val_step, 4 * b + k)
                    for h in range(2):
                        for q in range(Q):
                            i = h * Q + q
                            if k == 0:
                                ins = dve.tensor_scalar(vt[:, h, q, :], corners[:, k, i, :], o_cw[:, k, i:i + 1],
                                                        None, ALU.mult)
                            else:
                                ins = dve.scalar_tensor_tensor(vt[:, h, q, :], corners[:, k, i, :],
                                                               o_cw[:, k, i:i + 1], vt[:, h, q, :],
                                                               ALU.mult, ALU.add)
                    ins.then_inc(val_step, 1)
                    if k == 3:
                        dve.wait_ge(val_step, 4 * b + 4)
                        dve.sem_inc(val_done, 1)

                def add_y(i):
                    if i == 0:
                        dve.wait_ge(xres_ld, 16 * (b + 1))
                    dve.wait_ge(at_full, AT_USES * b + AT_Y + i + 1)
                    cols = slice(i * YCOL, (i + 1) * YCOL)
                    dve.tensor_tensor(x_res[:, cols], at_ps[0:C, 0:YCOL], x_res[:, cols], ALU.add).then_inc(at_free, 1)

                def rest_of_y():
                    for i in range(4, 2 * Q):
                        add_y(i)
                    dve.wait_ge(at_free, AT_USES * (b + 1))
                    dve.sem_inc(y_step, 2 * Q)

                def gates():
                    u = slot["ffn"]
                    n = [G_STEPS * u]

                    def link(ins):
                        ins.then_inc(g_step, 1)
                        n[0] += 1
                        dve.wait_ge(g_step, n[0])

                    by_e = [SUB, E, SUBS]
                    dve.wait_ge(scored, TILES * (u + 1))
                    dve.tensor_tensor(g_s[:, :, :], score_ps, gate_b[u // NB][:, :].unsqueeze(2).broadcast_to(by_e),
                                      ALU.add).then_inc(g_scores_read, 1)
                    dve.wait_ge(g_scores_read, u + 1)
                    link(dve.tensor_reduce(g_m[:, :], g_s[:, :, :].rearrange("p e s -> p s e"), AX_X, ALU.max))
                    link(dve.tensor_tensor(g_s[:, :, :], g_s[:, :, :], g_m[:, :].unsqueeze(1).broadcast_to(by_e),
                                           ALU.subtract))
                    dve.wait_ge(g_exp, u + 1)
                    link(dve.tensor_reduce(g_m[:, :], g_p[:, :, :].rearrange("p e s -> p s e"), AX_X, ALU.add))
                    link(dve.reciprocal(g_r[:, :], g_m[:, :]))
                    link(dve.tensor_tensor(g_p[:, :, :], g_p[:, :, :], g_r[:, :].unsqueeze(1).broadcast_to(by_e),
                                           ALU.mult))
                    for i in range(E):
                        p_i = g_p[:, i, :].unsqueeze(1).broadcast_to(by_e)
                        dve.tensor_tensor(g_gt[:, i], p_i, g_p[:, :, :], ALU.is_gt)
                        ins = dve.tensor_tensor(g_eq[:, i], p_i, g_p[:, :, :], ALU.is_equal)
                    link(ins)
                    for i in range(E):
                        mask = before[:, i * E:(i + 1) * E].unsqueeze(2).broadcast_to(by_e)
                        ins = dve.tensor_tensor(g_eq[:, i], g_eq[:, i], mask, ALU.mult)
                    link(ins)
                    link(dve.tensor_tensor(g_gt[:, :, :, :].rearrange("p i j s -> p (i j s)"),
                                           g_gt[:, :, :, :].rearrange("p i j s -> p (i j s)"),
                                           g_eq[:, :, :, :].rearrange("p i j s -> p (i j s)"), ALU.add))
                    link(dve.tensor_reduce(g_rank[:, :, :].rearrange("p j s -> p (j s)"),
                                           g_gt[:, :, :, :].rearrange("p i j s -> p (j s) i"), AX_X, ALU.add))
                    link(dve.scalar_tensor_tensor(g_p[:, :, :].rearrange("p e s -> p (e s)"),
                                                  g_rank[:, :, :].rearrange("p e s -> p (e s)"), 1.5,
                                                  g_p[:, :, :].rearrange("p e s -> p (e s)"), ALU.is_lt, ALU.mult))
                    link(dve.tensor_reduce(g_m[:, :], g_p[:, :, :].rearrange("p e s -> p s e"), AX_X, ALU.add))
                    link(dve.tensor_scalar(g_m[:, :], g_m[:, :], TOPK_EPS, None, ALU.add))
                    link(dve.reciprocal(g_r[:, :], g_m[:, :]))
                    link(dve.tensor_tensor(g_s[:, :, :], g_p[:, :, :], g_r[:, :].unsqueeze(1).broadcast_to(by_e),
                                           ALU.mult))

                if slot["ffn"] is not None:
                    gates()
                if b is not None:
                    dve.wait_ge(xq_ld, 16 * Q * (b + 1))
                if slot["conv"] is not None:
                    dve.wait_ge(xq_ld, 16 * Q * (NB + slot["conv"] + 1))
                    dve.wait_ge(c_bias, G * (slot["conv"] + 1))
                if slot["conv"] == 0:
                    dve.sem_inc(c_step, G)
                if slot["ffn"] is not None and slot["ffn"] > 0:
                    dve.wait_ge(ffn_st[slot["ffn"] - 1], stored(slot["ffn"] - 1, TILES))
                steps(dve, slot, body, {
                    3: {"combine0": [norm_off], "normalize1": [apply_off]},
                    4: {"combine0": [offsets], "combine1": [positions]},
                    5: {"end": [lambda: sample(0), lambda: sample(1)]},
                    6: {"combine0": [lambda: sample(2), lambda: sample(3)], "combine2": [lambda: add_y(0)],
                        "combine3": [lambda: add_y(1), lambda: add_y(2)], "sum": [lambda: add_y(3)]}},
                    {4: prepare_weights, 6: rest_of_y} if b == 0 else {6: rest_of_y})
                if slot is SLOTS[0]:
                    dve.wait_ge(taps_set, 1)


def _constants():
    import numpy as np
    i = np.arange(E)
    before = (i[:, None] < i[None, :]).astype(np.float32).reshape(E * E)
    q_mask = (np.arange(128)[:, None] % Q == np.arange(Q)[None, :]).astype(np.float32)
    ref = (np.linspace(0.5, KSIDE - 0.5, KSIDE).astype(np.float32) / np.float32(KSIDE) * 2 - 1).astype(np.float32)
    point = (np.arange(Q)[None, None, :] * QPTS + np.arange(2)[None, :, None] * HPTS
             + np.arange(HPTS)[:, None, None]).reshape(HPTS, GQ)
    ref_pos = np.stack([ref[point // KSIDE], ref[point % KSIDE]], axis=1).reshape(HPTS, 2 * GQ)
    to_quarters = (np.arange(32)[:, None] == np.arange(128)[None, :] // Q).astype(np.float32)
    return {"c_to_quarters": to_quarters, "c_ident": np.eye(128, dtype=np.float32), "c_before": before, "c_q_mask": q_mask,
            "c_ref_pos": np.ascontiguousarray(ref_pos)}


def kernel(**inputs):
    import numpy as np
    import concourse.bacc as bacc
    from concourse.bass_utils import run_bass_kernel_spmd

    nc = bacc.Bacc("TRN2", target_bir_lowering=False, num_devices=1)
    arrays, aps = {}, {}
    for name, value in {**inputs, **_constants()}.items():
        v = np.ascontiguousarray(value)
        arrays[f"in_{name}"] = v
        aps[name] = nc.dram_tensor(f"in_{name}", v.shape, mybir.dt.from_np(v.dtype), kind="ExternalInput").ap()
    out = nc.dram_tensor("out_x", (NB, C, SIDE, SIDE), F32, kind="ExternalOutput").ap()
    metaformer_kernel(nc, aps, out)
    r = run_bass_kernel_spmd(nc, [arrays], core_ids=[0])
    return r.results[0]["out_x"]
```

```python
import math
from contextlib import ExitStack

import concourse.bass as bass
from concourse import mybir

F32 = mybir.dt.float32
F32R = mybir.dt.float32r
I32 = mybir.dt.int32
U32 = mybir.dt.uint32
ALU = mybir.AluOpType
ACT = mybir.ActivationFunctionType
AX_X = mybir.AxisListType.X

NB, C, SIDE = 4, 96, 56
PIX = SIDE * SIDE
KSIDE = SIDE // 2
POINTS = KSIDE * KSIDE
E, HID = 4, 384
SCALE = 32 ** -0.5

SUB = 2 * SIDE
NSUB = 4
TILE = NSUB * SUB
TILES = PIX // TILE
SUBS = TILES * NSUB
CHUNKS = E * HID // 128
CPE = HID // 128
G = 3
Q = 4
QPIX = PIX // Q
QROWS = SIDE // Q
QPTS = POINTS // Q
HPTS = QPTS // 2
GQ = 2 * Q
VBLK = QPIX // SUB
YCOL = QPIX // 2
PAD_A, PAD_C = 1, 3
ROWS_A, ROWS_C = QROWS + 2 * PAD_A, QROWS + 2 * PAD_C
LN_C_EPS, LN_T_EPS, TOPK_EPS = 1e-6, 1e-5, 1e-9

HID_RING, H_BANKS, Y_BANKS = 4, 2, 2

SLOTS = [
    dict(lnc=("a", 0)),
    dict(lnc=("a", 1), attn=0),
    dict(lnf=0, lnc=("a", 2), attn=1),
    dict(ffn=0, lnf=1, lnc=("a", 3), attn=2),
    dict(ffn=1, lnf=2, lnc=("c", 0), attn=3),
    dict(ffn=2, lnf=3, lnc=("c", 1), conv=0),
    dict(ffn=3, lnf=4, lnc=("c", 2), conv=1),
    dict(ffn=4, lnf=5, lnc=("c", 3), conv=2),
    dict(ffn=5, lnf=6, conv=3),
    dict(ffn=6, lnf=7),
    dict(ffn=7),
]
_ln_jobs, _lnc_jobs, _last = 0, 0, None
for _s in SLOTS:
    for _k in ("ffn", "lnf", "lnc", "attn", "conv"):
        _s.setdefault(_k, None)
    _s["ln_base"] = _ln_jobs
    _s["lnc_base"] = _lnc_jobs
    _lnc_jobs += TILES * (_s["lnc"] is not None)
    _s["ln_step"] = (_s["lnc"] is not None) + (_s["lnf"] is not None)
    _ln_jobs += TILES * _s["ln_step"]
    _s["before"] = _last
    _last = _s


def metaformer_kernel(nc, a, out):
    with ExitStack() as ctx:
        def sb(name, shape, dt=F32):
            return ctx.enter_context(nc.sbuf_tensor(name, shape, dt))

        def bank(name):
            return ctx.enter_context(nc.psum_tensor(name, [128, 512], F32))

        def sem(name):
            return ctx.enter_context(nc.semaphore(name))

        def scratch(name, shape):
            return nc.dram_tensor(name, shape, F32, kind="Internal").ap()

        norm = {"a": scratch("norm_a", (NB, C, (SIDE + 2 * PAD_A) * SIDE)),
                "c": scratch("norm_c", (NB, C, (SIDE + 2 * PAD_C) * SIDE))}
        pad = {"a": PAD_A, "c": PAD_C}
        x_in = a["x"].rearrange("b c h w -> b c (h w)")
        x_attn = scratch("x_attn", (NB + 1, C, PIX))[1:NB + 1]
        x_ffn0 = scratch("x_ffn0", (NB + 1, C, PIX))[1:NB + 1]
        x_conv = scratch("x_conv", (NB + 1, C, PIX))[1:NB + 1]
        x_out = out.rearrange("b c h w -> b c (h w)")
        value_pairs = [scratch(f"value_pairs{b}", (PIX, 2, C)) for b in range(NB)]
        gates_dram = scratch("gates_dram", (2 * NB + 1, E * PIX))[1:2 * NB + 1]
        ln_src = {"a": x_in, "c": x_ffn0}
        ffn_src = [x_attn] * NB + [x_conv] * NB
        ffn_dst = [x_ffn0] * NB + [x_out] * NB

        ident = sb("ident", [128, 128])
        q_mask = sb("q_mask", [128, Q])
        ref_pos = sb("ref_pos", [HPTS, 2 * GQ])
        zeros = sb("zeros", [128, PAD_C * SIDE])
        minus_half = sb("minus_half", [128, GQ])
        eps = {"c": sb("eps_c", [128, GQ]), "f": sb("eps_f", [128, GQ])}
        w1h = [sb(f"w1h{l}", [C, E * HID], F32R) for l in range(2)]
        w1l = [sb(f"w1l{l}", [C, E * HID], F32R) for l in range(2)]
        w2 = [sb(f"w2_{l}", [128, CHUNKS, C]) for l in range(2)]
        b1 = [sb(f"b1_{l}", [128, CHUNKS]) for l in range(2)]
        b2 = [sb(f"b2_{l}", [C, E]) for l in range(2)]
        gate_w = [sb(f"gate_w{l}", [C, E]) for l in range(2)]
        gate_b = [sb(f"gate_b{l}", [SUB, E]) for l in range(2)]
        ln_gb = sb("ln_gb", [HPTS, 2, C])
        w_off2 = sb("w_off2", [HPTS, 2, C])
        w_out = sb("w_out", [C, C])
        w_out_q = sb("w_out_q", [C, C * Q])
        w_exp = sb("w_exp", [128, G, Q * C])
        conv_w = {"w_a": (4, G, 9), "b_a": (4, G), "w_c": (G, 49), "w53": (G, 15), "w35": (G, 15),
                  "w7": (2, G, 7), "w5": (2, G, 5), "b_c": (3, G)}
        CONV_W = sum(math.prod(shape) for shape in conv_w.values())
        rows_w = sb("rows_w", [32, CONV_W])
        all_w = sb("all_w", [128, CONV_W])
        to_quarters = sb("to_quarters", [32, 128])

        def views(tile):
            at, parts = 0, []
            for shape in conv_w.values():
                n = math.prod(shape)
                names = "xyz"[:len(shape)]
                parts.append(tile[:, at:at + n].rearrange(
                    f"p ({' '.join(names)}) -> p {' '.join(names)}", **dict(zip(names, shape))))
                at += n
            return parts

        w_a, b_a, w_c, w53, w35, w7, w5, b_c = views(all_w)
        diag = sb("diag", [128, G, 7, 128])

        ln_x = {"f": sb("ln_x_f", [C, TILE]), "c": sb("ln_x_c", [C, TILE])}
        ln_stats = sb("ln_stats", [SUB, NSUB, 6])
        ln_mv = sb("ln_mv", [SUB, NSUB, 2])
        ln_ve = sb("ln_ve", [SUB, NSUB])
        ln_neg = sb("ln_neg", [SUB, NSUB])
        ln_bias = sb("ln_bias", [SUB, NSUB])
        minus_one = sb("minus_one", [SUB, NSUB])
        ln_rstd = sb("ln_rstd", [SUB, NSUB])
        ln_tok = sb("ln_tok", [SUB, NSUB, C])
        ln_cm = {"f": sb("ln_cm_f", [C, TILE]), "c": sb("ln_cm_c", [C, TILE])}

        xh = sb("xh", [C, PIX], F32R)
        xl = sb("xl", [C, PIX], F32R)
        hidden = [sb(f"hidden{i}", [128, TILE]) for i in range(HID_RING)]
        gate_t = [sb(f"gate_t{i}", [C, 2, TILE]) for i in range(2)]
        part = sb("part", [C, E, TILE])
        pair = sb("pair", [C, 2, TILE])
        res = sb("res", [C, TILE])
        ffn_out = sb("ffn_out", [C, TILE])

        raw_w1 = [part[:, :, :].rearrange("p e n -> p (e n)")[:, 0:E * HID],
                  diag[0:C, :, :, :].rearrange("p g y n -> p (g y n)")[:, 0:E * HID]]

        SE = E * SUBS
        g_s = sb("g_s", [SUB, E, SUBS])
        g_p = sb("g_p", [SUB, E, SUBS])
        g_m = sb("g_m", [SUB, SUBS])
        g_r = sb("g_r", [SUB, SUBS])
        g_gt = sb("g_gt", [SUB, E, E, SUBS])
        g_rank = sb("g_rank", [SUB, E, SUBS])
        g_tr = sb("g_tr", [SE, SUB])

        xq = sb("xq", [128, G, ROWS_C * SIDE])
        acc = [sb(f"acc{i}", [128, G, QPIX]) for i in range(2)]
        value, query = acc
        key = sb("key", [128, G, QPTS])
        off = sb("off", [128, G, QPTS])
        pixels = sb("pixels", [SUB, 4 * GQ * C])
        v_tok = pixels[:, 0:VBLK * Q * C].rearrange("p (q j c) -> p q j c", j=VBLK, q=Q)
        corner_pairs = pixels[0:HPTS, :].rearrange("p (r g n) -> p r g n", r=2, g=GQ)
        off_t = sb("off_t", [HPTS, 2, G * 128])
        key_t = sb("key_t", [HPTS, 2, G * 128])
        val_t = sb("val_t", [HPTS, 2, G * 128])
        o_stats = sb("o_stats", [HPTS, GQ, 6])
        o_mv = sb("o_mv", [HPTS, GQ, 2])
        o_ve = sb("o_ve", [HPTS, GQ])
        o_rstd = sb("o_rstd", [HPTS, GQ])
        o_n = sb("o_n", [HPTS, GQ, C])
        o_pos = sb("o_pos", [HPTS, 2, GQ])
        o_int = sb("o_int", [HPTS, 2, GQ], I32)
        o_fl = sb("o_fl", [HPTS, 2, GQ])
        o_gt = sb("o_gt", [HPTS, 2, GQ])
        o_w = sb("o_w", [HPTS, 2, GQ])
        o_u = sb("o_u", [HPTS, 2, GQ])
        o_idf = sb("o_idf", [HPTS, GQ])
        o_idx = sb("o_idx", [HPTS, 2, GQ], U32)
        o_cw = sb("o_cw", [HPTS, 4, GQ])
        kv = sb("kv", [128, G, 128])
        m2 = sb("m2", [128, G, Q * C])
        x_res = sb("x_res", [C, PIX])

        h_ps = [bank(f"h_ps{i}") for i in range(H_BANKS)]
        y_ps = [bank(f"y_ps{i}") for i in range(Y_BANKS)]
        lt_ps, lb_ps, lg_ps, at_ps = bank("lt_ps"), bank("lb_ps"), bank("lg_ps"), bank("at_ps")
        score_ps = lg_ps[0:SUB, 0:SE].rearrange("p (e s) -> p e s", e=E)

        ident_ld = sem("ident_ld")
        taps_ld = sem("taps_ld")
        const_ld = sem("const_ld")
        taps_spread = sem("taps_spread")
        taps_set = sem("taps_set")
        w1_split = sem("w1_split")
        pool_set = sem("pool_set")
        pads_done = sem("pads_done")
        wexp_ps = sem("wexp_ps")
        w_out_spread = sem("w_out_spread")
        wexp_done = sem("wexp_done")
        wc_done = sem("wc_done")
        diag_set = sem("diag_set")
        wc_chain_sem = sem("wc_chain_sem")
        val_step = sem("val_step")
        ln_loaded = {"f": sem("ln_loaded_f"), "c": sem("ln_loaded_c")}
        ln_turned = sem("ln_turned")
        ln_stat = sem("ln_stat")
        ln_var = sem("ln_var")
        ln_eps = sem("ln_eps")
        ln_root = sem("ln_root")
        ln_scale = sem("ln_scale")
        ln_applied = sem("ln_applied")
        ln_back = sem("ln_back")
        ln_moved = sem("ln_moved")
        scored = sem("scored")
        split = sem("split")
        norm_st = {(k, b): sem(f"norm_st_{k}{b}") for k in "ac" for b in range(NB)}
        h_full = sem("h_full")
        gelu_done = sem("gelu_done")
        hid_used = sem("hid_used")
        y_used = sem("y_used")
        gate_ld = [sem(f"gate_ld{i}") for i in range(2)]
        res_ld = sem("res_ld")
        summed = sem("summed")
        ffn_st = [sem(f"ffn_st{u}") for u in range(2 * NB)]
        g_step = sem("g_step")
        g_exp = sem("g_exp")
        g_scores_read = sem("g_scores_read")
        g_turned = sem("g_turned")
        g_moved = sem("g_moved")
        gates_st = [sem(f"gates_st{u}") for u in range(2 * NB)]
        xq_ld = sem("xq_ld")
        a_step = sem("a_step")
        at_full = sem("at_full")
        at_free = sem("at_free")
        o_step = sem("o_step")
        o_var = sem("o_var")
        o_eps = sem("o_eps")
        o_scale = sem("o_scale")
        o_gelu = sem("o_gelu")
        o_tanh = sem("o_tanh")
        o_index = sem("o_index")
        values_st = sem("values_st")
        gathered = [sem(f"gathered{r}") for r in range(2)]
        val_done = sem("val_done")
        xres_ld = sem("xres_ld")
        attn_st = [sem(f"attn_st{b}") for b in range(NB)]
        acc_ld = [sem(f"acc_ld{b}") for b in range(NB)]
        c_step = sem("c_step")
        c_bias = sem("c_bias")
        conv_st = [sem(f"conv_st{b}") for b in range(NB)]

        A_TAPS, Q_TAPS = G * 27, G * 9
        A_ALL = A_TAPS + Q_TAPS
        PIECES = 2 * G
        C_ALL = 42 * G + PIECES
        AT_USES = 2 + VBLK + 2 + 1 + G + 2 * Q
        AT_OFF, AT_VAL, AT_KEY, AT_KV, AT_M2, AT_Y = 0, 2, 2 + VBLK, 4 + VBLK, 5 + VBLK, 5 + VBLK + G
        O_STEPS, G_STEPS = 18, 12
        LATE_Y = 3
        TURNS = 2
        KEY_TURNS = 5
        GATES_TURN = 3
        const_count, taps_count = [0], [0]

        def ffn_at(slot, m):
            return slot["ffn"] * TILES + m

        def lnf_at(slot, m):
            return slot["lnf"] * TILES + m

        def stored(u, tiles):
            return (32 if u == NB else 16) * tiles

        def ln_jobs(slot, m):
            jobs = []
            n = slot["ln_base"] + slot["ln_step"] * m
            if slot["lnc"] is not None:
                jobs.append(("c", n))
                n = n + 1
            if slot["lnf"] is not None:
                jobs.append(("f", n))
            return jobs

        STAGES = {"c": dict(turn_in=2, apply=6, turn_back=7, move=8), "f": dict(turn_in=8, apply=11)}
        STAGES_BEFORE = dict(turn_back=1, move=2, scores=4)
        LAST_STAGES = {"c": dict(turn_in=3, apply=5, turn_back=6, move=7),
                       "f": dict(turn_in=6, apply=9, turn_back=10, move=11, scores=CHUNKS)}

        def is_last(m):
            return isinstance(m, int) and m == TILES - 1

        def norm_hooks(slot, m, stages, beside):
            hooks = {}

            def put(kind, n, tile, table):
                for stage, c in table.items():
                    if stage in stages:
                        hooks.setdefault(c, []).append(
                            lambda stage=stage: stages[stage](slot, tile, kind, n))

            jobs = ln_jobs(slot, m)
            if slot["lnf"] is not None and not (isinstance(m, int) and m == 0):
                put("f", jobs[-1][1] - slot["ln_step"], m - 1, STAGES_BEFORE)
            for kind, n in jobs:
                put(kind, n, m, (LAST_STAGES if is_last(m) else STAGES)[kind])
            for c, more in beside.items():
                hooks[c] = hooks.get(c, []) + more
            return hooks

        def steps(eng, slot, body, beside, behind={}, unroll=False):
            if unroll:
                for m in range(TILES):
                    body(m, None, beside.get(m, {}))
                return
            first = None if slot["attn"] is None else "first"
            body(0, first, beside.get(0, {}))
            if slot["attn"] is None:
                with eng.Fori(1, TILES - 1) as m:
                    body(m, None, {})
                body(TILES - 1, None, {})
                return
            with eng.Fori(1, 3) as m:
                body(m, first, {})
            for m in range(3, TILES):
                body(m, "second" if m < 6 else None, beside.get(m, {}))
                if m in behind:
                    behind[m]()

        def norm_before(slot):
            kind, b = slot["lnc"]
            if b > 0:
                return kind, b - 1
            return ("a", NB - 1) if kind == "c" else None

        block = ctx.enter_context(nc.Block())

        @block.sync
        def _(sp):
            sp.dma_start(ident[:, :], a["c_ident"]).then_inc(ident_ld, 16)
            sp.wait_ge(pool_set, 2)
            for k in "ac":
                n = pad[k] * SIDE
                for at in (0, n + PIX):
                    sp.dma_start(norm[k][:, :, at:at + n].rearrange("b c n -> c b n"),
                                 zeros[0:C, 0:n].unsqueeze(1).broadcast_to([C, NB, n])).then_inc(pads_done, 16)

            def const(dst, src):
                sp.dma_start(dst, src).then_inc(const_ld, 16)
                const_count[0] += 1

            def load_constants():
                with nc.allow_non_contiguous_dma("small"):
                    const(w_out[:, :], a["L0_conv_w_out"])
                    const(q_mask[:, :], a["c_q_mask"])
                    for l in range(2):
                        f = f"L{l}_ffn_"
                        const(raw_w1[l].rearrange("p (e h) -> p e h", e=E), a[f + "w1"].rearrange("e d h -> d e h"))
                        const(w2[l][:, :, :], a[f + "w2"].rearrange("e (j p) d -> p (e j) d", p=128))
                        const(b1[l][:, :], a[f + "b1"].rearrange("e (j p) -> p (e j)", p=128))
                        const(b2[l][:, :], a[f + "b2"].rearrange("e d -> d e"))
                        const(gate_w[l][:, :], a[f + "gate_w"])
                        const(gate_b[l][:, :], a[f + "gate_b"].partition_broadcast(SUB))

            def load_norm(slot, kind, n, at):
                if not (isinstance(n, int) and n == 0):
                    sp.wait_ge(ln_turned, n)
                if kind == "c":
                    k, b = slot["lnc"]
                    src = ln_src[k][b]
                else:
                    u = slot["lnf"]
                    src = ffn_src[u][u % NB]
                sp.dma_start(ln_x[kind][:, :], src[:, at]).then_inc(ln_loaded[kind], 16)

            def load_gates(slot, k, i, at):
                rows = gates_dram[slot["ffn"]].rearrange("(e t) -> e t", e=E)
                sp.wait_ge(y_used, Y_BANKS * i + E * k)
                sp.dma_start(gate_t[i][:, :, :], rows[2 * i:2 * i + 2, at].partition_broadcast(C))\
                    .then_inc(gate_ld[i], 16)

            def load_res(slot, k, at):
                u = slot["ffn"]
                sp.wait_ge(summed, 3 * k)
                sp.dma_start(res[:, :], ffn_src[u][u % NB][:, at]).then_inc(res_ld, 16)

            def body(m, part_of, beside):
                slot = body.slot
                more = not (isinstance(m, int) and m == TILES - 1)
                then = bass.ds(m * TILE + TILE, TILE)
                for kind, n in ln_jobs(slot, m):
                    if more:
                        load_norm(slot, kind, n + 1, then)
                    if kind == "c":
                        k, b = slot["lnc"]
                        sp.wait_ge(ln_moved, n + 1)
                        sp.dma_start(norm[k][b][:, bass.ds(m * TILE + pad[k] * SIDE, TILE)], ln_cm["c"][:, :])\
                            .then_inc(norm_st[k, b], 16)
                for also in beside.get("loads", []):
                    also()
                if slot["ffn"] is not None:
                    u, k = slot["ffn"], ffn_at(slot, m)
                    if more:
                        for i in range(2):
                            load_gates(slot, k + 1, i, then)
                        load_res(slot, k + 1, then)
                    sp.wait_ge(summed, 3 * k + 3)
                    for c0, c1 in ((C // 2, C), (0, C // 2)) if u == NB else ((0, C),):
                        sp.dma_start(ffn_dst[u][u % NB][c0:c1, bass.ds(m * TILE, TILE)], ffn_out[c0:c1, :])\
                            .then_inc(ffn_st[u], 16)

            def load_quarters(k, b, rows):
                src = norm[k][b].rearrange("(g c) n -> c g n", g=G)
                for q in range(Q):
                    sp.dma_start(xq[q::Q, :, 0:rows * SIDE], src[:, :, q * QPIX:q * QPIX + rows * SIDE])\
                        .then_inc(xq_ld, 16)

            def load_acc(b):
                for q in range(Q):
                    sp.dma_start(acc[b % 2][q::Q], x_ffn0[b].rearrange("(g c) (q n) -> q c g n", g=G, q=Q)[q])\
                        .then_inc(acc_ld[b], 16)

            for slot in SLOTS:
                body.slot = slot
                start = slice(0, TILE)
                if slot["lnc"] is not None:
                    k, b = slot["lnc"]
                    if k == "c":
                        sp.wait_ge(ffn_st[b], stored(b, TILES))
                    load_norm(slot, "c", slot["ln_base"], start)
                if slot["attn"] is not None:
                    b = slot["attn"]
                    if b == 0:
                        sp.wait_ge(pads_done, 16 * 4)
                    sp.wait_ge(norm_st["a", b], 16 * TILES)
                    sp.wait_ge(a_step, A_ALL * b)
                    load_quarters("a", b, ROWS_A)
                if slot["conv"] is not None:
                    b = slot["conv"]
                    sp.wait_ge(norm_st["c", b], 16 * TILES)
                    sp.wait_ge(a_step, A_ALL * NB)
                    if b > 0:
                        sp.wait_ge(c_step, C_ALL * b)
                    load_quarters("c", b, ROWS_C)
                if slot["before"] is not None and slot["before"]["attn"] is not None:
                    b = slot["before"]["attn"]
                    sp.wait_ge(at_free, AT_USES * (b + 1))
                    sp.dma_start(x_attn[b], x_res[:, :]).then_inc(attn_st[b], 16)
                if slot["before"] is not None and slot["before"]["conv"] is not None:
                    b = slot["before"]["conv"]
                    sp.wait_ge(c_step, C_ALL * (b + 1))
                    for q in range(Q):
                        sp.dma_start(x_conv[b].rearrange("(g c) (q n) -> q c g n", g=G, q=Q)[q],
                                     acc[b % 2][q::Q]).then_inc(conv_st[b], 16)
                if slot["ffn"] is not None:
                    u, k = slot["ffn"], ffn_at(slot, 0)
                    load_res(slot, k, start)
                    sp.wait_ge(gates_st[u], 16)
                    for i in range(2):
                        load_gates(slot, k, i, start)
                if slot["lnf"] is not None:
                    u = slot["lnf"]
                    sp.wait_ge(attn_st[u] if u < NB else conv_st[u - NB], 16 if u < NB else 16 * Q)
                    load_norm(slot, "f", slot["ln_base"], start)
                if slot["attn"] is not None:
                    b = slot["attn"]
                    if b > 0:
                        sp.wait_ge(attn_st[b - 1], 16)
                    sp.dma_start(x_res[:, :], x_in[b]).then_inc(xres_ld, 16)
                if slot["conv"] is not None and slot["conv"] + 1 < NB:
                    if slot["conv"] > 0:
                        sp.wait_ge(conv_st[slot["conv"] - 1], 16 * Q)
                    else:
                        sp.wait_ge(at_free, AT_USES * NB)
                    load_acc(slot["conv"] + 1)

                def store_values():
                    b = slot["attn"]
                    sp.wait_ge(at_free, AT_USES * b + AT_VAL + VBLK)
                    v = pixels[:, 0:Q * VBLK * C].rearrange("p (s c) -> p s c", c=C)
                    for dst, src in ((value_pairs[b][:, 0].rearrange("(s p) c -> p s c", p=SUB), v),
                                     (value_pairs[b][SUB - 1:PIX - 1, 1].rearrange("(s p) c -> p s c", p=SUB),
                                      v[:, 1:]),
                                     (value_pairs[b][0:SUB - 1, 1], v[1:SUB, 0])):
                        sp.dma_start(dst, src).then_inc(values_st, 16)
                    if b == NB - 1:
                        load_acc(0)

                if slot["attn"] == 0:
                    load_constants()
                steps(sp, slot, body, {3: {"loads": [store_values]}})
            for u in range(2 * NB):
                sp.wait_ge(ffn_st[u], stored(u, TILES))

        @block.scalar
        def _(act):
            act.sem_inc(gelu_done, H_BANKS)

            def load(dst, src):
                act.dma_start(dst, src).then_inc(taps_ld, 16)
                taps_count[0] += 1

            with nc.allow_non_contiguous_dma("small"):
                load(to_quarters[:, :], a["c_to_quarters"])
                r_w_a, r_b_a, r_w_c, r_w53, r_w35, r_w7, r_w5, r_b_c = views(rows_w)
                for n, w in enumerate(("v", "k", "off1", "q")):
                    load(r_w_a[:, n], a[f"L0_conv_w_{w}"].rearrange("(g c) o h w -> c g (o h w)", g=G))
                    load(r_b_a[:, n], a[f"L0_conv_b_{w}"].rearrange("(g c) -> c g", g=G))
                for dst, w in ((r_w_c, "w77"), (r_w53, "w53"), (r_w35, "w35"), (r_w7[:, 0], "w7h"),
                               (r_w7[:, 1], "w7w"), (r_w5[:, 0], "w5h"), (r_w5[:, 1], "w5w")):
                    load(dst, a[f"L1_conv_{w}"].rearrange("(g c) o h w -> c g (o h w)", g=G))
                for n, w in enumerate(("b77", "b53", "b35")):
                    load(r_b_c[:, n], a[f"L1_conv_{w}"].rearrange("(g c) -> c g", g=G))
                load(ref_pos[:, :], a["c_ref_pos"])
                load(ln_gb[:, 0], a["L0_conv_ln_g"].partition_broadcast(HPTS))
                load(ln_gb[:, 1], a["L0_conv_ln_b"].partition_broadcast(HPTS))
                load(w_off2[:, :], a["L0_conv_w_off2"].partition_broadcast(HPTS))

            def add_bias(b):
                act.wait_ge(acc_ld[b], 16 * Q)
                act.wait_ge(wc_done, 1)
                for g in range(G):
                    act.activation(acc[b % 2][:, g, :], acc[b % 2][:, g, :], ACT.Identity, bias=b_c[:, 0, g:g + 1])\
                        .then_inc(c_bias, 1)

            def make_diagonals():
                act.wait_ge(wc_done, 1)
                for g in range(G):
                    for dy in range(7):
                        w = w_c[:, g, 7 * dy + 3:7 * dy + 4]
                        ins = act.activation(diag[:, g, dy, :], ident[:, :], ACT.Identity, scale=w)
                ins.then_inc(diag_set, 1)

            def apply(slot, m, kind, n):
                act.wait_ge(ln_scale, n + 1)
                if not (isinstance(n, int) and n == 0):
                    act.wait_ge(ln_back, n)
                for s in range(NSUB):
                    ins = act.activation(ln_tok[:, s, :], lt_ps[0:SUB, s * C:(s + 1) * C], ACT.Identity,
                                         bias=ln_bias[:, s:s + 1], scale=ln_rstd[:, s:s + 1])
                ins.then_inc(ln_applied, 1)

            def move(slot, m, kind, n):
                act.wait_ge(ln_back, n + 1)
                if kind == "f":
                    act.wait_ge(scored, lnf_at(slot, m))
                    act.wait_ge(split, lnf_at(slot, m))
                else:
                    act.wait_ge(norm_st[slot["lnc"]], 16 * m)
                if kind == "f":
                    if slot["ffn"] is not None:
                        act.wait_ge(h_full, CHUNKS * ffn_at(slot, m) + CHUNKS)
                    act.copy(xh[:, bass.ds(m * TILE, TILE)], lb_ps[0:C, 0:TILE])
                act.copy(ln_cm[kind][:, :], lb_ps[0:C, 0:TILE]).then_inc(ln_moved, 1)

            def body(m, part_of, beside):
                slot = body.slot
                hooks = norm_hooks(slot, m, dict(apply=apply, move=move), beside)
                if slot["ffn"] is None:
                    for c in sorted(hooks):
                        for hook in hooks[c]:
                            hook()
                    return
                k, l = ffn_at(slot, m), slot["ffn"] // NB
                for c in range(CHUNKS):
                    act.wait_ge(h_full, CHUNKS * k + c + 1)
                    act.wait_ge(hid_used, CHUNKS * k + c + 1)
                    act.activation(hidden[c % HID_RING][:, :], h_ps[c % H_BANKS][:, 0:TILE], ACT.Gelu,
                                   bias=b1[l][:, c:c + 1]).then_inc(gelu_done, 1)
                    for hook in hooks.get(c, []):
                        hook()

            for slot in SLOTS:
                body.slot = slot
                b = slot["attn"]
                base = AT_USES * (b or 0)
                if slot["lnc"] is not None and norm_before(slot) is not None:
                    act.wait_ge(norm_st[norm_before(slot)], 16 * TILES)

                def full(i):
                    act.wait_ge(at_full, base + i + 1)

                def take_off(h):
                    full(AT_OFF + h)
                    act.copy(off_t[:, h, :], at_ps[0:HPTS, 0:G * 128]).then_inc(at_free, 1)

                def take_value(j):
                    full(AT_VAL + j)
                    act.copy(v_tok[:, :, j, :].rearrange("p q c -> p c q"),
                             at_ps[0:SUB, 0:G * 128].rearrange("p (c q) -> p c q", q=Q)).then_inc(at_free, 1)

                def take_key(h):
                    full(AT_KEY + h)
                    act.copy(key_t[:, h, :], at_ps[0:HPTS, 0:G * 128]).then_inc(at_free, 1)

                def gelu():
                    act.wait_ge(o_step, O_STEPS * b + 4)
                    act.activation(o_n[:, :, :], o_n[:, :, :], ACT.Gelu).then_inc(o_gelu, 1)

                def tanh():
                    act.wait_ge(o_step, O_STEPS * b + 9)
                    act.activation(o_pos[:, :, :], o_pos[:, :, :], ACT.Tanh).then_inc(o_tanh, 1)

                def take_kv():
                    full(AT_KV)
                    for h in range(4):
                        r = slice(32 * h, 32 * h + 32)
                        ins = act.activation(kv[r, :, r],
                                             at_ps[r, 0:G * 128].rearrange("p (g n) -> p g n", g=G)[:, :, r],
                                             ACT.Copy, scale=SCALE)
                    ins.then_inc(at_free, 1)

                def take_m2(g):
                    full(AT_M2 + g)
                    act.copy(m2[:, g, :], at_ps[:, 0:Q * C]).then_inc(at_free, 1)

                takes = [lambda h=h: take_off(h) for h in range(2)]
                takes += [lambda j=j: take_value(j) for j in range(VBLK)]
                takes += [lambda h=h: take_key(h) for h in range(2)]
                def exp_scores():
                    u = slot["ffn"]
                    act.wait_ge(g_step, G_STEPS * u + 2)
                    act.activation(g_p[:, :, :], g_s[:, :, :], ACT.Exp).then_inc(g_exp, 1)

                def take_gates():
                    u = slot["ffn"]
                    act.wait_ge(g_turned, u + 1)
                    if u > 0:
                        act.wait_ge(gates_st[u - 1], 16)
                    act.copy(g_tr[:, :], lg_ps[0:SE, 128:128 + SUB]).then_inc(g_moved, 1)
                    act.wait_ge(g_moved, u + 1)
                    act.dma_start(gates_dram[u].rearrange("(s t) -> s t", t=SUB), g_tr[:, :]).then_inc(gates_st[u], 16)

                behind = {}
                if b == 0:
                    behind = {6: make_diagonals}
                elif b == NB - 1:
                    behind = {4: lambda: add_bias(0)}
                steps(act, slot, body, {
                    0: {} if slot["ffn"] is None else {1: [exp_scores], GATES_TURN: [take_gates]},
                    3: {**{TURNS + i: [take] for i, take in enumerate(takes[:AT_KEY - 1])},
                        TURNS + AT_KEY - 1: [takes[AT_KEY - 1], gelu]},
                    4: {3: [tanh], **{KEY_TURNS + i: [take] for i, take in enumerate(takes[AT_KEY:])}},
                    6: {1: [take_kv], **{2 + g: [lambda g=g: take_m2(g)] for g in range(G)}}}, behind)
                if slot is SLOTS[0]:
                    act.wait_ge(taps_spread, 1)
                    act.copy(all_w[:, :], at_ps[:, 0:CONV_W]).then_inc(taps_set, 1)
                if slot["conv"] is not None and slot["conv"] + 1 < NB:
                    add_bias(slot["conv"] + 1)

        N_CONST, N_TAPS = const_count[0], taps_count[0]

        @block.gpsimd
        def _(pool):
            pool.memset(zeros[:, :], 0.0).then_inc(pool_set, 1)
            pool.memset(kv[:, :, :], 0.0).then_inc(pool_set, 1)
            pool.memset(minus_half[:, :], -0.5).then_inc(pool_set, 1)
            pool.memset(eps["c"][:, :], LN_C_EPS).then_inc(pool_set, 1)
            pool.memset(eps["f"][:, :], LN_T_EPS).then_inc(pool_set, 1)
            pool.memset(minus_one[:, :], -1.0).then_inc(pool_set, 1)
            pool.memset(g_gt[:, :, :, :], 0.0).then_inc(pool_set, 1)
            pool.wait_ge(pool_set, 7)

            def body(m, part_of, beside):
                slot = body.slot
                for i, (kind, n) in enumerate(ln_jobs(slot, m)):
                    pool.wait_ge(ln_var, n + 1)
                    pool.wait_ge(ln_applied, n)
                    pool.tensor_tensor(ln_ve[:, :], ln_mv[:, :, 1], eps[kind][0:SUB, 0:NSUB], ALU.add)
                    pool.tensor_tensor(ln_neg[:, :], ln_mv[:, :, 0], minus_one[:, :], ALU.mult).then_inc(ln_eps, 1)
                    pool.wait_ge(ln_eps, n + 1)
                    pool.tensor_tensor(ln_rstd[:, :], ln_ve[:, :], minus_half[0:SUB, 0:NSUB], ALU.pow)\
                        .then_inc(ln_root, 1)
                    pool.wait_ge(ln_root, n + 1)
                    pool.tensor_tensor(ln_bias[:, :], ln_neg[:, :], ln_rstd[:, :], ALU.mult).then_inc(ln_scale, 1)
                    for more in beside.get(i, []):
                        more()
                for more in beside.get("end", []):
                    more()

            for slot in SLOTS:
                body.slot = slot

                def scale_off():
                    b = slot["attn"]
                    pool.wait_ge(o_var, b + 1)
                    pool.tensor_scalar(o_ve[:, :], o_mv[:, :, 1], LN_T_EPS, None, ALU.add).then_inc(o_eps, 1)
                    pool.wait_ge(o_eps, b + 1)
                    pool.tensor_tensor(o_rstd[:, :], o_ve[:, :], minus_half[0:HPTS, :], ALU.pow).then_inc(o_scale, 1)

                def gather(r):
                    b = slot["attn"]
                    pool.wait_ge(o_index, b + 1)
                    pool.wait_ge(values_st, 48 * (b + 1))
                    for g in range(GQ):
                        pool.indirect_dma_start(
                            corner_pairs[:, r, g, :], None,
                            value_pairs[b][0:PIX - 1].rearrange("n i c -> n (i c)"),
                            bass.IndirectOffsetOnAxis(ap=o_idx[:, r, g:g + 1], axis=0)).then_inc(gathered[r], 16)

                steps(pool, slot, body, {
                    3: {0: [scale_off]},
                    4: {0: [lambda: gather(0)], "end": [lambda: gather(1)]}})

        @block.tensor
        def _(pe):
            pe.sem_inc(hid_used, HID_RING)
            pe.wait_ge(ident_ld, 16)

            def spread_w_out():
                pe.wait_ge(w_out_spread, 1)
                pe.wait_ge(at_free, AT_KV)
                for g in range(G):
                    if g > 0:
                        pe.wait_ge(wexp_done, g)
                    pe.matmul(at_ps[:, 0:C], w_out_q[:, g * 128:(g + 1) * 128], ident[0:C, 0:C],
                              start=True, stop=True).then_inc(wexp_ps, 1)
                pe.wait_ge(wexp_done, G)

            def turn_in(slot, m, kind, n):
                pe.wait_ge(ln_loaded[kind], 16 * ((lnf_at(slot, m) if kind == "f" else slot["lnc_base"] + m) + 1))
                pe.wait_ge(ln_applied, n)
                for s in range(NSUB):
                    last = pe.transpose(lt_ps[0:SUB, s * C:(s + 1) * C], ln_x[kind][:, s * SUB:(s + 1) * SUB],
                                        ident[0:C, 0:C])
                last.then_inc(ln_turned, 1)

            def turn_back(slot, m, kind, n):
                pe.wait_ge(ln_applied, n + 1)
                pe.wait_ge(ln_moved, n)
                for s in range(NSUB):
                    last = pe.transpose(lb_ps[0:C, s * SUB:(s + 1) * SUB], ln_tok[:, s, :], ident[0:SUB, 0:SUB])
                last.then_inc(ln_back, 1)

            def scores(slot, m, kind, n):
                u = slot["lnf"]
                if isinstance(m, int) and m == 0 and u > 0:
                    pe.wait_ge(g_scores_read, u)
                pe.wait_ge(ln_moved, n + 1)
                for s in range(NSUB):
                    last = pe.matmul(score_ps[:, :, bass.ds(m * NSUB + s, 1)].rearrange("p e s -> p (e s)"),
                                     ln_cm["f"][:, s * SUB:(s + 1) * SUB], gate_w[u // NB][:, :],
                                     start=True, stop=True)
                last.then_inc(scored, 1)

            def second(slot, m, c):
                k, l = ffn_at(slot, m), slot["ffn"] // NB
                e, j = c // CPE, c % CPE
                pe.wait_ge(gelu_done, H_BANKS + CHUNKS * k + c + 1)
                if j == 0:
                    pe.wait_ge(y_used, E * k + e + 1)
                pe.matmul(y_ps[e % Y_BANKS][0:C, 0:TILE], w2[l][:, c, :], hidden[c % HID_RING][:, :],
                          start=(j == 0), stop=(j == CPE - 1)).then_inc(hid_used, 1)

            def body(m, part_of, beside):
                slot = body.slot
                hooks = norm_hooks(slot, m, dict(turn_in=turn_in, turn_back=turn_back, scores=scores), beside)
                if slot["ffn"] is None:
                    for c in sorted(hooks):
                        for hook in hooks[c]:
                            hook()
                    return
                k, l = ffn_at(slot, m), slot["ffn"] // NB
                pe.wait_ge(split, k + 1)
                for c in range(CHUNKS):
                    pe.wait_ge(gelu_done, CHUNKS * k + c + 1)
                    ps = h_ps[c % H_BANKS][:, 0:TILE]
                    cols = bass.ds(m * TILE, TILE)
                    hi, lo = w1h[l][:, c * 128:(c + 1) * 128], w1l[l][:, c * 128:(c + 1) * 128]
                    pe.matmul(ps, hi, xh[:, cols], start=True, stop=False)
                    pe.matmul(ps, hi, xl[:, cols], start=False, stop=False)
                    pe.matmul(ps, lo, xh[:, cols], start=False, stop=True).then_inc(h_full, 1)
                    for hook in hooks.get(c, []):
                        hook()
                    if c > 0:
                        second(slot, m, c - 1)
                second(slot, m, CHUNKS - 1)
                for hook in hooks.get(CHUNKS, []):
                    hook()

            def times_query(b, i):
                if i == 0:
                    pe.wait_ge(a_step, A_ALL * (b + 1))
                q, h = i // 2, i % 2
                pe.wait_ge(at_free, AT_USES * b + AT_Y + i)
                for g in range(G):
                    last = pe.matmul(at_ps[0:C, 0:YCOL], m2[:, g, q * C:(q + 1) * C],
                                     query[:, g, h * YCOL:(h + 1) * YCOL], start=(g == 0), stop=(g == G - 1))
                last.then_inc(at_full, 1)

            for slot in SLOTS:
                body.slot = slot
                b = slot["attn"]
                base = AT_USES * (b or 0)

                def use(i):
                    if base + i > 0:
                        pe.wait_ge(at_free, base + i)

                def turn(i, src, width):
                    use(i)
                    for g in range(G):
                        last = pe.transpose(at_ps[0:width, g * 128:(g + 1) * 128], src(g), ident[:, :])
                    last.then_inc(at_full, 1)

                def turn_off(h):
                    if h == 0:
                        pe.wait_ge(a_step, A_ALL * b + A_TAPS)
                    turn(AT_OFF + h, lambda g: off[:, g, h * HPTS:(h + 1) * HPTS], HPTS)

                def turn_value(j):
                    turn(AT_VAL + j, lambda g: value[:, g, j * SUB:(j + 1) * SUB], SUB)

                def turn_key(h):
                    turn(AT_KEY + h, lambda g: key[:, g, h * HPTS:(h + 1) * HPTS], HPTS)

                def keys_values():
                    pe.wait_ge(val_done, b + 1)
                    use(AT_KV)
                    for g in range(G):
                        for h in range(2):
                            last = pe.matmul(at_ps[:, g * 128:(g + 1) * 128], val_t[:, h, g * 128:(g + 1) * 128],
                                             key_t[:, h, g * 128:(g + 1) * 128], start=(h == 0), stop=(h == 1))
                    last.then_inc(at_full, 1)

                def times_w_out(g):
                    use(AT_M2 + g)
                    pe.matmul(at_ps[:, 0:Q * C], kv[:, g, :], w_exp[:, g, :], start=True, stop=True)\
                        .then_inc(at_full, 1)

                turns = [lambda h=h: turn_off(h) for h in range(2)]
                turns += [lambda j=j: turn_value(j) for j in range(VBLK)]
                turns += [lambda h=h: turn_key(h) for h in range(2)]
                def turn_gates():
                    u = slot["ffn"]
                    pe.wait_ge(g_step, G_STEPS * (u + 1))
                    pe.transpose(lg_ps[0:SE, 128:128 + SUB], g_s[:, :, :].rearrange("p e s -> p (e s)"),
                                 ident[0:SUB, 0:SUB]).then_inc(g_turned, 1)

                beside_first = {} if slot["ffn"] is None else {GATES_TURN: [turn_gates]}
                if slot["before"] is not None and slot["before"]["attn"] is not None:
                    for n in range(LATE_Y):
                        beside_first[n] = [lambda n=n: times_query(slot["before"]["attn"], 2 * Q - LATE_Y + n)]
                def middle_column(m, dy):
                    g, h, n = m // 2, m % 2, AT_USES * NB + PIECES * slot["conv"] + m
                    if dy == 0:
                        pe.wait_ge(at_free, n)
                        if m == 0:
                            pe.wait_ge(diag_set, 1)
                            pe.wait_ge(xq_ld, 16 * Q * (NB + slot["conv"] + 1))
                    at = dy * SIDE + h * YCOL
                    ins = pe.matmul(at_ps[:, 0:YCOL], diag[:, g, dy, :], xq[:, g, at:at + YCOL],
                                    start=(dy == 0), stop=(dy == 6))
                    if dy == 6:
                        ins.then_inc(at_full, 1)

                if slot["conv"] is not None:
                    table = {m: {5 + dy: [lambda m=m, dy=dy: middle_column(m, dy)] for dy in range(7)}
                             for m in range(PIECES)}
                    for c, hooks in beside_first.items():
                        table[0][c] = hooks + table[0].get(c, [])
                    steps(pe, slot, body, table, unroll=True)
                    continue
                steps(pe, slot, body, {
                    0: beside_first,
                    3: {TURNS + i: [t] for i, t in enumerate(turns[:AT_KEY])},
                    4: {KEY_TURNS + i: [t] for i, t in enumerate(turns[AT_KEY:])},
                    6: {1: [keys_values], **{2 + g: [lambda g=g: times_w_out(g)] for g in range(G)},
                        **{5 + i: [lambda i=i: times_query(b, i)] for i in range(2 * Q - LATE_Y)}}},
                    {4: spread_w_out} if b == 0 else {})
                if slot is SLOTS[0]:
                    pe.wait_ge(taps_ld, 16 * N_TAPS)
                    pe.matmul(at_ps[:, 0:CONV_W], to_quarters[:, :], rows_w[:, :], start=True, stop=True)\
                        .then_inc(taps_spread, 1)

        @block.vector
        def _(dve):
            dve.sem_inc(y_used, Y_BANKS)
            def prepare_weights():
                dve.wait_ge(const_ld, 16 * N_CONST)
                for l in range(2):
                    raw = raw_w1[l]
                    dve.tensor_copy(w1h[l][:, :], raw).then_inc(w1_split, 1)
                    dve.wait_ge(w1_split, 2 * l + 1)
                    dve.tensor_tensor(w1l[l][:, :], raw, w1h[l][:, :].bitcast(F32), ALU.subtract).then_inc(w1_split, 1)
                dve.tensor_copy(w_out_q[:, :].rearrange("p (c q) -> p c q", q=Q),
                                w_out[:, :].unsqueeze(2).broadcast_to([C, C, Q]))\
                    .then_inc(w_out_spread, 1)
                for g in range(G):
                    dve.wait_ge(wexp_ps, g + 1)
                    for q in range(Q):
                        ins = dve.tensor_scalar(w_exp[:, g, q * C:(q + 1) * C], at_ps[:, 0:C], q_mask[:, q:q + 1], None,
                                                ALU.mult)
                    ins.then_inc(wexp_done, 1)
                n_wc = [0]

                def wc_chain(ins):
                    ins.then_inc(wc_chain_sem, 1)
                    n_wc[0] += 1
                    dve.wait_ge(wc_chain_sem, n_wc[0])

                wcv = w_c[:, :, :].rearrange("p g (h w) -> p g h w", w=7)
                v53 = w53[:, :, :].rearrange("p g (h w) -> p g h w", w=3)
                v35 = w35[:, :, :].rearrange("p g (h w) -> p g h w", w=5)
                wc_chain(dve.tensor_tensor(wcv[:, :, 1:6, 2:5], wcv[:, :, 1:6, 2:5], v53, ALU.add))
                wc_chain(dve.tensor_tensor(wcv[:, :, 2:5, 1:6], wcv[:, :, 2:5, 1:6], v35, ALU.add))
                for w, n in ((w7, 7), (w5, 5)):
                    o = (7 - n) // 2
                    for g in range(G):
                        for i in range(n):
                            row = wcv[:, g, o + i, o:o + n]
                            ins = dve.scalar_tensor_tensor(row, w[:, 1, g, :], w[:, 0, g, i:i + 1], row,
                                                           ALU.mult, ALU.add)
                    wc_chain(ins)
                wc_chain(dve.tensor_tensor(b_c[:, 0], b_c[:, 0], b_c[:, 1], ALU.add))
                dve.tensor_tensor(b_c[:, 0], b_c[:, 0], b_c[:, 2], ALU.add).then_inc(wc_done, 1)
                dve.wait_ge(wc_done, 1)

            def normalize(n):
                dve.wait_ge(ln_turned, n + 1)
                for s in range(NSUB):
                    ins = dve.bn_stats(ln_stats[:, s, :], lt_ps[0:SUB, s * C:(s + 1) * C])
                ins.then_inc(ln_stat, 1)
                dve.wait_ge(pool_set, 7)
                dve.wait_ge(ln_stat, n + 1)
                for s in range(NSUB):
                    ins = dve.bn_aggr(ln_mv[:, s, :], ln_stats[:, s, :])
                ins.then_inc(ln_var, 1)

            def split_tile(slot, m, n):
                dve.wait_ge(ln_moved, n + 1)
                cols = bass.ds(m * TILE, TILE)
                dve.tensor_tensor(xl[:, cols], ln_cm["f"][:, :], xh[:, cols].bitcast(F32), ALU.subtract)\
                    .then_inc(split, 1)

            def combine(slot, m, e):
                k, l = ffn_at(slot, m), slot["ffn"] // NB
                dve.wait_ge(hid_used, HID_RING + CHUNKS * k + CPE * (e + 1))
                dve.wait_ge(gate_ld[e // 2], 16 * (k + 1))
                if e == 0:
                    dve.wait_ge(summed, 3 * k)
                dve.scalar_tensor_tensor(part[:, e, :], y_ps[e % Y_BANKS][0:C, 0:TILE], b2[l][:, e:e + 1],
                                         gate_t[e // 2][:, e % 2, :], ALU.add, ALU.mult).then_inc(y_used, 1)

            def sum_pairs(slot, m):
                k = ffn_at(slot, m)
                dve.wait_ge(y_used, Y_BANKS + E * (k + 1))
                dve.tensor_tensor(pair[:, :, :], part[:, 0:2, :], part[:, 2:4, :], ALU.add).then_inc(summed, 1)

            def sum_experts(slot, m):
                k = ffn_at(slot, m)
                dve.wait_ge(summed, 3 * k + 1)
                dve.tensor_tensor(part[:, 0, :], pair[:, 0, :], pair[:, 1, :], ALU.add).then_inc(summed, 1)

            def sum_residual(slot, m):
                k, u = ffn_at(slot, m), slot["ffn"]
                dve.wait_ge(summed, 3 * k + 2)
                dve.wait_ge(res_ld, 16 * (k + 1))
                if not (isinstance(m, int) and m == 0):
                    dve.wait_ge(ffn_st[u], stored(u, m))
                dve.tensor_tensor(ffn_out[:, :], part[:, 0, :], res[:, :], ALU.add).then_inc(summed, 1)

            def taps3(out_ap, in_ap, n, g, base, at, step, stride):
                side = SIDE // stride
                rows_in = in_ap.rearrange("p (r x) -> p r x", x=SIDE)
                rows_out = out_ap.rearrange("p (r x) -> p r x", x=side)
                order = [(0, 1)] + [(dy, dx) for dy in range(3) for dx in range(3) if (dy, dx) != (0, 1)]
                done = []
                for i, (dy, dx) in enumerate(order):
                    x0 = 1 if dx == 0 else 0
                    x1 = side - 1 if dx == 2 and stride == 1 else side
                    c0 = stride * x0 + dx - 1
                    nr = QROWS // stride
                    src = rows_in[:, dy:dy + stride * (nr - 1) + 1:stride, c0:c0 + stride * (x1 - x0 - 1) + 1:stride]
                    dst = rows_out[:, :, x0:x1]
                    w = w_a[:, n, g, dy * 3 + dx:dy * 3 + dx + 1]

                    def op(i=i, src=src, dst=dst, w=w):
                        if i == 0:
                            ins = dve.tensor_scalar(dst, src, w, b_a[:, n, g], ALU.mult, ALU.add)
                        else:
                            dve.wait_ge(a_step, base + at + step * (i - 1) + 1)
                            ins = dve.scalar_tensor_tensor(dst, src, w, dst, ALU.mult, ALU.add)
                        ins.then_inc(a_step, 1)
                    done.append(op)
                return done

            def attn_taps(slot, m, part_of):
                base = A_ALL * slot["attn"]
                g = bass.ds(m if part_of == "first" else m - 3, 1)
                src = xq[:, g, 0:ROWS_A * SIDE].rearrange("p g n -> p (g n)")

                def one(t):
                    return t[:, g, :].rearrange("p g n -> p (g n)")
                if part_of == "first":
                    base = base + 27 * m
                    lists = [taps3(one(value), src, 0, g, base, 0, 3, 1), taps3(one(key), src, 1, g, base, 1, 3, 2),
                             taps3(one(off), src, 2, g, base, 2, 3, 2)]
                    return [op for three in zip(*lists) for op in three]
                base = base + A_TAPS + 9 * (m - 3)
                return taps3(one(query), src, 3, g, base, 0, 1, 1)

            c_count, c_last = [0], [0] * G

            def conv_taps(slot, m):
                b = slot["conv"]
                ops = []

                def step(g, ins):
                    ins.then_inc(c_step, 1)
                    c_count[0] += 1
                    c_last[g] = c_count[0]

                for dx in (2, 0, 1, 4, 5, 6):
                    x0, x1 = max(0, 3 - dx), SIDE - max(0, dx - 3)
                    for g in range(G):
                        src = xq[:, g, m * SIDE:m * SIDE + QPIX].rearrange("p (r x) -> p r x", x=SIDE)[
                            :, :, x0 + dx - 3:x1 + dx - 3]
                        dst = acc[b % 2][:, g, :].rearrange("p (r x) -> p r x", x=SIDE)[:, :, x0:x1]

                        def op(g=g, src=src, dst=dst, w=w_c[:, g, m * 7 + dx:m * 7 + dx + 1]):
                            if c_last[g] > 0:
                                dve.wait_ge(c_step, c_last[g])
                            step(g, dve.scalar_tensor_tensor(dst, src, w, dst, ALU.mult, ALU.add))
                        ops.append(op)

                def add_middle(g, h):
                    half = acc[b % 2][:, g, h * YCOL:(h + 1) * YCOL]
                    dve.wait_ge(at_full, AT_USES * NB + PIECES * b + m + 1)
                    dve.wait_ge(c_step, c_last[g])
                    ins = dve.tensor_tensor(half, at_ps[:, 0:YCOL], half, ALU.add)
                    step(g, ins)
                    dve.wait_ge(c_step, c_last[g])
                    dve.sem_inc(at_free, 1)
                if m < PIECES:
                    ops.append(lambda: add_middle(m // 2, m % 2))
                return ops

            ORDER = ("combine0", "split", "normalize0", "combine1", "combine2", "normalize1", "combine3", "sum",
                     "sum_experts", "sum_residual", "end")
            LAST_ORDER = ("combine0", "split", "normalize0", "combine1", "normalize1", "combine2", "combine3",
                          "sum", "sum_experts", "sum_residual", "split_last", "end")
            TAPS_BEFORE = dict(combine0=6, split=1, normalize0=1, combine1=20, combine2=26, normalize1=1, combine3=12,
                               sum=8, sum_experts=4, sum_residual=4, split_last=1)
            TAPS_BEFORE_FIRST = dict(combine0=30, split=1, normalize0=1, combine1=20, combine2=20, normalize1=1,
                                     combine3=10, sum=4, sum_experts=4, sum_residual=4, split_last=4)

            def body(m, part_of, beside):
                slot = body.slot
                ops = []
                if part_of is not None:
                    ops = attn_taps(slot, m, part_of)
                if slot["conv"] is not None:
                    ops = conv_taps(slot, m)
                jobs = ln_jobs(slot, m)
                work = {}
                for kind, n in jobs:
                    work["normalize0" if kind == "c" else "normalize1"] = lambda n=n: normalize(n)
                if slot["ffn"] is not None:
                    for e in range(E):
                        work[f"combine{e}"] = lambda e=e: combine(slot, m, e)
                    work["sum"] = lambda: sum_pairs(slot, m)
                    work["sum_experts"] = lambda: sum_experts(slot, m)
                    work["sum_residual"] = lambda: sum_residual(slot, m)
                if slot["lnf"] is not None:
                    if not (isinstance(m, int) and m == 0):
                        work["split"] = lambda: split_tile(slot, m - 1, jobs[-1][1] - slot["ln_step"])
                    if is_last(m):
                        work["split_last"] = lambda: split_tile(slot, m, jobs[-1][1])
                order = LAST_ORDER if is_last(m) else ORDER
                share = TAPS_BEFORE_FIRST if isinstance(m, int) and m == 0 else TAPS_BEFORE
                whole = sum(share[name] for name in order if name in work)
                at = done = 0
                for name in order:
                    if name in work:
                        done += share[name]
                        till = len(ops) * done // whole
                        for op in ops[at:till]:
                            op()
                        at = till
                    for more in beside.get(name, []):
                        more()
                    if name in work:
                        work[name]()

            def chain(b, n0):
                n = [n0]

                def link(ins, wait=True):
                    ins.then_inc(o_step, 1)
                    n[0] += 1
                    if wait:
                        dve.wait_ge(o_step, O_STEPS * b + n[0])
                return link

            def add_y(b, i):
                if i == 0:
                    dve.wait_ge(xres_ld, 16 * (b + 1))
                dve.wait_ge(at_full, AT_USES * b + AT_Y + i + 1)
                cols = slice(i * YCOL, (i + 1) * YCOL)
                dve.tensor_tensor(x_res[:, cols], at_ps[0:C, 0:YCOL], x_res[:, cols], ALU.add).then_inc(at_free, 1)

            for slot in SLOTS:
                body.slot = slot
                b = slot["attn"]

                def norm_off():
                    base = AT_USES * b
                    dve.wait_ge(at_free, base + AT_OFF + 2)
                    link = chain(b, 0)
                    v = off_t[:, :, :].rearrange("p h (c q) -> p h q c", q=Q)
                    for h in range(2):
                        for q in range(Q):
                            ins = dve.bn_stats(o_stats[:, h * Q + q, :], v[:, h, q, :])
                    link(ins)
                    for i in range(GQ):
                        ins = dve.bn_aggr(o_mv[:, i, :], o_stats[:, i, :])
                    ins.then_inc(o_var, 1)

                def apply_off():
                    link = chain(b, 1)
                    v = off_t[:, :, :].rearrange("p h (c q) -> p h q c", q=Q)
                    dve.wait_ge(o_scale, b + 1)
                    for h in range(2):
                        for q in range(Q):
                            i = h * Q + q
                            ins = dve.tensor_scalar(o_n[:, i, :], v[:, h, q, :], o_mv[:, i, 0:1], o_rstd[:, i:i + 1],
                                                    ALU.subtract, ALU.mult)
                    link(ins)
                    full = [HPTS, GQ, C]
                    link(dve.tensor_tensor(o_n[:, :, :], o_n[:, :, :], ln_gb[:, 0].unsqueeze(1).broadcast_to(full),
                                           ALU.mult))
                    link(dve.tensor_tensor(o_n[:, :, :], o_n[:, :, :], ln_gb[:, 1].unsqueeze(1).broadcast_to(full),
                                           ALU.add))

                def offsets():
                    link = chain(b, 4)
                    full = [HPTS, GQ, C]
                    dve.wait_ge(o_gelu, b + 1)
                    tmp = off_t[:, :, :].rearrange("p h n -> p (h n)").rearrange("p (g c) -> p g c", c=C)
                    for i in range(2):
                        link(dve.tensor_tensor(tmp, o_n[:, :, :], w_off2[:, i].unsqueeze(1).broadcast_to(full),
                                               ALU.mult))
                        link(dve.tensor_reduce(o_pos[:, i, :], tmp, AX_X, ALU.add))
                    link(dve.tensor_tensor(o_pos[:, :, :], o_pos[:, :, :],
                                           ref_pos[:, :].rearrange("p (i g) -> p i g", i=2), ALU.add))

                def positions():
                    link = chain(b, 9)
                    dve.wait_ge(o_tanh, b + 1)
                    link(dve.tensor_scalar(o_pos[:, :, :], o_pos[:, :, :], 1.0, 0.5 * (SIDE - 1), ALU.add, ALU.mult))
                    link(dve.tensor_copy(o_int[:, :, :], o_pos[:, :, :]))
                    link(dve.tensor_copy(o_fl[:, :, :], o_int[:, :, :]))
                    link(dve.tensor_tensor(o_gt[:, :, :], o_fl[:, :, :], o_pos[:, :, :], ALU.is_gt))
                    link(dve.tensor_tensor(o_fl[:, :, :], o_fl[:, :, :], o_gt[:, :, :], ALU.subtract))
                    link(dve.tensor_scalar(o_fl[:, :, :], o_fl[:, :, :], 0.0, float(SIDE - 2), ALU.max, ALU.min))
                    dve.tensor_tensor(o_w[:, :, :], o_pos[:, :, :], o_fl[:, :, :], ALU.subtract)
                    link(dve.scalar_tensor_tensor(o_idf[:, :], o_fl[:, 0, :], float(SIDE), o_fl[:, 1, :],
                                                  ALU.mult, ALU.add))
                    link(dve.tensor_scalar(o_u[:, :, :], o_w[:, :, :], -1.0, 1.0, ALU.mult, ALU.add))
                    for k, d in enumerate((0, SIDE)):
                        ins = dve.tensor_scalar(o_idx[:, k, :], o_idf[:, :], float(d), None, ALU.add)
                    ins.then_inc(o_index, 1)
                    for k, (wy, wx) in enumerate(((o_u, o_u), (o_u, o_w), (o_w, o_u), (o_w, o_w))):
                        ins = dve.tensor_tensor(o_cw[:, k, :], wy[:, 0, :], wx[:, 1, :], ALU.mult)
                    link(ins)

                def sample(k):
                    dve.wait_ge(gathered[k // 2], 16 * GQ * (b + 1))
                    corner = corner_pairs[:, k // 2, :, k % 2 * C:k % 2 * C + C]
                    vt = val_t[:, :, :].rearrange("p h (c q) -> p h q c", q=Q)
                    if k > 0:
                        dve.wait_ge(val_step, 4 * b + k)
                    for h in range(2):
                        for q in range(Q):
                            i = h * Q + q
                            if k == 0:
                                ins = dve.tensor_scalar(vt[:, h, q, :], corner[:, i, :], o_cw[:, k, i:i + 1],
                                                        None, ALU.mult)
                            else:
                                ins = dve.scalar_tensor_tensor(vt[:, h, q, :], corner[:, i, :],
                                                               o_cw[:, k, i:i + 1], vt[:, h, q, :],
                                                               ALU.mult, ALU.add)
                    ins.then_inc(val_step, 1)
                    if k == 3:
                        dve.wait_ge(val_step, 4 * b + 4)
                        dve.sem_inc(val_done, 1)

                def gates():
                    u = slot["ffn"]
                    n = [G_STEPS * u]

                    def link(ins):
                        ins.then_inc(g_step, 1)
                        n[0] += 1
                        dve.wait_ge(g_step, n[0])

                    by_e = [SUB, E, SUBS]
                    dve.wait_ge(scored, TILES * (u + 1))
                    dve.tensor_tensor(g_s[:, :, :], score_ps, gate_b[u // NB][:, :].unsqueeze(2).broadcast_to(by_e),
                                      ALU.add).then_inc(g_scores_read, 1)
                    dve.wait_ge(g_scores_read, u + 1)
                    link(dve.tensor_reduce(g_m[:, :], g_s[:, :, :].rearrange("p e s -> p s e"), AX_X, ALU.max))
                    link(dve.tensor_tensor(g_s[:, :, :], g_s[:, :, :], g_m[:, :].unsqueeze(1).broadcast_to(by_e),
                                           ALU.subtract))
                    dve.wait_ge(g_exp, u + 1)
                    link(dve.tensor_reduce(g_m[:, :], g_p[:, :, :].rearrange("p e s -> p s e"), AX_X, ALU.add))
                    link(dve.reciprocal(g_r[:, :], g_m[:, :]))
                    link(dve.tensor_tensor(g_p[:, :, :], g_p[:, :, :], g_r[:, :].unsqueeze(1).broadcast_to(by_e),
                                           ALU.mult))
                    for i in range(E):
                        for js, compare in ((slice(0, i), ALU.is_gt), (slice(i + 1, E), ALU.is_ge)):
                            if js.start < js.stop:
                                shape = [SUB, js.stop - js.start, SUBS]
                                ins = dve.tensor_tensor(g_gt[:, i, js], g_p[:, i, :].unsqueeze(1).broadcast_to(shape),
                                                        g_p[:, js, :], compare)
                    link(ins)
                    link(dve.tensor_reduce(g_rank[:, :, :].rearrange("p j s -> p (j s)"),
                                           g_gt[:, :, :, :].rearrange("p i j s -> p (j s) i"), AX_X, ALU.add))
                    link(dve.scalar_tensor_tensor(g_p[:, :, :].rearrange("p e s -> p (e s)"),
                                                  g_rank[:, :, :].rearrange("p e s -> p (e s)"), 1.5,
                                                  g_p[:, :, :].rearrange("p e s -> p (e s)"), ALU.is_lt, ALU.mult))
                    link(dve.tensor_reduce(g_m[:, :], g_p[:, :, :].rearrange("p e s -> p s e"), AX_X, ALU.add))
                    link(dve.tensor_scalar(g_m[:, :], g_m[:, :], TOPK_EPS, None, ALU.add))
                    link(dve.reciprocal(g_r[:, :], g_m[:, :]))
                    link(dve.tensor_tensor(g_s[:, :, :], g_p[:, :, :], g_r[:, :].unsqueeze(1).broadcast_to(by_e),
                                           ALU.mult))

                last = slot["before"]["attn"] if slot["before"] is not None else None
                if last is not None:
                    add_y(last, 2 * Q - LATE_Y)
                if slot["ffn"] is not None:
                    gates()
                if last is not None:
                    for i in range(2 * Q - LATE_Y + 1, 2 * Q):
                        add_y(last, i)
                if b is not None:
                    dve.wait_ge(xq_ld, 16 * Q * (b + 1))
                if slot["conv"] is not None:
                    dve.wait_ge(xq_ld, 16 * Q * (NB + slot["conv"] + 1))
                    dve.wait_ge(c_bias, G * (slot["conv"] + 1))
                if slot["ffn"] is not None and slot["ffn"] > 0:
                    dve.wait_ge(ffn_st[slot["ffn"] - 1], stored(slot["ffn"] - 1, TILES))
                if slot["conv"] is not None:
                    steps(dve, slot, body, {}, unroll=True)
                    continue
                steps(dve, slot, body, {
                    3: {"combine1": [norm_off], "combine3": [apply_off]},
                    4: {"combine0": [offsets], "combine1": [positions]},
                    5: {"combine2": [lambda: sample(0), lambda: sample(1)],
                        "combine3": [lambda: sample(2), lambda: sample(3)]},
                    6: {"combine1": [lambda: add_y(b, 0)], "normalize1": [lambda: add_y(b, 1)],
                        "combine2": [lambda: add_y(b, 2), lambda: add_y(b, 3)],
                        "combine3": [lambda: add_y(b, 4)]}},
                    {4: prepare_weights} if b == 0 else {})
                if slot is SLOTS[0]:
                    dve.wait_ge(taps_set, 1)


def _constants():
    import numpy as np
    q_mask = (np.arange(128)[:, None] % Q == np.arange(Q)[None, :]).astype(np.float32)
    ref = (np.linspace(0.5, KSIDE - 0.5, KSIDE).astype(np.float32) / np.float32(KSIDE) * 2 - 1).astype(np.float32)
    point = (np.arange(Q)[None, None, :] * QPTS + np.arange(2)[None, :, None] * HPTS
             + np.arange(HPTS)[:, None, None]).reshape(HPTS, GQ)
    ref_pos = np.stack([ref[point // KSIDE], ref[point % KSIDE]], axis=1).reshape(HPTS, 2 * GQ)
    to_quarters = (np.arange(32)[:, None] == np.arange(128)[None, :] // Q).astype(np.float32)
    return {"c_to_quarters": to_quarters, "c_ident": np.eye(128, dtype=np.float32), "c_q_mask": q_mask,
            "c_ref_pos": np.ascontiguousarray(ref_pos)}


def kernel(**inputs):
    import numpy as np
    import concourse.bacc as bacc
    from concourse.bass_utils import run_bass_kernel_spmd

    nc = bacc.Bacc("TRN2", target_bir_lowering=False, num_devices=1)
    arrays, aps = {}, {}
    for name, value in {**inputs, **_constants()}.items():
        v = np.ascontiguousarray(value)
        arrays[f"in_{name}"] = v
        aps[name] = nc.dram_tensor(f"in_{name}", v.shape, mybir.dt.from_np(v.dtype), kind="ExternalInput").ap()
    out = nc.dram_tensor("out_x", (NB, C, SIDE, SIDE), F32, kind="ExternalOutput").ap()
    metaformer_kernel(nc, aps, out)
    r = run_bass_kernel_spmd(nc, [arrays], core_ids=[0])
    return r.results[0]["out_x"]
```
